# Optimizing a Trainium2 kernel written in Bass

```python
import numpy as np
import jax
import jax.numpy as jnp

def _softmax(x, axis=-1):
    return jax.nn.softmax(x, axis=axis)

def _gelu(x):
    return jax.nn.gelu(x, approximate=True)

def _silu(x):
    return jax.nn.silu(x)

def _sigmoid(x):
    return jax.nn.sigmoid(x)

def _layernorm(x, axis=-1, eps=1e-05):
    m = jnp.mean(x, axis=axis, keepdims=True)
    v = jnp.var(x, axis=axis, keepdims=True)
    return (x - m) / jnp.sqrt(v + eps)

def _scatter_add(tgt, idx, src, axis=0):
    return tgt.at[idx].add(src)

def _segment_sum(src, seg, n):
    return jax.ops.segment_sum(src, seg, n)
kernel_name = 'mk_decoder_preln_d2_seqx_r4_89046e'

def setup_inputs(seed: int=0):
    np.random.seed(seed)
    _w = jnp.asarray

    def _rec_inputs():
        import jax
        import jax.numpy as jnp
        _rk = jax.random.key(seed)
        x = 0.5 + 0.2887 * jax.random.normal(jax.random.fold_in(_rk, 1), (4, 512, 512), jnp.float32)
        _lenS = 512 - jax.random.randint(jax.random.fold_in(_rk, 7), (4,), 0, max(1, 512 // 4) + 1, jnp.int32)
        _lenS2 = 512 - jax.random.randint(jax.random.fold_in(_rk, 8), (4,), 0, max(1, 512 // 4) + 1, jnp.int32)
        _ctx_512P = jax.random.normal(jax.random.fold_in(_rk, 11), (4, 16, 128), jnp.float32)
        _ctx_512c = jax.random.dirichlet(jax.random.fold_in(_rk, 511), 0.3 * jnp.ones((16,), jnp.float32), (4, 512))
        _ctx_512t = jnp.einsum('bsk,bkd->bsd', _ctx_512c, _ctx_512P)
        _ctx_512t = _ctx_512t * jax.lax.rsqrt(jnp.mean(jnp.square(_ctx_512t)) + 1e-12) * 0.953939
        ctx_512 = -0.000392918 + 0.999932 * (_ctx_512t + 0.3 * jax.random.normal(jax.random.fold_in(_rk, 611), (4, 512, 128), jnp.float32))
        return (x, ctx_512)
    x, ctx_512 = _rec_inputs()

    def _L0_attn_setup():
        import jax, jax.numpy as jnp
        import numpy as np
        HIDDEN = 512
        N_HEADS = 16
        HEAD_DIM = HIDDEN // N_HEADS

        def rotate_half(x):
            x1, x2 = jnp.split(x, 2, axis=-1)
            return jnp.concatenate([-x2, x1], axis=-1)
        key = jax.random.key(seed)
        k0, k1, k2, k3, k4 = jax.random.split(key, 5)
        B, S = (1, 512)
        scale = 1.0 / np.sqrt(HIDDEN)
        return {'hidden_states': jax.random.normal(k0, (B, S, HIDDEN), dtype=jnp.float32), 'Wq': jax.random.normal(k1, (HIDDEN, HIDDEN), dtype=jnp.float32) * scale, 'Wk': jax.random.normal(k2, (HIDDEN, HIDDEN), dtype=jnp.float32) * scale, 'Wv': jax.random.normal(k3, (HIDDEN, HIDDEN), dtype=jnp.float32) * scale, 'Wo': jax.random.normal(k4, (HIDDEN, HIDDEN), dtype=jnp.float32) * scale, 'gate': jnp.zeros((1, N_HEADS, 1, 1), dtype=jnp.float32)}
    _L0_attn_all = _L0_attn_setup()
    _L0_attn_in = {k: v for k, v in _L0_attn_all.items() if k in ('Wq', 'Wk', 'Wv', 'Wo', 'gate')}
    del _L0_attn_all

    def _L0_xattn_setup():
        import jax, jax.numpy as jnp
        import numpy as np
        B, N, D = (16, 512, 128)
        H = 4
        TOP_K_RATIO = 0.3
        key = jax.random.key(seed)
        k1, k2, k3, k4 = jax.random.split(key, 4)
        h = jax.random.normal(k1, (B, N, D), dtype=jnp.float32)
        adj_raw = jax.random.uniform(k2, (B, N, N), dtype=jnp.float32)
        lim = 1.0 / np.sqrt(D)
        Wq = jax.random.uniform(k3, (D, D), minval=-lim, maxval=lim, dtype=jnp.float32)
        Wk = jax.random.uniform(k4, (D, D), minval=-lim, maxval=lim, dtype=jnp.float32)
        gamma_raw = jnp.float32(-0.85)
        return {'h': h, 'adj_raw': adj_raw, 'Wq': Wq, 'Wk': Wk, 'gamma_raw': gamma_raw}
    _L0_xattn_all = _L0_xattn_setup()
    _L0_xattn_in = {k: v for k, v in _L0_xattn_all.items() if k in ('Wq', 'Wk', 'gamma_raw')}
    del _L0_xattn_all

    def _L0_ffn_setup():
        import jax, jax.numpy as jnp
        import numpy as np
        B, S, H = (2, 256, 512)
        I = 256
        E = 32
        Z = 32
        K = 8
        SCALE = 1.5
        CAP = 256
        EPS = 1e-20

        def _moe_forward(x, w_cls, bias, w_gate_up, w_down):
            T = x.shape[0] * x.shape[1]
            xf = x.reshape(T, H)
            logits = xf.astype(jnp.float32) @ w_cls.T
            scores = jax.nn.softmax(logits, axis=-1)
            _, topk_idx = jax.lax.top_k(scores + bias[None, :], K)
            w = jnp.take_along_axis(scores, topk_idx, axis=-1)
            w = w / (w.sum(-1, keepdims=True) + EPS) * SCALE
            routed = topk_idx < E
            w_r = jnp.where(routed, w, 0.0)
            w_z = jnp.where(routed, 0.0, w)
            N = T * K
            flat_ids = jnp.where(routed, topk_idx, E).reshape(-1)
            x_exp = jnp.repeat(xf, K, axis=0)
            order = jnp.argsort(flat_ids)
            ids_s = flat_ids[order]
            counts = jax.ops.segment_sum(jnp.ones(N, jnp.int32), flat_ids, num_segments=E + 1)
            starts = jnp.cumsum(counts) - counts
            pos = jnp.arange(N) - starts[ids_s]
            buf = jnp.zeros((E, CAP, H), xf.dtype).at[ids_s, pos].set(x_exp[order], mode='drop')
            gu = jnp.einsum('ech,ehf->ecf', buf, w_gate_up)
            g, u = jnp.split(gu, 2, axis=-1)
            act = jax.nn.silu(g) * u
            y = jnp.einsum('eci,eih->ech', act, w_down)
            valid = (ids_s < E) & (pos < CAP)
            y_tok = jnp.where(valid[:, None], y[jnp.clip(ids_s, 0, E - 1), jnp.clip(pos, 0, CAP - 1)], 0.0)
            y_exp = jnp.zeros((N, H), xf.dtype).at[order].set(y_tok).reshape(T, K, H)
            routed_out = jnp.einsum('tk,tkh->th', w_r, y_exp)
            out = routed_out * (1.0 + w_z.sum(-1, keepdims=True))
            return out.reshape(x.shape)
        key = jax.random.key(seed)
        ks = jax.random.split(key, 5)
        x = jax.random.normal(ks[0], (B, S, H), jnp.float32)
        w_cls = jax.random.normal(ks[1], (E + Z, H), jnp.float32) / np.float32(np.sqrt(H))
        bias = jax.random.normal(ks[2], (E + Z,), jnp.float32) * 0.02
        w_gate_up = jax.random.normal(ks[3], (E, H, 2 * I), jnp.float32) * 0.02
        w_down = jax.random.normal(ks[4], (E, I, H), jnp.float32) * 0.02
        return {'x': x, 'w_cls': w_cls, 'bias': bias, 'w_gate_up': w_gate_up, 'w_down': w_down}
    _L0_ffn_all = _L0_ffn_setup()
    _L0_ffn_in = {k: v for k, v in _L0_ffn_all.items() if k in ('w_cls', 'bias', 'w_gate_up', 'w_down')}
    del _L0_ffn_all

    def _L1_attn_setup():
        import jax, jax.numpy as jnp
        import numpy as np
        HIDDEN_DIM = 512
        NUM_HEADS = 16
        HEAD_DIM = HIDDEN_DIM // NUM_HEADS
        BATCH = 2
        SEQ = 512
        key = jax.random.key(seed)
        ks = jax.random.split(key, 5)
        scale = 1.0 / np.sqrt(HIDDEN_DIM)
        x = jax.random.normal(ks[0], (BATCH, SEQ, HIDDEN_DIM), dtype=jnp.float32)
        w_q = jax.random.normal(ks[1], (HIDDEN_DIM, HIDDEN_DIM), dtype=jnp.float32) * scale
        w_k = jax.random.normal(ks[2], (HIDDEN_DIM, HIDDEN_DIM), dtype=jnp.float32) * scale
        w_v = jax.random.normal(ks[3], (HIDDEN_DIM, HIDDEN_DIM), dtype=jnp.float32) * scale
        w_o = jax.random.normal(ks[4], (HIDDEN_DIM, HIDDEN_DIM), dtype=jnp.float32) * scale
        return {'x': x, 'w_q': w_q, 'w_k': w_k, 'w_v': w_v, 'w_o': w_o}
    _L1_attn_all = _L1_attn_setup()
    _L1_attn_in = {k: v for k, v in _L1_attn_all.items() if k in ('w_q', 'w_k', 'w_v', 'w_o')}
    del _L1_attn_all

    def _L1_xattn_setup():
        import jax, jax.numpy as jnp
        import numpy as np
        B, S, H, NH, L = (2, 512, 512, 16, 128)
        HD = H // NH
        key = jax.random.key(seed)
        k1, k2, k3, k4, k5 = jax.random.split(key, 5)
        scale = 0.02
        return {'q': jax.random.normal(k1, (B, S, H), dtype=jnp.float32), 'latent_kv': jax.random.normal(k2, (B, S, L), dtype=jnp.float32), 'Wq': jax.random.normal(k3, (H, H), dtype=jnp.float32) * scale, 'Wkv_expand': jax.random.normal(k4, (2 * H, L), dtype=jnp.float32) * scale, 'Wout': jax.random.normal(k5, (H, H), dtype=jnp.float32) * scale}
    _L1_xattn_all = _L1_xattn_setup()
    _L1_xattn_in = {k: v for k, v in _L1_xattn_all.items() if k in ('Wq', 'Wkv_expand', 'Wout')}
    del _L1_xattn_all

    def _L1_ffn_setup():
        import jax, jax.numpy as jnp
        import numpy as np
        B, S, D, H = (4, 512, 512, 2048)

        def fwht(x):
            orig_shape = x.shape
            n = orig_shape[-1]
            x = x.reshape(-1, n)
            h = 1
            while h < n:
                xb = x.reshape(-1, n // (2 * h), 2, h)
                a = xb[:, :, 0, :]
                b = xb[:, :, 1, :]
                x = jnp.stack([a + b, a - b], axis=2).reshape(-1, n)
                h *= 2
            scale = jnp.asarray(1.0 / np.sqrt(n), dtype=x.dtype)
            return (x * scale).reshape(orig_shape)
        key = jax.random.key(seed)
        kx, k1, k2, k3 = jax.random.split(key, 4)
        x = jax.random.normal(kx, (B, S, D), dtype=jnp.float32)
        W1 = jax.random.normal(k1, (H, D), dtype=jnp.float32) * (1.0 / np.sqrt(D))
        W2 = jax.random.normal(k2, (D, H), dtype=jnp.float32) * (1.0 / np.sqrt(H))
        W3 = jax.random.normal(k3, (H, D), dtype=jnp.float32) * (1.0 / np.sqrt(D))
        return {'x': x, 'W1': W1, 'W2': W2, 'W3': W3}
    _L1_ffn_all = _L1_ffn_setup()
    _L1_ffn_in = {k: v for k, v in _L1_ffn_all.items() if k in ('W1', 'W2', 'W3')}
    del _L1_ffn_all
    return {'x': x, 'ctx_512': ctx_512, 'L0_attn_Wq': _L0_attn_in['Wq'], 'L0_attn_Wk': _L0_attn_in['Wk'], 'L0_attn_Wv': _L0_attn_in['Wv'], 'L0_attn_Wo': _L0_attn_in['Wo'], 'L0_attn_gate': _L0_attn_in['gate'], 'L0_xattn_Wq': _L0_xattn_in['Wq'], 'L0_xattn_Wk': _L0_xattn_in['Wk'], 'L0_xattn_gamma_raw': _L0_xattn_in['gamma_raw'], 'L0_ffn_w_cls': _L0_ffn_in['w_cls'], 'L0_ffn_bias': _L0_ffn_in['bias'], 'L0_ffn_w_gate_up': _L0_ffn_in['w_gate_up'], 'L0_ffn_w_down': _L0_ffn_in['w_down'], 'L1_attn_w_q': _L1_attn_in['w_q'], 'L1_attn_w_k': _L1_attn_in['w_k'], 'L1_attn_w_v': _L1_attn_in['w_v'], 'L1_attn_w_o': _L1_attn_in['w_o'], 'L1_xattn_Wq': _L1_xattn_in['Wq'], 'L1_xattn_Wkv_expand': _L1_xattn_in['Wkv_expand'], 'L1_xattn_Wout': _L1_xattn_in['Wout'], 'L1_ffn_W1': _L1_ffn_in['W1'], 'L1_ffn_W2': _L1_ffn_in['W2'], 'L1_ffn_W3': _L1_ffn_in['W3']}

def reference(x, ctx_512, L0_attn_Wq, L0_attn_Wk, L0_attn_Wv, L0_attn_Wo, L0_attn_gate, L0_xattn_Wq, L0_xattn_Wk, L0_xattn_gamma_raw, L0_ffn_w_cls, L0_ffn_bias, L0_ffn_w_gate_up, L0_ffn_w_down, L1_attn_w_q, L1_attn_w_k, L1_attn_w_v, L1_attn_w_o, L1_xattn_Wq, L1_xattn_Wkv_expand, L1_xattn_Wout, L1_ffn_W1, L1_ffn_W2, L1_ffn_W3):
    import jax
    import jax.numpy as jnp

    def _L0_attn_ref(hidden_states, Wq, Wk, Wv, Wo, gate):
        import jax, jax.numpy as jnp
        import numpy as np
        HIDDEN = 512
        N_HEADS = 16
        HEAD_DIM = HIDDEN // N_HEADS

        def rotate_half(x):
            x1, x2 = jnp.split(x, 2, axis=-1)
            return jnp.concatenate([-x2, x1], axis=-1)
        B, S, H = hidden_states.shape
        q = hidden_states @ Wq.T
        k = hidden_states @ Wk.T
        v = hidden_states @ Wv.T
        inv_freq = 1.0 / 10000.0 ** (jnp.arange(0, H, 2, dtype=jnp.float32) / H)
        t = jnp.arange(S, dtype=jnp.float32)
        freqs = t[:, None] * inv_freq[None, :]
        emb = jnp.concatenate([freqs, freqs], axis=-1)[None]
        cos, sin = (jnp.cos(emb), jnp.sin(emb))
        q = q * cos + rotate_half(q) * sin
        k = k * cos + rotate_half(k) * sin

        def split_heads(x):
            return x.reshape(B, S, N_HEADS, HEAD_DIM).transpose(0, 2, 1, 3)
        q, k, v = (split_heads(q), split_heads(k), split_heads(v))
        k_feat = jax.nn.elu(k) + 1.0
        memory = jnp.einsum('bhsd,bhse->bhde', k_feat, v)
        norm_term = k_feat.sum(axis=2)
        q_feat = jax.nn.elu(q) + 1.0
        mem_out = jnp.einsum('bhsd,bhde->bhse', q_feat, memory)
        denom = jnp.einsum('bhsd,bhd->bhs', q_feat, norm_term)[..., None]
        mem_out = mem_out / denom
        scale = 1.0 / jnp.sqrt(jnp.float32(HEAD_DIM))
        scores = jnp.einsum('bhqd,bhkd->bhqk', q, k) * scale
        attn = jnp.einsum('bhqk,bhkd->bhqd', jax.nn.softmax(scores, axis=-1), v)
        g = jax.nn.sigmoid(gate)
        combined = g * mem_out + (1.0 - g) * attn
        combined = combined.transpose(0, 2, 1, 3).reshape(B, S, H)
        return combined @ Wo.T

    def _L0_xattn_ref(h, adj_raw, Wq, Wk, gamma_raw):
        import jax, jax.numpy as jnp
        import numpy as np
        B, N, D = (16, 512, 128)
        H = 4
        TOP_K_RATIO = 0.3
        b, n, dm = h.shape
        d = dm // H
        Q = (h @ Wq.T).reshape(b, n, H, d).transpose(0, 2, 1, 3)
        K = (h @ Wk.T).reshape(b, n, H, d).transpose(0, 2, 1, 3)
        sim = jnp.einsum('bhnd,bhmd->bnm', Q, K) / (jnp.sqrt(jnp.float32(d)) * H)
        k = max(1, int(n * TOP_K_RATIO))
        topk_vals = jax.lax.top_k(sim, k)[0]
        threshold = topk_vals[:, :, -1:]
        sparse_mask = (sim >= threshold).astype(sim.dtype)
        A_learned = jax.nn.sigmoid(sim) * sparse_mask
        A_learned = (A_learned + jnp.swapaxes(A_learned, -1, -2)) * 0.5
        gamma = jax.nn.sigmoid(gamma_raw)
        return (1.0 - gamma) * adj_raw + gamma * A_learned

    def _L0_ffn_ref(x, w_cls, bias, w_gate_up, w_down):
        import jax, jax.numpy as jnp
        import numpy as np
        B, S, H = (2, 256, 512)
        I = 256
        E = 32
        Z = 32
        K = 8
        SCALE = 1.5
        CAP = 256
        EPS = 1e-20

        def _moe_forward(x, w_cls, bias, w_gate_up, w_down):
            T = x.shape[0] * x.shape[1]
            xf = x.reshape(T, H)
            logits = xf.astype(jnp.float32) @ w_cls.T
            scores = jax.nn.softmax(logits, axis=-1)
            _, topk_idx = jax.lax.top_k(scores + bias[None, :], K)
            w = jnp.take_along_axis(scores, topk_idx, axis=-1)
            w = w / (w.sum(-1, keepdims=True) + EPS) * SCALE
            routed = topk_idx < E
            w_r = jnp.where(routed, w, 0.0)
            w_z = jnp.where(routed, 0.0, w)
            N = T * K
            flat_ids = jnp.where(routed, topk_idx, E).reshape(-1)
            x_exp = jnp.repeat(xf, K, axis=0)
            order = jnp.argsort(flat_ids)
            ids_s = flat_ids[order]
            counts = jax.ops.segment_sum(jnp.ones(N, jnp.int32), flat_ids, num_segments=E + 1)
            starts = jnp.cumsum(counts) - counts
            pos = jnp.arange(N) - starts[ids_s]
            buf = jnp.zeros((E, CAP, H), xf.dtype).at[ids_s, pos].set(x_exp[order], mode='drop')
            gu = jnp.einsum('ech,ehf->ecf', buf, w_gate_up)
            g, u = jnp.split(gu, 2, axis=-1)
            act = jax.nn.silu(g) * u
            y = jnp.einsum('eci,eih->ech', act, w_down)
            valid = (ids_s < E) & (pos < CAP)
            y_tok = jnp.where(valid[:, None], y[jnp.clip(ids_s, 0, E - 1), jnp.clip(pos, 0, CAP - 1)], 0.0)
            y_exp = jnp.zeros((N, H), xf.dtype).at[order].set(y_tok).reshape(T, K, H)
            routed_out = jnp.einsum('tk,tkh->th', w_r, y_exp)
            out = routed_out * (1.0 + w_z.sum(-1, keepdims=True))
            return out.reshape(x.shape)
        return _moe_forward(x, w_cls, bias, w_gate_up, w_down)

    def _L1_attn_ref(x, w_q, w_k, w_v, w_o):
        import jax, jax.numpy as jnp
        import numpy as np
        HIDDEN_DIM = 512
        NUM_HEADS = 16
        HEAD_DIM = HIDDEN_DIM // NUM_HEADS
        BATCH = 2
        SEQ = 512
        q = jnp.einsum('bsd,ed->bse', x, w_q)
        k = jnp.einsum('bsd,ed->bse', x, w_k)
        v = jnp.einsum('bsd,ed->bse', x, w_v)
        b, s, _ = q.shape
        q = q.reshape(b, s, NUM_HEADS, HEAD_DIM).transpose(0, 2, 1, 3)
        k = k.reshape(b, s, NUM_HEADS, HEAD_DIM).transpose(0, 2, 1, 3)
        v = v.reshape(b, s, NUM_HEADS, HEAD_DIM).transpose(0, 2, 1, 3)
        scale = 1.0 / np.sqrt(HEAD_DIM)
        scores = jnp.einsum('bhqd,bhkd->bhqk', q, k) * scale
        p = jax.nn.softmax(scores, axis=-1)
        o = jnp.einsum('bhqk,bhkd->bhqd', p, v)
        o = o.transpose(0, 2, 1, 3).reshape(b, s, HIDDEN_DIM)
        return jnp.einsum('bsd,ed->bse', o, w_o)

    def _L1_xattn_ref(q, latent_kv, Wq, Wkv_expand, Wout):
        import jax, jax.numpy as jnp
        import numpy as np
        B, S, H, NH, L = (2, 512, 512, 16, 128)
        HD = H // NH
        b, sq, _ = q.shape
        sk = latent_kv.shape[1]
        qp = q @ Wq.T
        kv = latent_kv @ Wkv_expand.T
        k, v = jnp.split(kv, 2, axis=-1)
        qh = qp.reshape(b, sq, NH, HD).transpose(0, 2, 1, 3)
        kh = k.reshape(b, sk, NH, HD).transpose(0, 2, 1, 3)
        vh = v.reshape(b, sk, NH, HD).transpose(0, 2, 1, 3)
        inv_sqrt_d = 1.0 / jnp.sqrt(jnp.float32(HD))
        scores = jnp.einsum('bhqd,bhkd->bhqk', qh, kh) * inv_sqrt_d
        causal = jnp.tril(jnp.ones((sq, sk), dtype=bool))
        scores = jnp.where(causal, scores, jnp.finfo(scores.dtype).min)
        attn = jax.nn.softmax(scores, axis=-1)
        out = jnp.einsum('bhqk,bhkd->bhqd', attn, vh)
        out = out.transpose(0, 2, 1, 3).reshape(b, sq, H)
        return out @ Wout.T

    def _L1_ffn_ref(x, W1, W2, W3):
        import jax, jax.numpy as jnp
        import numpy as np
        B, S, D, H = (4, 512, 512, 2048)

        def fwht(x):
            orig_shape = x.shape
            n = orig_shape[-1]
            x = x.reshape(-1, n)
            h = 1
            while h < n:
                xb = x.reshape(-1, n // (2 * h), 2, h)
                a = xb[:, :, 0, :]
                b = xb[:, :, 1, :]
                x = jnp.stack([a + b, a - b], axis=2).reshape(-1, n)
                h *= 2
            scale = jnp.asarray(1.0 / np.sqrt(n), dtype=x.dtype)
            return (x * scale).reshape(orig_shape)
        up_gate = jnp.einsum('bsd,hd->bsh', x, W1)
        up_lin = jnp.einsum('bsd,hd->bsh', x, W3)
        hidden = jax.nn.silu(up_gate) * up_lin
        hidden = fwht(hidden)
        out = jnp.einsum('bsh,dh->bsd', hidden, W2)
        return out
    x = x + _L0_attn_ref(_layernorm(x, axis=-1), L0_attn_Wq, L0_attn_Wk, L0_attn_Wv, L0_attn_Wo, L0_attn_gate)
    x = x + _L0_xattn_ref(ctx_512, _layernorm(x, axis=-1), L0_xattn_Wq, L0_xattn_Wk, L0_xattn_gamma_raw)
    x = x + _L0_ffn_ref(_layernorm(x, axis=-1), L0_ffn_w_cls, L0_ffn_bias, L0_ffn_w_gate_up, L0_ffn_w_down)
    x = x + _L1_attn_ref(_layernorm(x, axis=-1), L1_attn_w_q, L1_attn_w_k, L1_attn_w_v, L1_attn_w_o)
    x = x + _L1_xattn_ref(_layernorm(x, axis=-1), ctx_512, L1_xattn_Wq, L1_xattn_Wkv_expand, L1_xattn_Wout)
    x = x + _L1_ffn_ref(_layernorm(x, axis=-1), L1_ffn_W1, L1_ffn_W2, L1_ffn_W3)
    return x

_drawn_inputs = setup_inputs


def setup_inputs(seed=0):
    import zlib

    import numpy as np

    out = dict(_drawn_inputs(seed))
    spreads = {'L0_attn_gate': (0.0, 0.8)}
    factors = {'L0_ffn_bias': 13.763,
     'L1_xattn_Wq': 24.846,
     'L0_ffn_w_cls': 3.104,
     'L0_ffn_w_gate_up': 2.834,
     'L0_ffn_w_down': 2.83}
    for name, (base, spread) in spreads.items():
        noise = np.random.default_rng([zlib.crc32(name.encode()), seed]).standard_normal(out[name].shape)
        drawn = base * np.exp(spread * noise) if base else spread * noise
        out[name] = jnp.asarray(drawn.astype(out[name].dtype))
    for name, factor in factors.items():
        out[name] = (out[name] * factor).astype(out[name].dtype)
    return out
```

```python
from contextlib import ExitStack, contextmanager

import concourse.bass as bass
from concourse import mybir

ALU = mybir.AluOpType
ACT = mybir.ActivationFunctionType
AX = mybir.AxisListType
F32 = mybir.dt.float32
F32R = mybir.dt.float32r
BF16 = mybir.dt.bfloat16
I32 = mybir.dt.int32
U32 = mybir.dt.uint32

P = 128
B, S, D = 4, 512, 512
T = B * S
NT = S // P
NC = D // P
H, HD = 16, 32
HC = P // HD
L = 128
EPS = 1e-5
SCALE = HD ** -0.5
VW = 66
NEG = -1e30


class Env:
    pass


@contextmanager
def semaphores(nc):
    taken = []

    def take(name):
        taken.append(nc.alloc_semaphore(name=name))
        return taken[-1]

    yield take
    nc.clear_and_free_semaphores(taken)
    nc.all_engine_barrier()


def split_mm(pe, out, lhs, rhs, start, stop):
    (lh, ll), (rh, rl) = lhs, rhs
    pe.matmul(out, lh, rh, start=start, stop=False, skip_group_check=True)
    pe.matmul(out, lh, rl, start=False, stop=False, skip_group_check=True)
    return pe.matmul(out, ll, rh, start=False, stop=stop, skip_group_check=True)


def tiles(ap):
    return ap.rearrange("(t p) d -> p t d", p=P)



def constants(nc, env):
    with semaphores(nc) as take, ExitStack() as ctx:
        done = take("const_done")
        copied = take("const_copied")
        scratch = ctx.enter_context(nc.sbuf_tensor("const_scratch", [P, HC * 7 * HD], F32))
        block = ctx.enter_context(nc.Block())
        ident = env.ident
        sel = scratch[:].rearrange("p (j m) -> p j m", j=HC)

        @block.gpsimd
        def _(pool):
            pool.memset(ident[:], 0.0).then_inc(done, 1)
            pool.memset(scratch[:], 0.0).then_inc(done, 1)
            pool.memset(env.minus_half[:], -0.5).then_inc(done, 1)
            pool.memset(env.blockmask[:], 1.0).then_inc(done, 1)
            pool.wait_ge(done, 4)
            mask = env.blockmask[:].rearrange("p (h w) -> p h w", w=HD + 1)
            pool.affine_select(out=mask, in_=mask, compare_op=ALU.is_ge, fill=0.0, base=0,
                               pattern=[[-HD, HC], [0, HD + 1]], channel_multiplier=1).then_inc(done, 1)
            pool.wait_ge(done, 5)
            pool.affine_select(out=mask, in_=mask, compare_op=ALU.is_ge, fill=0.0, base=HD - 1,
                               pattern=[[HD, HC], [0, HD + 1]], channel_multiplier=-1).then_inc(done, 1)
            pool.affine_select(out=ident[:], in_=ident[:], compare_op=ALU.not_equal, fill=1.0, base=0,
                               pattern=[[-1, P]], channel_multiplier=1).then_inc(done, 1)
            for at, n in ((2, 2), (6, 1)):
                part = sel[:, :, at * HD:(at + n) * HD].rearrange("p j (k m) -> p j k m", m=HD)
                pool.affine_select(out=part, in_=part, compare_op=ALU.not_equal, fill=1.0, base=0,
                                   pattern=[[-HD, HC], [0, n], [-1, HD]], channel_multiplier=1).then_inc(done, 1)

        @block.vector
        def _(dve):
            dve.wait_ge(done, 9)
            dve.tensor_copy(env.ident_r[:], ident[:]).then_inc(copied, 1)
            dve.tensor_copy(env.sel[:], sel).then_inc(copied, 1)
            dve.tensor_scalar(env.one_r[:], ident[:, 0:1], 0.0, 1.0, ALU.mult, ALU.add).then_inc(copied, 1)
            dve.wait_ge(copied, 3)


def causal_masks(nc, qk, kq):
    with semaphores(nc) as take, ExitStack() as ctx:
        made, copied = take("causal_made"), take("causal_copied")
        raw = ctx.enter_context(nc.sbuf_tensor("causal_raw", [P, 2, P], F32))
        block = ctx.enter_context(nc.Block())

        @block.gpsimd
        def _(pool):
            pool.memset(raw[:], 0.0).then_inc(made, 1)
            pool.wait_ge(made, 1)
            pool.affine_select(out=raw[:, 0, :], in_=raw[:, 0, :], compare_op=ALU.is_ge, fill=NEG, base=0,
                               pattern=[[-1, P]], channel_multiplier=1).then_inc(made, 1)
            pool.affine_select(out=raw[:, 1, :], in_=raw[:, 1, :], compare_op=ALU.is_ge, fill=NEG, base=0,
                               pattern=[[1, P]], channel_multiplier=-1).then_inc(made, 1)

        @block.vector
        def _(dve):
            dve.wait_ge(made, 3)
            dve.tensor_copy(qk[:], raw[:, 0, :]).then_inc(copied, 1)
            dve.tensor_copy(kq[:], raw[:, 1, :]).then_inc(copied, 1)
            dve.wait_ge(copied, 2)



def load_weights(nc, env, tag, jobs):
    stages = [(n, r) for n, (w, _, _) in enumerate(jobs) for r in range(w.shape[0] // 512)]
    with semaphores(nc) as take, ExitStack() as ctx:
        sem = lambda n: take(f"{tag}_{n}")
        raw = ctx.enter_context(nc.sbuf_tensor(f"{tag}_raw", [P, 2, NT, 512], F32))
        ps = ctx.enter_context(nc.psum_tensor(f"{tag}_ps", [P, 8, 512], F32))
        loaded = [sem(f"loaded{i}") for i in range(2)]
        turned, high_done, low_done = sem("turned"), sem("high_done"), sem("low_done")
        block = ctx.enter_context(nc.Block())
        banks = []
        for s, (n, _) in enumerate(stages):
            banks += [(s, c) for c in range(jobs[n][0].shape[1] // P)]

        @block.sync
        def _(sp):
            for s, (n, r) in enumerate(stages):
                w = jobs[n][0]
                if s >= 2:
                    sp.wait_ge(turned, sum(1 for q, _ in banks if q <= s - 2))
                sp.dma_start(raw[:, s % 2, :, 0:w.shape[1]],
                             tiles(w[r * 512:(r + 1) * 512, :])).then_inc(loaded[s % 2], 16)

        @block.tensor
        def _(pe):
            for u, (s, c) in enumerate(banks):
                pe.wait_ge(loaded[s % 2], 16 * (s // 2 + 1))
                if u >= 8:
                    pe.wait_ge(low_done, u - 7)
                for t in range(NT):
                    mm = pe.transpose(ps[:, u % 8, t * P:(t + 1) * P],
                                      raw[:, s % 2, t, c * P:(c + 1) * P], env.ident[:])
                mm.then_inc(turned, 1)

        @block.scalar
        def _(act):
            for u, (s, c) in enumerate(banks):
                n, r = stages[s]
                act.wait_ge(turned, u + 1)
                act.copy(jobs[n][1][:, c, r * 512:(r + 1) * 512], ps[:, u % 8, :]).then_inc(high_done, 1)

        @block.vector
        def _(dve):
            for u, (s, c) in enumerate(banks):
                n, r = stages[s]
                cols = slice(r * 512, (r + 1) * 512)
                dve.wait_ge(high_done, u + 1)
                dve.tensor_tensor(jobs[n][2][:, c, cols], ps[:, u % 8, :],
                                  jobs[n][1][:, c, cols].bitcast(F32), ALU.subtract).then_inc(low_done, 1)



class Signal:

    def __init__(self, nc, sem, per, start=1):
        self.sem, self.per, self.start = sem, per, start
        if start:
            nc.sync.sem_inc(sem, start)

    def wait(self, eng, b, n):
        assert self.start or n > 0
        eng.wait_ge(self.sem, b * self.per + n + self.start)


def batches(eng, body):
    with eng.Fori(0, B - 1) as b:
        body(b, True)
    body(B - 1, False)


def attention(nc, env, tag, x_in, x_out, wq, wk, wv, wo, gate=None, ctx_in=None, causal=False):
    linear = gate is not None
    KC = NC if ctx_in is None else 1
    with semaphores(nc) as take, ExitStack() as ctx:
        def sb(name, shape, dtype=F32):
            return ctx.enter_context(nc.sbuf_tensor(f"{tag}_{name}", shape, dtype))

        def sem(name):
            return take(f"{tag}_{name}")

        def signal(name, per, start=1):
            return Signal(nc, sem(name), per, start)

        def pair(name, shape):
            return sb(f"{name}_hi", shape, F32R), sb(f"{name}_lo", shape, F32R)

        wqT, wkT, wvT, woT = pair("wq", [P, NC, D]), pair("wk", [P, KC, D]), pair("wv", [P, KC, D]), pair("wo", [P, NC, D])
        load_weights(nc, env, f"{tag}_w", [(wq, *wqT), (wk, *wkT), (wv, *wvT), (wo, *woT)])

        if causal:
            causal_qk, causal_kq = sb("causal_qk", [P, P], F32R), sb("causal_kq", [P, P], F32R)
            causal_masks(nc, causal_qk, causal_kq)
        NST = 3
        xs = sb("xs", [P, NT, D])
        res = sb("res", [P, 2, D])
        xnT = pair("xnT", [P, NC, S])
        qT, kT = pair("qT", [P, NC, S]), pair("kT", [P, NC, S])
        v_split = sb("v_split", [P, NT, H, VW], F32R)
        qs, ks = sb("qs", [P, NST, S], F32R), sb("ks", [P, NST, S], F32R)
        probs = sb("probs", [P, NT, S])
        probs_hi, probs_lo = sb("probs_hi", [P, NT, S], F32R), sb("probs_lo", [P, NT, S], F32R)
        heads_out = sb("heads_out", [P, NT, D])
        u_sb = sb("u_sb", [P, 2, S])
        stats, mv = sb("stats", [P, NT, 6]), sb("mv", [P, NT, 2])
        rstd = sb("rstd", [P, NT])
        carrier = sb("carrier", [P, 1])
        negmax = sb("negmax", [P, 2, NT])
        dneg = sb("dneg", [P, 2, S], F32R)
        rsum = sb("rsum", [P, NT])
        piece_a, piece_b = sb("piece_a", [P, NT, HD]), sb("piece_b", [P, NT, HD])
        if ctx_in is not None:
            ctx_sb = sb("ctx_sb", [P, NT, L])
            cT = pair("cT", [P, 1, S])
        if linear:
            HW = HC * (HD + 1)
            cosT, sinT = sb("cosT", [P, NC // 2, S]), sb("sinT", [P, NC // 2, S])
            gate_e, g_not, g_sig = sb("gate_e", [P, H]), sb("g_not", [P, H]), sb("g_sig", [P, H])
            spare = xs[:].rearrange("p t d -> p (t d)")
            v_one = spare[:, 0:NT * HW].rearrange("p (t h w) -> p t h w", t=NT, h=HC)
            mem = spare[:, NT * HW:(NT + 1) * HW].rearrange("p (h w) -> p h w", h=HC)
            den = spare[:, (NT + 1) * HW:(NT + 1) * HW + 2 * HC].rearrange("p (t h) -> p t h", t=2)
            feat_k, feat_q = u_sb[:, 0, :], u_sb[:, 1, :]
        ps = ctx.enter_context(nc.psum_tensor(f"{tag}_ps", [P, 8, 512], F32))

        def kf(c):
            return heads_out[:, :, c * P:(c + 1) * P]

        NXT = NC + (ctx_in is not None)
        ONES = 2 if linear else 1
        NS = 6 if linear else 4
        xs_in, ctx_loaded = signal("xs_in", 16), signal("ctx_loaded", 16)
        res_in = [signal(f"res_in{i}", 32) for i in range(2)]
        res_out = [signal(f"res_out{i}", 32) for i in range(2)]
        stat, rstd_done, xn_done = signal("stat", 3 * NT), signal("rstd_done", 1), signal("xn_done", NT)
        xT_ready, xT_hi, xT_lo = signal("xT_ready", NXT), signal("xT_hi", NXT), signal("xT_lo", NXT)
        q_ready, q_hi, q_lo = signal("q_ready", 2 * NC), signal("q_hi", 2 * NC), signal("q_lo", 2 * NC)
        rot_mul, rot_done = signal("rot_mul", 4 * NC), signal("rot_done", 2 * NC)
        v_ready, v_hi, v_lo = signal("v_ready", NT), signal("v_hi", NT), signal("v_lo", NT)
        stack_ready, stack_done = signal("stack_ready", 2 * H), signal("stack_done", 2 * H)
        qk_ready, max_done = signal("qk_ready", H * NT), signal("max_done", H * NT)
        dneg_done = signal("dneg_done", H)
        kq_ready, exp_done = signal("kq_ready", H * NT), signal("exp_done", H * NT)
        ph_act, ph_dve = signal("ph_act", H * len(PH_ACT)), signal("ph_dve", H * (NT - len(PH_ACT)))
        pl_dve, pl_pool = signal("pl_dve", H * len(PL_DVE)), signal("pl_pool", H * (NT - len(PL_DVE)))
        pv_step, u_done, uT_ready = signal("pv_step", H * NT), signal("u_done", H), signal("uT_ready", H)
        norm = signal("norm", H * NS)
        oT_ready, oT_hi, oT_lo = signal("oT_ready", NC), signal("oT_hi", NC), signal("oT_lo", NC)
        y_ready, y_done = signal("y_ready", NT), signal("y_done", NT)
        sum_done, clip_done, fexp_done, feat_done = (signal(n, 2 * NC) for n in ("sum_done", "clip_done", "fexp_done", "feat_done"))
        kf_ready, kf_done, v_one_done = signal("kf_ready", NC), signal("kf_done", NC), signal("v_one_done", NC)
        one_col = signal("one_col", 1)
        mem_ready, mem_done = signal("mem_ready", NC), signal("mem_done", NC)
        mo_ready, mo_step = signal("mo_ready", 2 * NC), signal("mo_step", 6 * NC)
        const_in, ones_done, gates = sem("const_in"), sem("ones_done"), sem("gates")

        reader, bank_of, before = {}, {}, {}
        last = [None] * 8

        def plan(key, bank, sig, n):
            reader[key], bank_of[key], before[key] = (sig, n), bank, last[bank]
            last[bank] = key

        pairs = [(w, c) for w in "qk" for c in ((0, 2, 1, 3) if linear else range(NC))]
        stage = [(("xT", c), xT_lo, c + 1) for c in range(NC)]
        stage += [(("cT", 0), xT_lo, NXT)] if ctx_in is not None else []
        stage += [(k, rot_done, n // 2 * 2 + 2) if linear else (k, q_lo, n + 1) for n, k in enumerate(pairs)]
        stage += [(("v", t), v_lo, t + 1) for t in range(NT)]
        for c in range(NC if linear else 0):
            stage += [(("kf", c), kf_done, c + 1), (("mem", c), mem_done, c + 1),
                      (("mo", c, 0), mo_step, 6 * c + 3), (("mo", c, 1), mo_step, 6 * c + 6)]
        RING = 4
        for i in range(-1, H):
            for kind, t in SCORES:
                if kind == "kq" and i >= 0:
                    stage.append((("kq", i, t), exp_done, i * NT + t + 1))
                if kind == "qk" and i + 1 < H:
                    stage.append((("qk", i + 1, t), max_done, (i + 1) * NT + t + 1))
        for n, (key, sig, k) in enumerate(stage):
            plan(key, n % RING, sig, k)
        for h in range(H):
            plan(("pv", h), 4 + h % 2, u_done, h + 1)
        for i in range(-2, H + 2):
            if i + 2 < H:
                plan(("qs", i + 2), 6, stack_done, 2 * (i + 2) + 1)
                plan(("ks", i + 2), 7, stack_done, 2 * (i + 2) + 2)
            if i >= 2:
                plan(("uT", i - 2), 6 + i % 2, norm, (i - 1) * NS)
        for c in range(NC):
            plan(("oT", c), c, oT_lo, c + 1)
        for t in range(NT):
            plan(("y", t), t, y_done, t + 1)

        def bank(key, lo=0, hi=512, rows=P):
            return ps[0:rows, bank_of[key], lo:hi]

        def low_done(eng, b, h, t):
            sig, ts = (pl_dve, PL_DVE) if t in PL_DVE else (pl_pool, PL_POOL)
            sig.wait(eng, b, h * len(ts) + ts.index(t) + 1)

        def high_done(eng, b, h, t):
            sig, ts = (ph_act, PH_ACT) if t in PH_ACT else (ph_dve, PH_DVE)
            sig.wait(eng, b, h * len(ts) + ts.index(t) + 1)

        def keys_from(t):
            return t * P if causal else 0

        def rotated(n):
            return (probs, heads_out)[n // 2 % 2][:, 2 * (n % 2), :]

        def select(j, kind):
            at = {"q_lo": 0, "k_lo": 1, "q_hi": 2, "k_hi": 3}[kind] * HD
            return env.sel[:, j, at:at + P]

        block = ctx.enter_context(nc.Block())

        @block.sync
        def _(sp):
            if linear:
                sp.dma_start(cosT[:], env.cos.rearrange("(c p) s -> p c s", p=P)).then_inc(const_in, 16)
                sp.dma_start(sinT[:], env.sin.rearrange("(c p) s -> p c s", p=P)).then_inc(const_in, 16)
                sp.dma_start(gate_e[:], gate.rearrange("a h b c -> (a b c h)").partition_broadcast(P)).then_inc(const_in, 16)
            x_rows = x_in.rearrange("(b t p) d -> b p t d", p=P, t=NT)
            tile_in = x_in.rearrange("(b t p) d -> t b p d", p=P, t=NT)
            tile_out = x_out.rearrange("(b t p) d -> t b p d", p=P, t=NT)

            def load(b):
                sp.dma_start(xs[:], x_rows[bass.ds(b, 1)].rearrange("b p t d -> (b p) t d")).then_inc(xs_in.sem, 16)
                if ctx_in is not None:
                    sp.dma_start(ctx_sb[:], ctx_in.rearrange("(b t p) d -> b p t d", p=P, t=NT)[bass.ds(b, 1)]
                                 .rearrange("b p t d -> (b p) t d")).then_inc(ctx_loaded.sem, 16)

            def store(b, t):
                y_done.wait(sp, b, t + 1)
                sp.dma_start(tile_out[t, bass.ds(b, 1)].rearrange("b p d -> (b p) d"), res[:, t % 2, :]).then_inc(res_out[t % 2].sem, 16)

            def body(b, more):
                if more:
                    xT_ready.wait(sp, b, NXT)
                    if linear:
                        mo_step.wait(sp, b, 6 * NC)
                    load(b + 1)
                for t in range(NT):
                    res_out[t % 2].wait(sp, b, t // 2 * 16)
                    sp.dma_start(res[:, t % 2, :], tile_in[t, bass.ds(b, 1)].rearrange("b p d -> (b p) d")).then_inc(res_in[t % 2].sem, 16)
                    if t >= 1:
                        store(b, t - 1)
                store(b, NT - 1)

            load(0)
            batches(sp, body)
            for i in range(2):
                res_out[i].wait(sp, B, 0)

        @block.tensor
        def _(pe):
            def take(b, key):
                prev = before[key] if before[key] is not None else last[bank_of[key]]
                sig, n = reader[prev]
                sig.wait(pe, b, n if before[key] is not None else 0)

            def stack(b, h):
                c, j = h // HC, h % HC
                for which, (hi, lo) in (("qs", qT), ("ks", kT)):
                    take(b, (which, h))
                    pe.matmul(bank((which, h)), select(j, which[0] + "_hi"), hi[:, c, :], start=True, stop=False)
                    pe.matmul(bank((which, h)), select(j, which[0] + "_lo"), lo[:, c, :], start=False, stop=True).then_inc(stack_ready.sem, 1)

            def scores_qk(b, h, t):
                if t == 0:
                    stack_done.wait(pe, b, 2 * h + 2)
                take(b, ("qk", h, t))
                n = (t + 1) * P if causal else S
                mm = pe.matmul(bank(("qk", h, t), 0, n), qs[:, h % NST, t * P:(t + 1) * P], ks[:, h % NST, 0:n],
                               start=True, stop=not causal, skip_group_check=True)
                if causal:
                    mm = pe.matmul(bank(("qk", h, t), n - P, n), env.ident_r[:], causal_qk[:],
                                   start=False, stop=True, skip_group_check=True)
                mm.then_inc(qk_ready.sem, 1)

            def scores_kq(b, h, t):
                take(b, ("kq", h, t))
                if t == 0:
                    dneg_done.wait(pe, b, h + 1)
                lo = keys_from(t)
                pe.matmul(bank(("kq", h, t), lo, S), ks[:, h % NST, t * P:(t + 1) * P], qs[:, h % NST, lo:S],
                          start=True, stop=False, skip_group_check=True)
                if causal:
                    pe.matmul(bank(("kq", h, t), lo, lo + P), env.ident_r[:], causal_kq[:],
                              start=False, stop=False, skip_group_check=True)
                mm = pe.matmul(bank(("kq", h, t), lo, S), env.one_r[:].to_broadcast([P, P]), dneg[:, h % 2, lo:S], start=False, stop=True, skip_group_check=True)
                mm.then_inc(kq_ready.sem, 1)

            def weigh(b, h, t):
                if t == 0:
                    take(b, ("pv", h))
                low_done(pe, b, h, t)
                lo = keys_from(t)
                for part in (probs_hi, probs_lo):
                    mm = pe.matmul(bank(("pv", h), lo, S, VW - 1), v_split[:, t, h, 0:VW - 1], part[:, t, lo:S],
                                   start=t == 0 and part is probs_hi, stop=t == NT - 1 and part is probs_lo, skip_group_check=True)
                mm.then_inc(pv_step.sem, 1)

            def turn_sums(b, h):
                u_done.wait(pe, b, h + 1)
                take(b, ("uT", h))
                for t in range(NT):
                    mm = pe.transpose(bank(("uT", h), t * VW, t * VW + VW - 1), u_sb[0:VW - 1, h % 2, t * P:(t + 1) * P],
                                      env.ident[0:VW - 1, 0:VW - 1])
                mm.then_inc(uT_ready.sem, 1)

            def linear_chunk(b, c):
                feat_done.wait(pe, b, 2 * c + 1)
                take(b, ("kf", c))
                for t in range(NT):
                    mm = pe.transpose(bank(("kf", c), t * P, (t + 1) * P), feat_k[:, t * P:(t + 1) * P], env.ident[:])
                mm.then_inc(kf_ready.sem, 1)
                kf_done.wait(pe, b, c + 1)
                if c == 0:
                    one_col.wait(pe, b, 1)
                v_one_done.wait(pe, b, c + 1)
                take(b, ("mem", c))
                for t in range(NT):
                    mm = pe.matmul(bank(("mem", c), 0, HW), kf(c)[:, t, :], v_one[:, t].rearrange("p h w -> p (h w)"),
                                   start=t == 0, stop=t == NT - 1)
                mm.then_inc(mem_ready.sem, 1)
                mem_done.wait(pe, b, c + 1)
                feat_done.wait(pe, b, 2 * c + 2)
                for half in range(2):
                    take(b, ("mo", c, half))
                    for t in range(2):
                        at = (2 * half + t) * P
                        mm = pe.matmul(bank(("mo", c, half), t * HW, (t + 1) * HW), feat_q[:, at:at + P],
                                       mem.rearrange("p h w -> p (h w)"), start=t == 0, stop=t == 1, skip_group_check=True)
                    mm.then_inc(mo_ready.sem, 1)

            def body(b, more):
                for c in range(NC):
                    take(b, ("xT", c))
                    for t in range(NT):
                        if c == 0:
                            xn_done.wait(pe, b, t + 1)
                        mm = pe.transpose(bank(("xT", c), t * P, (t + 1) * P), xs[:, t, c * P:(c + 1) * P], env.ident[:])
                    mm.then_inc(xT_ready.sem, 1)
                if ctx_in is not None:
                    take(b, ("cT", 0))
                    ctx_loaded.wait(pe, b, 16)
                    for t in range(NT):
                        mm = pe.transpose(bank(("cT", 0), t * P, (t + 1) * P), ctx_sb[:, t, :], env.ident[:])
                    mm.then_inc(xT_ready.sem, 1)

                xT_lo.wait(pe, b, NC)
                for which, c in pairs:
                    from_ctx = which == "k" and ctx_in is not None
                    if from_ctx:
                        xT_lo.wait(pe, b, NXT)
                    w, src = (wqT if which == "q" else wkT), (cT if from_ctx else xnT)
                    take(b, (which, c))
                    for dc in range(KC if which == "k" else NC):
                        mm = split_mm(pe, bank((which, c)), [p[:, dc, c * P:(c + 1) * P] for p in w], [p[:, dc, :] for p in src],
                                      dc == 0, dc == (KC if which == "k" else NC) - 1)
                    mm.then_inc(q_ready.sem, 1)
                for t in range(NT):
                    take(b, ("v", t))
                    for dc in range(KC):
                        mm = split_mm(pe, bank(("v", t)), [p[:, dc, t * P:(t + 1) * P] for p in (xnT if ctx_in is None else cT)],
                                      [p[:, dc, :] for p in wvT], dc == 0, dc == KC - 1)
                    mm.then_inc(v_ready.sem, 1)
                for c in range(NC if linear else 0):
                    linear_chunk(b, c)

                q_lo.wait(pe, b, 2 * NC)
                stack(b, 0)
                stack(b, 1)
                for t in range(NT):
                    scores_qk(b, 0, t)
                v_lo.wait(pe, b, NT)
                for i in range(H + 2):
                    for kind, t in SCORES:
                        if kind == "kq" and t >= 1 and 1 <= i <= H:
                            weigh(b, i - 1, t - 1)
                        if kind == "kq" and i < H:
                            scores_kq(b, i, t)
                        if kind == "qk" and i + 1 < H:
                            scores_qk(b, i + 1, t)
                        if (kind, t) == ("kq", 2) and i + 2 < H:
                            stack(b, i + 2)
                    if i >= 2:
                        turn_sums(b, i - 2)
                    if 1 <= i <= H:
                        weigh(b, i - 1, NT - 1)

                norm.wait(pe, b, H * NS)
                for c in range(NC):
                    take(b, ("oT", c))
                    for t in range(NT):
                        mm = pe.transpose(bank(("oT", c), t * P, (t + 1) * P), heads_out[:, t, c * P:(c + 1) * P], env.ident[:])
                    mm.then_inc(oT_ready.sem, 1)
                for t in range(NT):
                    take(b, ("y", t))
                    for dc in range(NC):
                        if t == 0:
                            oT_lo.wait(pe, b, dc + 1)
                        mm = split_mm(pe, bank(("y", t)), [p[:, dc, t * P:(t + 1) * P] for p in (probs_hi, probs_lo)],
                                      [p[:, dc, :] for p in woT], dc == 0, dc == NC - 1)
                    mm.then_inc(y_ready.sem, 1)

            pe.wait_ge(ones_done, ONES)
            batches(pe, body)

        @block.scalar
        def _(act):
            def stack_out(b, h):
                for n, (dst, which) in enumerate(((qs, "qs"), (ks, "ks"))):
                    stack_ready.wait(act, b, 2 * h + n + 1)
                    act.copy(dst[:, h % NST, :], bank((which, h))).then_inc(stack_done.sem, 1)

            def body(b, more):
                for c in range(NXT):
                    xT_ready.wait(act, b, c + 1)
                    if c < NC:
                        act.copy(xnT[0][:, c, :], bank(("xT", c))).then_inc(xT_hi.sem, 1)
                    else:
                        act.copy(cT[0][:, 0, :], bank(("cT", 0))).then_inc(xT_hi.sem, 1)
                for n, (which, c) in enumerate(pairs):
                    dst = (qT if which == "q" else kT)[0][:, c, :]
                    if linear:
                        rot_done.wait(act, b, n + 1)
                        act.copy(dst, rotated(n)).then_inc(q_hi.sem, 1)
                    else:
                        q_ready.wait(act, b, n + 1)
                        act.copy(dst, bank((which, c))).then_inc(q_hi.sem, 1)
                for t in range(NT):
                    v_ready.wait(act, b, t + 1)
                    act.copy(v_split[:, t, :, 0:HD], bank(("v", t)).rearrange("p (h w) -> p h w", w=HD)).then_inc(v_hi.sem, 1)
                for c in range(NC if linear else 0):
                    for w in range(2):
                        clip_done.wait(act, b, 2 * c + w + 1)
                        act.activation(probs[:, 2 * w + 1, :], probs[:, 2 * w + 1, :], ACT.Exp).then_inc(fexp_done.sem, 1)
                    kf_ready.wait(act, b, c + 1)
                    act.copy(kf(c), bank(("kf", c)).rearrange("p (t d) -> p t d", d=P)).then_inc(kf_done.sem, 1)
                stack_out(b, 0)
                stack_out(b, 1)
                for i in range(H + 2):
                    for t in range(NT):
                        lo = keys_from(t)
                        if i < H:
                            kq_ready.wait(act, b, i * NT + t + 1)
                            if i >= 1:
                                low_done(act, b, i - 1, t)
                            act.activation(probs[:, t, lo:S], bank(("kq", i, t), lo, S), ACT.Exp, scale=SCALE).then_inc(exp_done.sem, 1)
                        if t == 0 and i >= 2:
                            h = i - 2
                            pv_step.wait(act, b, (h + 1) * NT)
                            if h >= 2:
                                uT_ready.wait(act, b, h - 1)
                            act.copy(u_sb[0:VW - 1, h % 2, :], bank(("pv", h), 0, S, VW - 1)).then_inc(u_done.sem, 1)
                        if t == 2 and i + 2 < H:
                            stack_out(b, i + 2)
                        if t in PH_ACT and i < H:
                            exp_done.wait(act, b, i * NT + t + 1)
                            if i >= 1:
                                pv_step.wait(act, b, (i - 1) * NT + t + 1)
                            act.copy(probs_hi[:, t, lo:S], probs[:, t, lo:S]).then_inc(ph_act.sem, 1)
                for c in range(NC):
                    oT_ready.wait(act, b, c + 1)
                    act.copy(probs_hi[:, c, :], bank(("oT", c))).then_inc(oT_hi.sem, 1)

            if linear:
                act.wait_ge(const_in, 48)
                act.activation(gate_e[:], gate_e[:], ACT.Exp, scale=-1.0).then_inc(gates, 1)
            batches(act, body)

        @block.vector
        def _(dve):
            def layernorm(b):
                xs_in.wait(dve, b, 16)
                for t in range(NT):
                    dve.bn_stats(stats[:, t, :], xs[:, t, :]).then_inc(stat.sem, 1)
                stat.wait(dve, b, NT)
                dve.memset(carrier[:], 0.0)
                for t in range(NT):
                    dve.bn_aggr(mv[:, t, :], stats[:, t, :]).then_inc(stat.sem, 1)
                for t in range(NT):
                    stat.wait(dve, b, NT + t + 1)
                    dve.tensor_scalar(mv[:, t, 1:2], mv[:, t, 1:2], EPS, None, ALU.add).then_inc(stat.sem, 1)
                rstd_done.wait(dve, b, 1)
                for t in range(NT):
                    dve.tensor_scalar(xs[:, t, :], xs[:, t, :], mv[:, t, 0:1], rstd[:, t:t + 1],
                                      ALU.subtract, ALU.mult).then_inc(xn_done.sem, 1)

            def low(dst, hi, src, sig):
                dve.tensor_tensor(dst, src, hi.bitcast(F32), ALU.subtract).then_inc(sig.sem, 1)

            def maxima(b, h, t):
                n = (t + 1) * P if causal else S
                qk_ready.wait(dve, b, h * NT + t + 1)
                dve.reduce_max(negmax[:, h % 2, t:t + 1], bank(("qk", h, t), 0, n), AX.X, negate=True).then_inc(max_done.sem, 1)

            def diagonals(b, h):
                max_done.wait(dve, b, (h + 1) * NT)
                if h >= 2:
                    kq_ready.wait(dve, b, (h - 1) * NT)
                dve.tensor_tensor(dneg[:, h % 2, :].rearrange("p (t k) -> p t k", k=P), env.ident[:].rearrange("p (o k) -> p o k", o=1).to_broadcast([P, NT, P]),
                                  negmax[:, h % 2, :].rearrange("p (t o) -> p t o", o=1).to_broadcast([P, NT, P]), ALU.mult).then_inc(dneg_done.sem, 1)

            def high(b, h, t):
                lo = keys_from(t)
                exp_done.wait(dve, b, h * NT + t + 1)
                if h >= 1:
                    pv_step.wait(dve, b, (h - 1) * NT + t + 1)
                dve.tensor_copy(probs_hi[:, t, lo:S], probs[:, t, lo:S]).then_inc(ph_dve.sem, 1)

            def low_probs(b, h, t):
                lo = keys_from(t)
                high_done(dve, b, h, t)
                low(probs_lo[:, t, lo:S], probs_hi[:, t, lo:S], probs[:, t, lo:S], pl_dve)

            def normalise(b, h):
                uT = bank(("uT", h), 0, NT * VW).rearrange("p (t w) -> p t w", w=VW)
                out = heads_out[:, :, h * HD:(h + 1) * HD]
                n = h * NS

                def step(k, ins):
                    ins.then_inc(norm.sem, 1)
                    norm.wait(dve, b, n + k)

                uT_ready.wait(dve, b, h + 1)
                step(1, dve.reciprocal(rsum[:], uT[:, :, HD]))
                if linear:
                    step(2, dve.tensor_scalar(rsum[:], rsum[:], g_not[:, h:h + 1], None, ALU.mult))
                by = rsum[:].rearrange("p (t o) -> p t o", o=1).to_broadcast([P, NT, HD])
                dve.tensor_tensor(piece_a[:], uT[:, :, 0:HD], by, ALU.mult).then_inc(norm.sem, 1)
                dve.tensor_tensor(piece_b[:], uT[:, :, HD + 1:2 * HD + 1], by, ALU.mult).then_inc(norm.sem, 1)
                if linear:
                    norm.wait(dve, b, n + 4)
                    step(5, dve.tensor_tensor(piece_a[:], piece_a[:], piece_b[:], ALU.add))
                    dve.tensor_tensor(out, out, piece_a[:], ALU.add).then_inc(norm.sem, 1)
                else:
                    norm.wait(dve, b, n + 3)
                    dve.tensor_tensor(out, piece_a[:], piece_b[:], ALU.add).then_inc(norm.sem, 1)

            def rotate(b, pair):
                which, c = pairs[2 * pair]
                tmp = (probs, heads_out)[pair % 2]
                first, second = bank((which, c)), bank((which, c + 2))
                q_ready.wait(dve, b, 2 * pair + 2)
                if pair >= 2:
                    q_lo.wait(dve, b, 2 * pair - 2)
                for k, (src, table) in enumerate(((first, cosT), (second, sinT), (second, cosT), (first, sinT))):
                    dve.tensor_tensor(tmp[:, k, :], src, table[:, c, :], ALU.mult).then_inc(rot_mul.sem, 1)
                rot_mul.wait(dve, b, 4 * pair + 2)
                dve.tensor_tensor(tmp[:, 0, :], tmp[:, 0, :], tmp[:, 1, :], ALU.subtract).then_inc(rot_done.sem, 1)
                rot_mul.wait(dve, b, 4 * pair + 4)
                dve.tensor_tensor(tmp[:, 2, :], tmp[:, 2, :], tmp[:, 3, :], ALU.add).then_inc(rot_done.sem, 1)

            def features(b, c):
                for w, feat in enumerate((feat_k, feat_q)):
                    sum_done.wait(dve, b, 2 * c + w + 1)
                    dve.tensor_scalar(probs[:, 2 * w + 1, :], probs[:, 2 * w, :], 0.0, None, ALU.min).then_inc(clip_done.sem, 1)
                for w, feat in enumerate((feat_k, feat_q)):
                    fexp_done.wait(dve, b, 2 * c + w + 1)
                    if c >= 1:
                        (kf_ready.wait(dve, b, c) if w == 0 else mo_ready.wait(dve, b, 2 * c))
                    dve.scalar_tensor_tensor(out=feat, in0=probs[:, 2 * w, :], scalar=0.0, in1=probs[:, 2 * w + 1, :],
                                             op0=ALU.max, op1=ALU.add).then_inc(feat_done.sem, 1)

            def linear_out(b, c):
                mem_ready.wait(dve, b, c + 1)
                if c >= 1:
                    mo_ready.wait(dve, b, 2 * c)
                dve.tensor_tensor(mem.rearrange("p h w -> p (h w)"), bank(("mem", c), 0, HW), env.blockmask[:], ALU.mult).then_inc(mem_done.sem, 1)
                for half in range(2):
                    mo = bank(("mo", c, half), 0, 2 * HW).rearrange("p (t h w) -> p t h w", h=HC, w=HD + 1)
                    n = 6 * c + 3 * half
                    mo_ready.wait(dve, b, 2 * c + half + 1)
                    mo_step.wait(dve, b, n)
                    dve.reciprocal(den, mo[:, :, :, HD]).then_inc(mo_step.sem, 1)
                    mo_step.wait(dve, b, n + 1)
                    dve.tensor_tensor(den, den, g_sig[:, HC * c:HC * c + HC].rearrange("p (o h) -> p o h", o=1).to_broadcast([P, 2, HC]),
                                      ALU.mult).then_inc(mo_step.sem, 1)
                    mo_step.wait(dve, b, n + 2)
                    dve.tensor_tensor(heads_out[:, 2 * half:2 * half + 2, c * P:(c + 1) * P].rearrange("p t (h w) -> p t h w", w=HD),
                                      mo[:, :, :, 0:HD], den.rearrange("p t (h o) -> p t h o", o=1).to_broadcast([P, 2, HC, HD]),
                                      ALU.mult).then_inc(mo_step.sem, 1)

            def body(b, more):
                for c in range(NXT):
                    hi, lo = (xnT[0][:, c, :], xnT[1][:, c, :]) if c < NC else (cT[0][:, 0, :], cT[1][:, 0, :])
                    xT_hi.wait(dve, b, c + 1)
                    low(lo, hi, bank(("xT", c) if c < NC else ("cT", 0)), xT_lo)
                if linear:
                    xT_ready.wait(dve, b, NXT)
                    dve.memset(v_one[:, :, :, HD:HD + 1], 1.0).then_inc(one_col.sem, 1)
                    for pr in range(NC):
                        rotate(b, pr)
                else:
                    for n, (which, c) in enumerate(pairs):
                        hi, lo = (p[:, c, :] for p in (qT if which == "q" else kT))
                        q_hi.wait(dve, b, n + 1)
                        low(lo, hi, bank((which, c)), q_lo)
                for t in range(NT):
                    v_hi.wait(dve, b, t + 1)
                    low(v_split[:, t, :, HD + 1:2 * HD + 1], v_split[:, t, :, 0:HD],
                        bank(("v", t)).rearrange("p (h w) -> p h w", w=HD), v_lo)
                for c in range(NC if linear else 0):
                    features(b, c)
                    linear_out(b, c)
                for t in range(NT):
                    maxima(b, 0, t)
                diagonals(b, 0)
                for i in range(H + 2):
                    if i + 1 < H:
                        for t in range(NT):
                            maxima(b, i + 1, t)
                        diagonals(b, i + 1)
                    for t in range(NT if i < H else 0):
                        if t in PH_DVE and t < NT - 1:
                            high(b, i, t)
                        if t in PL_DVE and t < NT - 1:
                            low_probs(b, i, t)
                    if i >= 2:
                        normalise(b, i - 2)
                    if i < H and NT - 1 in PH_DVE:
                        high(b, i, NT - 1)
                    if i < H and NT - 1 in PL_DVE:
                        low_probs(b, i, NT - 1)
                    if more and i == H // 2:
                        layernorm(b + 1)
                for c in range(NC):
                    oT_hi.wait(dve, b, c + 1)
                    low(probs_lo[:, c, :], probs_hi[:, c, :], bank(("oT", c)), oT_lo)
                for t in range(NT):
                    y_ready.wait(dve, b, t + 1)
                    res_in[t % 2].wait(dve, b, t // 2 * 16 + 16)
                    dve.tensor_tensor(res[:, t % 2, :], bank(("y", t)), res[:, t % 2, :], ALU.add).then_inc(y_done.sem, 1)

            dve.tensor_scalar(v_split[:, :, :, HD:HD + 1], env.ident[:, 0:NT * H].rearrange("p (t h o) -> p t h o", h=H, o=1), 0.0, 1.0,
                              ALU.mult, ALU.add).then_inc(ones_done, 1)
            if linear:
                dve.wait_ge(gates, 1)
                dve.tensor_scalar(gate_e[:], gate_e[:], 1.0, None, ALU.add).then_inc(gates, 1)
                dve.wait_ge(gates, 2)
                dve.reciprocal(g_sig[:], gate_e[:]).then_inc(gates, 1)
                dve.wait_ge(gates, 3)
                dve.tensor_scalar(g_not[:], g_sig[:], -1.0, 1.0, ALU.mult, ALU.add).then_inc(ones_done, 1)
                dve.wait_ge(ones_done, 2)
            layernorm(0)
            batches(dve, body)

        @block.gpsimd
        def _(pool):
            def rstds(b):
                stat.wait(pool, b, 3 * NT)
                pool.tensor_tensor(rstd[:], mv[:, :, 1], env.minus_half[:, 0:NT], ALU.pow).then_inc(rstd_done.sem, 1)

            def body(b, more):
                if linear:
                    for n, (which, c) in enumerate(pairs):
                        hi, lo = (p[:, c, :] for p in (qT if which == "q" else kT))
                        q_hi.wait(pool, b, n + 1)
                        pool.tensor_tensor(lo, rotated(n), hi.bitcast(F32), ALU.subtract).then_inc(q_lo.sem, 1)
                    for c in range(NC):
                        for w, (hi, lo) in enumerate((kT, qT)):
                            q_lo.wait(pool, b, 2 * NC)
                            if c >= 1:
                                feat_done.wait(pool, b, 2 * c + w - 1)
                            pool.tensor_tensor(probs[:, 2 * w, :], hi[:, c, :].bitcast(F32), lo[:, c, :].bitcast(F32), ALU.add).then_inc(sum_done.sem, 1)
                        v_lo.wait(pool, b, NT)
                        if c >= 1:
                            mem_ready.wait(pool, b, c)
                        hs = slice(HC * c, HC * c + HC)
                        pool.tensor_tensor(v_one[:, :, :, 0:HD], v_split[:, :, hs, 0:HD].bitcast(F32),
                                           v_split[:, :, hs, HD + 1:2 * HD + 1].bitcast(F32), ALU.add).then_inc(v_one_done.sem, 1)
                for i in range(H):
                    for t in PL_POOL:
                        lo = keys_from(t)
                        high_done(pool, b, i, t)
                        if i >= 1:
                            pv_step.wait(pool, b, (i - 1) * NT + t + 1)
                        pool.tensor_tensor(probs_lo[:, t, lo:S], probs[:, t, lo:S], probs_hi[:, t, lo:S].bitcast(F32),
                                           ALU.subtract).then_inc(pl_pool.sem, 1)
                    if more and i == H // 2:
                        rstds(b + 1)

            rstds(0)
            batches(pool, body)


PH_ACT, PH_DVE = (0, 1), (2, 3)
PL_DVE, PL_POOL = (1,), (0, 2, 3)
SCORES = (("kq", 0), ("qk", 0), ("qk", 1), ("kq", 1), ("qk", 2), ("qk", 3), ("kq", 2), ("kq", 3))


def alloc_consts(nc, env, ctx):
    def sb(name, shape, dtype=F32):
        return ctx.enter_context(nc.sbuf_tensor(name, shape, dtype))

    env.ident, env.ident_r, env.one_r = sb("ident", [P, P]), sb("ident_r", [P, P], F32R), sb("one_r", [P, 1], F32R)
    env.sel = sb("sel", [P, HC, 7 * HD], F32R)
    env.blockmask = sb("blockmask", [P, HC * (HD + 1)])
    env.minus_half = sb("minus_half", [P, NT])



E_ROUTED, E_ALL, TOPK = 32, 64, 8
CAP = 256
SLOTS = E_ROUTED * CAP
W_SCALE, W_EPS = 1.5, 1e-20
GRAPH_HEADS = 4
GRAPH_TOP = max(1, int(S * 0.3))
GRAPH_SCALE = 1.0 / ((L // GRAPH_HEADS) ** 0.5 * GRAPH_HEADS)


def graph_and_router(nc, env, tag, x_in, x_out, ctx_in, wq, wk, gamma, w_cls, bias, slot_rows, none_row, slots, weights):
    with semaphores(nc) as take, ExitStack() as ctx:
        def sb(name, shape, dtype=F32):
            return ctx.enter_context(nc.sbuf_tensor(f"{tag}_{name}", shape, dtype))

        def sem(name):
            return take(f"{tag}_{name}")

        def signal(name, per, start=1):
            return Signal(nc, sem(name), per, start)

        def pair(name, shape):
            return sb(f"{name}_hi", shape, F32R), sb(f"{name}_lo", shape, F32R)

        wqT, wkT, wcT = pair("wq", [P, L]), pair("wk", [P, L]), pair("wc", [P, NC, E_ALL])
        w_raw, wc_raw = sb("w_raw", [P, 2, L]), sb("wc_raw", [E_ALL, D])
        cin = sb("cin", [P, NT, L])
        cT, qT, kT = pair("cT", [P, S]), pair("qT", [P, S]), pair("kT", [P, S])
        sim, work = sb("sim", [P, NT, S]), sb("work", [P, NT, S])
        top = sb("top", [P, NT, 8])
        xs, xo, xn = sb("xs", [P, NT, D]), sb("xo", [P, NT, D]), sb("xn", [P, NT, D])
        stats, mv, rstd = sb("stats", [P, NT, 6]), sb("mv", [P, NT, 2]), sb("rstd", [P, NT])
        carrier = sb("carrier", [P, 1])
        pool_carrier = sb("pool_carrier", [P, 2])
        gam = sb("gam", [P, 4])
        xnT = pair("xnT", [P, NC, S])
        bias_sb = sb("bias", [P, E_ALL])
        iota_i, iota = sb("iota_i", [P, E_ALL], I32), sb("iota", [P, E_ALL])
        before, ones = sb("before", [P, P], BF16), sb("ones", [P, P], BF16)
        tri = sb("tri", [P, P])
        logit, expd, score, biased = (sb(n, [P, NT, E_ALL]) for n in ("logit", "expd", "score", "biased"))
        r4 = sb("r4", [P, 6, NT])
        top_v, top_i = sb("top_v", [P, NT, TOPK]), sb("top_i", [P, NT, TOPK], U32)
        choice = sb("choice", [P, NT * TOPK])
        hot = sb("hot", [P, NT, TOPK, E_ALL])
        prod = sb("prod", [P, NT, TOPK, E_ALL])
        mask = sb("mask", [P, NT, E_ROUTED], BF16)
        place = sb("place", [P, NT, E_ROUTED])
        taken = sb("taken", [P, E_ROUTED])
        k8 = sb("k8", [P, 5, NT * TOPK])
        slot_now = sb("slot_now", [P, NT * TOPK], I32)
        zeros = sb("zeros", [P, 4 * D])
        ZERO_DMAS = SLOTS // P // 4
        zeroed = sem("zeroed")
        ps = ctx.enter_context(nc.psum_tensor(f"{tag}_ps", [P, 8, 512], F32))

        def bcast_last(ap, n, width):
            return ap.rearrange("p (n o) -> p n o", o=1).to_broadcast([P, n, width])

        def bcast_mid(ap, n):
            return ap.rearrange("p (o w) -> p o w", o=1).to_broadcast([P, n, ap.shape[-1]])

        MASK, ROUTE_STEPS = 11, 39
        in_sem, xs_in, ctx_sem, out_sem = sem("in"), signal("xs_in", 16), signal("ctx_in", 16), signal("x_out", 16)
        prep_pe, prep_act, prep_dve, prep_pool = sem("prep_pe"), sem("prep_act"), sem("prep_dve"), sem("prep_pool")
        turn, hi, lo = signal("turn", 3), signal("hi", 3), signal("lo", 3)
        xt, xhi, xlo = signal("xt", NC), signal("xhi", NC), signal("xlo", NC)
        sim_ready, sim_copied = signal("sim_ready", NT), signal("sim_copied", NT)
        ROUNDS = (GRAPH_TOP - 1) // 8
        maxed, struck = signal("maxed", NT * (ROUNDS + 1)), signal("struck", NT * ROUNDS)
        tanh_done, kept, adj = signal("tanh_done", NT), signal("kept", NT), signal("adj", NT)
        adjT, sums = signal("adjT", NT), signal("sums", 3 * NT)
        stat, rstd_done, xn_done = signal("stat", 6 * NT), signal("rstd_done", 2), signal("xn_done", 2 * NT)
        logits_ready, exp_done, route = signal("logits_ready", 1), signal("exp_done", 1), signal("route", ROUTE_STEPS)
        counted, slots_done, scattered = signal("counted", 1), signal("slots_done", 1), signal("scattered", NT * TOPK * 16, start=0)
        stored = signal("stored", 1)

        block = ctx.enter_context(nc.Block())

        @block.sync
        def _(sp):
            sp.wait_ge(prep_pool, 4)
            many = slot_rows.rearrange("(p q r) d -> q p (r d)", p=P, r=zeros.shape[1] // D)
            for q in range(ZERO_DMAS):
                sp.dma_start(many[q], zeros[:]).then_inc(zeroed, 16)
            sp.dma_start(none_row, zeros[0:1, 0:D]).then_inc(zeroed, 16)
            sp.dma_start(w_raw[:, 0, :], wq).then_inc(in_sem, 16)
            sp.dma_start(w_raw[:, 1, :], wk).then_inc(in_sem, 16)
            sp.dma_start(wc_raw[:], w_cls).then_inc(in_sem, 16)
            sp.dma_start(bias_sb[:], bias.partition_broadcast(P)).then_inc(in_sem, 16)
            sp.dma_start(gam[:, 0:1], gamma.partition_broadcast(P)).then_inc(in_sem, 16)

            def load(b):
                sp.dma_start(cin[:], ctx_in.rearrange("(b t p) d -> b p t d", p=P, t=NT)[bass.ds(b, 1)]
                             .rearrange("b p t d -> (b p) t d")).then_inc(ctx_sem.sem, 16)
                sp.dma_start(xs[:], x_in.rearrange("(b t p) d -> b p t d", p=P, t=NT)[bass.ds(b, 1)]
                             .rearrange("b p t d -> (b p) t d")).then_inc(xs_in.sem, 16)

            def body(b, more):
                sums.wait(sp, b, 3 * NT)
                sp.dma_start(x_out.rearrange("(b t p) d -> b p t d", p=P, t=NT)[bass.ds(b, 1)]
                             .rearrange("b p t d -> (b p) t d"), xo[:]).then_inc(out_sem.sem, 16)
                if more:
                    load(b + 1)

            load(0)
            batches(sp, body)
            out_sem.wait(sp, B, 0)
            sp.wait_ge(zeroed, 16 * (ZERO_DMAS + 1))

        @block.tensor
        def _(pe):
            pe.wait_ge(in_sem, 80)
            for n in range(2):
                pe.transpose(ps[:, n, 0:P], w_raw[:, n, :], env.ident[:]).then_inc(prep_pe, 1)
            for c in range(NC):
                mm = pe.transpose(ps[:, 2, c * E_ALL:(c + 1) * E_ALL], wc_raw[:, c * P:(c + 1) * P], env.ident[0:E_ALL, 0:E_ALL])
            mm.then_inc(prep_pe, 1)
            pe.wait_ge(prep_dve, 4)

            def body(b, more):
                ctx_sem.wait(pe, b, 16)
                route.wait(pe, b, 0)
                for t in range(NT):
                    mm = pe.transpose(ps[:, 0, t * P:(t + 1) * P], cin[:, t, :], env.ident[:])
                mm.then_inc(turn.sem, 1)
                lo.wait(pe, b, 1)
                for n, w in enumerate((wqT, wkT)):
                    split_mm(pe, ps[:, 1 + n, :], [p[:] for p in w], [p[:] for p in cT], True, True).then_inc(turn.sem, 1)
                lo.wait(pe, b, 3)
                for t in range(NT):
                    if t == 0:
                        xlo.wait(pe, b, 0)
                    split_mm(pe, ps[:, 4 + t, :], [p[:, t * P:(t + 1) * P] for p in qT], [p[:] for p in kT], True, True
                             ).then_inc(sim_ready.sem, 1)
                adj.wait(pe, b, NT)
                for t in range(NT):
                    for u in range(NT):
                        mm = pe.transpose(ps[:, 4 + t, u * P:(u + 1) * P], work[:, u, t * P:(t + 1) * P], env.ident[:])
                    mm.then_inc(adjT.sem, 1)
                xn_done.wait(pe, b, 2 * NT)
                for c in range(NC):
                    for t in range(NT):
                        mm = pe.transpose(ps[:, 4 + c, t * P:(t + 1) * P], xn[:, t, c * P:(c + 1) * P], env.ident[:])
                    mm.then_inc(xt.sem, 1)
                xlo.wait(pe, b, NC)
                for t in range(NT):
                    for c in range(NC):
                        mm = split_mm(pe, ps[:, 0, t * E_ALL:(t + 1) * E_ALL], [p[:, c, t * P:(t + 1) * P] for p in xnT],
                                      [p[:, c, :] for p in wcT], t == 0 and c == 0, t == NT - 1 and c == NC - 1)
                mm.then_inc(logits_ready.sem, 1)
                route.wait(pe, b, MASK)
                for t in range(NT):
                    pe.matmul(ps[:, 3, t * E_ROUTED:(t + 1) * E_ROUTED], before[:], mask[:, t, :], start=t == 0, stop=False,
                              skip_group_check=True)
                    for u in range(t):
                        pe.matmul(ps[:, 3, t * E_ROUTED:(t + 1) * E_ROUTED], ones[:], mask[:, u, :], start=False, stop=False,
                                  skip_group_check=True)
                for u in range(NT):
                    mm = pe.matmul(ps[:, 3, NT * E_ROUTED:(NT + 1) * E_ROUTED], ones[:], mask[:, u, :], start=False, stop=u == NT - 1,
                                   skip_group_check=True)
                mm.then_inc(counted.sem, 1)

            batches(pe, body)

        @block.scalar
        def _(act):
            for n, w in enumerate((wqT, wkT)):
                act.wait_ge(prep_pe, n + 1)
                act.copy(w[0][:], ps[:, n, 0:P]).then_inc(prep_act, 1)
            act.wait_ge(prep_pe, 3)
            act.copy(wcT[0][:].rearrange("p c e -> p (c e)"), ps[:, 2, 0:NC * E_ALL]).then_inc(prep_act, 1)
            act.activation(gam[:, 1:2], gam[:, 0:1], ACT.Exp, scale=-1.0).then_inc(prep_act, 1)

            def body(b, more):
                for n, dst in enumerate((cT, qT, kT)):
                    turn.wait(act, b, n + 1)
                    act.copy(dst[0][:], ps[:, n, :]).then_inc(hi.sem, 1)
                for t in range(NT):
                    sim_ready.wait(act, b, t + 1)
                    act.copy(sim[:, t, :], ps[:, 4 + t, :]).then_inc(sim_copied.sem, 1)
                for t in range(NT):
                    maxed.wait(act, b, NT * (ROUNDS + 1))
                    act.activation(work[:, t, :], sim[:, t, :], ACT.Tanh, scale=0.5 * GRAPH_SCALE).then_inc(tanh_done.sem, 1)
                for c in range(NC):
                    xt.wait(act, b, c + 1)
                    act.copy(xnT[0][:, c, :], ps[:, 4 + c, :]).then_inc(xhi.sem, 1)
                route.wait(act, b, 2)
                act.activation(expd[:], logit[:], ACT.Exp).then_inc(exp_done.sem, 1)

            batches(act, body)

        @block.vector
        def _(dve):
            for n, w in enumerate((wqT, wkT)):
                dve.wait_ge(prep_act, n + 1)
                dve.tensor_tensor(w[1][:], ps[:, n, 0:P], w[0][:].bitcast(F32), ALU.subtract).then_inc(prep_dve, 1)
            dve.wait_ge(prep_act, 3)
            dve.tensor_tensor(wcT[1][:].rearrange("p c e -> p (c e)"), ps[:, 2, 0:NC * E_ALL],
                              wcT[0][:].rearrange("p c e -> p (c e)").bitcast(F32), ALU.subtract).then_inc(prep_dve, 1)
            dve.wait_ge(prep_pool, 3)
            dve.tensor_copy(before[:], tri[:]).then_inc(prep_dve, 1)
            dve.memset(taken[:], 0.0).then_inc(prep_dve, 1)
            dve.tensor_copy(iota[:], iota_i[:]).then_inc(prep_dve, 1)
            dve.wait_ge(prep_act, 4)
            dve.tensor_scalar(gam[:, 0:1], gam[:, 1:2], 1.0, None, ALU.add).then_inc(prep_dve, 1)
            dve.wait_ge(prep_dve, 7)
            dve.reciprocal(gam[:, 1:2], gam[:, 0:1]).then_inc(prep_dve, 1)
            dve.wait_ge(prep_dve, 8)
            dve.tensor_scalar(gam[:, 2:3], gam[:, 1:2], 0.25, None, ALU.mult).then_inc(prep_dve, 1)
            dve.tensor_scalar(gam[:, 3:4], gam[:, 1:2], -1.0, 1.0, ALU.mult, ALU.add).then_inc(prep_dve, 1)
            dve.wait_ge(prep_dve, 10)

            def layernorm(b, src, k):
                for t in range(NT):
                    dve.bn_stats(stats[:, t, :], src[:, t, :]).then_inc(stat.sem, 1)
                stat.wait(dve, b, 3 * NT * k + NT)
                dve.memset(carrier[:], 0.0)
                for t in range(NT):
                    dve.bn_aggr(mv[:, t, :], stats[:, t, :]).then_inc(stat.sem, 1)
                stat.wait(dve, b, 3 * NT * k + 2 * NT)
                for t in range(NT):
                    dve.tensor_scalar(mv[:, t, 1:2], mv[:, t, 1:2], EPS, None, ALU.add).then_inc(stat.sem, 1)
                rstd_done.wait(dve, b, k + 1)
                for t in range(NT):
                    dve.tensor_scalar(xn[:, t, :], src[:, t, :], mv[:, t, 0:1], rstd[:, t:t + 1],
                                      ALU.subtract, ALU.mult).then_inc(xn_done.sem, 1)

            def body(b, more):
                for n, dst in enumerate((cT, qT, kT)):
                    hi.wait(dve, b, n + 1)
                    dve.tensor_tensor(dst[1][:], ps[:, n, :], dst[0][:].bitcast(F32), ALU.subtract).then_inc(lo.sem, 1)
                xs_in.wait(dve, b, 16)
                stored.wait(dve, b, 0)
                out_sem.wait(dve, b, 0)
                layernorm(b, xs, 0)
                for t in range(NT):
                    xn_done.wait(dve, b, t + 1)
                    dve.scalar_tensor_tensor(out=xo[:, t, :], in0=xn[:, t, :], scalar=gam[:, 3:4], in1=xs[:, t, :],
                                             op0=ALU.mult, op1=ALU.add).then_inc(sums.sem, 1)
                sim_copied.wait(dve, b, NT)
                adjT.wait(dve, b, 0)
                dve.memset(carrier[:], 0.0)
                for r in range(ROUNDS + 1):
                    src = sim if r == 0 else work
                    for t in range(NT):
                        dve.max(top[:, t, :], src[:, t, :]).then_inc(maxed.sem, 1)
                    maxed.wait(dve, b, NT * (r + 1))
                    dve.memset(carrier[:], 0.0)
                    if r < ROUNDS:
                        for t in range(NT):
                            dve.match_replace(work[:, t, :], top[:, t, :], src[:, t, :], 2 * NEG).then_inc(struck.sem, 1)
                        struck.wait(dve, b, NT * (r + 1))
                        dve.memset(carrier[:], 0.0)
                last = GRAPH_TOP - 1 - 8 * ROUNDS
                for t in range(NT):
                    tanh_done.wait(dve, b, t + 1)
                    dve.tensor_scalar(sim[:, t, :], sim[:, t, :], top[:, t, last:last + 1], gam[:, 2:3],
                                      ALU.is_ge, ALU.mult).then_inc(kept.sem, 1)
                for t in range(NT):
                    kept.wait(dve, b, t + 1)
                    dve.scalar_tensor_tensor(out=work[:, t, :], in0=work[:, t, :], scalar=1.0, in1=sim[:, t, :],
                                             op0=ALU.add, op1=ALU.mult).then_inc(adj.sem, 1)
                for t in range(NT):
                    adj.wait(dve, b, t + 1)
                    sums.wait(dve, b, t + 1)
                    dve.tensor_tensor(xo[:, t, :], xo[:, t, :], work[:, t, :], ALU.add).then_inc(sums.sem, 1)
                for t in range(NT):
                    adjT.wait(dve, b, t + 1)
                    sums.wait(dve, b, NT + t + 1)
                    dve.tensor_tensor(xo[:, t, :], xo[:, t, :], ps[:, 4 + t, :], ALU.add).then_inc(sums.sem, 1)
                sums.wait(dve, b, 3 * NT)
                layernorm(b, xo, 1)
                for c in range(NC):
                    xhi.wait(dve, b, c + 1)
                    dve.tensor_tensor(xnT[1][:, c, :], ps[:, 4 + c, :], xnT[0][:, c, :].bitcast(F32), ALU.subtract).then_inc(xlo.sem, 1)
                router(b)

            def router(b):
                n = [0]

                def step(ins, wait=True):
                    ins.then_inc(route.sem, 1)
                    n[0] += 1
                    if wait:
                        route.wait(dve, b, n[0])

                lg = ps[:, 0, 0:NT * E_ALL].rearrange("p (t e) -> p t e", e=E_ALL)
                logits_ready.wait(dve, b, 1)
                step(dve.reduce_max(r4[:, 0, :], lg, AX.X))
                step(dve.tensor_tensor(logit[:], lg, bcast_last(r4[:, 0, :], NT, E_ALL), ALU.subtract))
                exp_done.wait(dve, b, 1)
                step(dve.reduce_sum(r4[:, 1, :], expd[:], AX.X))
                step(dve.reciprocal(r4[:, 2, :], r4[:, 1, :]))
                step(dve.tensor_tensor(score[:], expd[:], bcast_last(r4[:, 2, :], NT, E_ALL), ALU.mult))
                step(dve.tensor_tensor(biased[:], score[:], bcast_mid(bias_sb[:], NT), ALU.add))
                dve.memset(carrier[:], 0.0)
                for t in range(NT):
                    mx = dve.max(top_v[:, t, :], biased[:, t, :])
                step(mx)
                dve.memset(carrier[:], 0.0)
                for t in range(NT):
                    mx = dve.max_index(top_i[:, t, :], top_v[:, t, :], biased[:, t, :])
                step(mx)
                step(dve.tensor_copy(choice[:], top_i[:].rearrange("p t k -> p (t k)")))
                step(dve.tensor_tensor(hot[:].rearrange("p t k e -> p (t k) e"), bcast_mid(iota[:], NT * TOPK),
                                       bcast_last(choice[:], NT * TOPK, E_ALL), ALU.is_equal))
                with nc.allow_low_precision(reason="zeros and ones"):
                    step(dve.tensor_reduce(mask[:], hot[:, :, :, 0:E_ROUTED].rearrange("p t k e -> p t e k"), AX.X, ALU.add), wait=False)
                assert n[0] == MASK
                for t in range(NT):
                    step(dve.tensor_tensor(prod[:, t], hot[:, t], bcast_mid(score[:, t, :], TOPK), ALU.mult), wait=t == NT - 1)
                step(dve.reduce_sum(k8[:, 0, :], prod[:].rearrange("p t k e -> p (t k) e"), AX.X))
                step(dve.reduce_sum(r4[:, 3, :], k8[:, 0, :].rearrange("p (t k) -> p t k", k=TOPK), AX.X))
                step(dve.tensor_scalar(r4[:, 3, :], r4[:, 3, :], W_EPS, None, ALU.add))
                step(dve.reciprocal(r4[:, 4, :], r4[:, 3, :]))
                step(dve.tensor_scalar(r4[:, 4, :], r4[:, 4, :], W_SCALE, None, ALU.mult))
                step(dve.tensor_tensor(k8[:, 0, :].rearrange("p (t k) -> p t k", k=TOPK), k8[:, 0, :].rearrange("p (t k) -> p t k", k=TOPK),
                                       bcast_last(r4[:, 4, :], NT, TOPK), ALU.mult))
                step(dve.tensor_scalar(k8[:, 1, :], choice[:], float(E_ROUTED), None, ALU.is_lt))
                step(dve.tensor_tensor(k8[:, 2, :], k8[:, 0, :], k8[:, 1, :], ALU.mult))
                step(dve.tensor_tensor(k8[:, 0, :], k8[:, 0, :], k8[:, 2, :], ALU.subtract))
                step(dve.reduce_sum(r4[:, 5, :], k8[:, 0, :].rearrange("p (t k) -> p t k", k=TOPK), AX.X))
                step(dve.tensor_scalar(r4[:, 5, :], r4[:, 5, :], 1.0, None, ALU.add))
                step(dve.tensor_tensor(k8[:, 2, :].rearrange("p (t k) -> p t k", k=TOPK), k8[:, 2, :].rearrange("p (t k) -> p t k", k=TOPK),
                                       bcast_last(r4[:, 5, :], NT, TOPK), ALU.mult))
                counted.wait(dve, b, 1)
                step(dve.tensor_tensor(place[:], ps[:, 3, 0:NT * E_ROUTED].rearrange("p (t e) -> p t e", e=E_ROUTED),
                                       bcast_mid(taken[:], NT), ALU.add))
                step(dve.tensor_tensor(taken[:], taken[:], ps[:, 3, NT * E_ROUTED:(NT + 1) * E_ROUTED], ALU.add))
                for t in range(NT):
                    step(dve.tensor_tensor(prod[:, t, :, 0:E_ROUTED], hot[:, t, :, 0:E_ROUTED], bcast_mid(place[:, t, :], TOPK), ALU.mult),
                         wait=t == NT - 1)
                step(dve.reduce_sum(k8[:, 3, :], prod[:, :, :, 0:E_ROUTED].rearrange("p t k e -> p (t k) e"), AX.X))
                step(dve.tensor_scalar(k8[:, 0, :], k8[:, 3, :], float(CAP), None, ALU.is_lt))
                step(dve.tensor_tensor(k8[:, 1, :], k8[:, 1, :], k8[:, 0, :], ALU.mult))
                step(dve.scalar_tensor_tensor(out=k8[:, 4, :], in0=choice[:], scalar=float(CAP), in1=k8[:, 3, :], op0=ALU.mult, op1=ALU.add))
                step(dve.scalar_tensor_tensor(out=k8[:, 4, :], in0=k8[:, 4, :], scalar=-float(SLOTS), in1=k8[:, 1, :], op0=ALU.add, op1=ALU.mult))
                step(dve.tensor_scalar(k8[:, 4, :], k8[:, 4, :], float(SLOTS), None, ALU.add))
                at = b * (NT * TOPK)
                stored.wait(dve, b, 0)
                dve.tensor_tensor(weights[:, bass.ds(at, NT * TOPK)], k8[:, 2, :], k8[:, 1, :], ALU.mult)
                dve.tensor_copy(slots[:, bass.ds(at, NT * TOPK)], k8[:, 4, :])
                dve.tensor_copy(slot_now[:], k8[:, 4, :]).then_inc(slots_done.sem, 1)
                assert n[0] == ROUTE_STEPS, n[0]

            batches(dve, body)

        @block.gpsimd
        def _(pool):
            pool.memset(tri[:], 1.0).then_inc(prep_pool, 1)
            pool.memset(ones[:], 1.0)
            pool.wait_ge(prep_pool, 1)
            pool.affine_select(out=tri[:], in_=tri[:], compare_op=ALU.is_gt, fill=0.0, base=0,
                               pattern=[[1, P]], channel_multiplier=-1).then_inc(prep_pool, 1)
            pool.iota(iota_i[:], pattern=[[1, E_ALL]], base=0, channel_multiplier=0).then_inc(prep_pool, 1)
            pool.memset(zeros[:], 0.0).then_inc(prep_pool, 1)

            def body(b, more):
                for k in range(2):
                    stat.wait(pool, b, 3 * NT * (k + 1))
                    pool.tensor_tensor(rstd[:], mv[:, :, 1], env.minus_half[:, 0:NT], ALU.pow).then_inc(rstd_done.sem, 1)
                slots_done.wait(pool, b, 1)
                pool.tensor_tensor(pool_carrier[:, 0:1], env.minus_half[:, 0:1], env.minus_half[:, 0:1], ALU.mult)
                for t in range(NT):
                    for k in range(TOPK):
                        n = t * TOPK + k
                        pool.indirect_dma_start(slot_rows, bass.IndirectOffsetOnAxis(slot_now[:, n:n + 1], 0), xn[:, t, :], None,
                                                bounds_check=SLOTS - 1, oob_is_err=False).then_inc(scattered.sem, 16)
                scattered.wait(pool, b, NT * TOPK * 16)
                pool.tensor_tensor(pool_carrier[:, 1:2], env.minus_half[:, 0:1], env.minus_half[:, 0:1], ALU.mult).then_inc(stored.sem, 1)

            pool.wait_ge(zeroed, 16 * (ZERO_DMAS + 1))
            batches(pool, body)
            stored.wait(pool, B, 0)



I_DIM = 256


def experts(nc, env, tag, slot_rows, out_rows, w_gate_up, w_down):
    F = 2 * I_DIM // P
    G = I_DIM // P
    CT = CAP // P
    PAIRS = E_ROUTED // 2
    with semaphores(nc) as take, ExitStack() as ctx:
        def sb(name, shape, dtype=F32):
            return ctx.enter_context(nc.sbuf_tensor(f"{tag}_{name}", shape, dtype))

        def signals(name, per):
            return [Signal(nc, take(f"{tag}_{name}{u}"), per) for u in range(2)]

        raw_gu, raw_d = sb("raw_gu", [P, 2, NC, 2 * I_DIM]), sb("raw_d", [P, 2, G, D])
        gu_hi, gu_lo = sb("gu_hi", [P, 2, NC, 2 * I_DIM], F32R), sb("gu_lo", [P, 2, NC, 2 * I_DIM], F32R)
        d_hi, d_lo = sb("d_hi", [P, 2, G, D], F32R), sb("d_lo", [P, 2, G, D], F32R)
        rows = sb("rows", [P, 2, CT, D])
        x_hi, x_lo = sb("x_hi", [P, 2, NC, CAP], F32R), sb("x_lo", [P, 2, NC, CAP], F32R)
        silu, hid = sb("silu", [P, 2, G * CAP]), sb("hid", [P, 2, G * CAP])
        h_hi, h_lo = sb("h_hi", [P, 2, G, CAP], F32R), sb("h_lo", [P, 2, G, CAP], F32R)
        y = sb("y", [P, 2, CT, D])
        ps = ctx.enter_context(nc.psum_tensor(f"{tag}_ps", [P, 8, 512], F32))

        w_in, rows_in, y_out = signals("w_in", 32), signals("rows_in", 16), signals("y_out", 16)
        gu_hi_done, gu_lo_done = signals("gu_hi_done", 1), signals("gu_lo_done", 1)
        d_hi_done, d_lo_done = signals("d_hi_done", 1), signals("d_lo_done", 1)
        turned, x_hi_done, x_lo_done = signals("turned", 1), signals("x_hi_done", 1), signals("x_lo_done", 1)
        gu_ready, silu_done, hid_done = signals("gu_ready", 1), signals("silu_done", 1), signals("hid_done", 1)
        h_hi_done, h_lo_done = signals("h_hi_done", 1), signals("h_lo_done", 1)
        y_ready, y_act, y_dve = signals("y_ready", CT), signals("y_act", 1), signals("y_dve", 1)

        def pairs(eng, body):
            with eng.Fori(0, PAIRS - 1) as i:
                body(i, 0, True)
                body(i, 1, True)
            body(PAIRS - 1, 0, False)
            body(PAIRS - 1, 1, False)

        gu_dram = w_gate_up.rearrange("e (c p) f -> e p c f", p=P)
        d_dram = w_down.rearrange("e (c p) f -> e p c f", p=P)
        rows_dram = slot_rows.rearrange("(e t p) d -> e p t d", p=P, t=CT)
        y_dram = out_rows.rearrange("(e t p) d -> e p t d", p=P, t=CT)
        block = ctx.enter_context(nc.Block())

        @block.sync
        def _(sp):
            def load(i, u):
                e = i * 2 + u
                gu_lo_done[u].wait(sp, i, 0)
                d_lo_done[u].wait(sp, i, 0)
                sp.dma_start(raw_gu[:, u], gu_dram[bass.ds(e, 1)].rearrange("e p c f -> (e p) c f")).then_inc(w_in[u].sem, 16)
                sp.dma_start(raw_d[:, u], d_dram[bass.ds(e, 1)].rearrange("e p c f -> (e p) c f")).then_inc(w_in[u].sem, 16)
                turned[u].wait(sp, i, 0)
                sp.dma_start(rows[:, u], rows_dram[bass.ds(e, 1)].rearrange("e p t d -> (e p) t d")).then_inc(rows_in[u].sem, 16)

            def body(i, u, more):
                if more:
                    load(i + 1, u)
                y_act[u].wait(sp, i, 1)
                y_dve[u].wait(sp, i, 1)
                sp.dma_start(y_dram[bass.ds(i * 2 + u, 1)].rearrange("e p t d -> (e p) t d"), y[:, u]).then_inc(y_out[u].sem, 16)

            load(0, 0)
            load(0, 1)
            pairs(sp, body)
            for u in range(2):
                y_out[u].wait(sp, PAIRS, 0)

        @block.tensor
        def _(pe):
            def turn(i, u, after):
                rows_in[u].wait(pe, i, 16)
                if after is not None:
                    x_lo_done[after[1]].wait(pe, after[0], 1)
                for c in range(NC):
                    for t in range(CT):
                        at = c * CAP + t * P
                        mm = pe.transpose(ps[:, at // 512, at % 512:at % 512 + P], rows[:, u, t, c * P:(c + 1) * P], env.ident[:])
                mm.then_inc(turned[u].sem, 1)

            def gate_up(i, u):
                gu_hi_done[u].wait(pe, i, 1)
                gu_lo_done[u].wait(pe, i, 1)
                x_lo_done[u].wait(pe, i, 1)
                hid_done[u].wait(pe, i, 0)
                for f in range(F):
                    at = f * CAP
                    for c in range(NC):
                        mm = split_mm(pe, ps[:, 2 + 2 * u + at // 512, at % 512:at % 512 + CAP],
                                      [w[:, u, c, f * P:(f + 1) * P] for w in (gu_hi, gu_lo)], [x[:, u, c, :] for x in (x_hi, x_lo)],
                                      c == 0, c == NC - 1)
                mm.then_inc(gu_ready[u].sem, 1)

            def down(i, u, after):
                h_lo_done[u].wait(pe, i, 1)
                d_hi_done[u].wait(pe, i, 1)
                d_lo_done[u].wait(pe, i, 1)
                if after is not None:
                    y_act[after[1]].wait(pe, *after[0])
                    y_dve[after[1]].wait(pe, *after[0])
                for t in range(CT):
                    for g in range(G):
                        mm = split_mm(pe, ps[:, 6 + t, :], [h[:, u, g, t * P:(t + 1) * P] for h in (h_hi, h_lo)],
                                      [w[:, u, g, :] for w in (d_hi, d_lo)], g == 0, g == G - 1)
                    mm.then_inc(y_ready[u].sem, 1)

            turn(0, 0, None)
            turn(0, 1, (0, 0))
            gate_up(0, 0)
            with pe.Fori(0, PAIRS - 1) as i:
                gate_up(i, 1)
                down(i, 0, ((i, 0), 1))
                turn(i + 1, 0, (i, 1))
                gate_up(i + 1, 0)
                down(i, 1, ((i, 1), 0))
                turn(i + 1, 1, (i + 1, 0))
            gate_up(PAIRS - 1, 1)
            down(PAIRS - 1, 0, ((PAIRS - 1, 0), 1))
            down(PAIRS - 1, 1, ((PAIRS - 1, 1), 0))

        def flat(ap):
            return ap.rearrange("p a b -> p (a b)")

        @block.scalar
        def _(act):
            def split_gu(i, u):
                w_in[u].wait(act, i, 32)
                gu_ready[u].wait(act, i, 0)
                act.copy(flat(gu_hi[:, u]), flat(raw_gu[:, u])).then_inc(gu_hi_done[u].sem, 1)

            def split_rest(i, u):
                y_ready[u].wait(act, i, 0)
                act.copy(flat(d_hi[:, u]), flat(raw_d[:, u])).then_inc(d_hi_done[u].sem, 1)
                turned[u].wait(act, i, 1)
                act.copy(flat(x_hi[:, u]), flat(ps[:, 0:2, :])).then_inc(x_hi_done[u].sem, 1)

            def body(i, u, more):
                gu_ready[u].wait(act, i, 1)
                act.activation(silu[:, u, :], ps[:, 2 + 2 * u, :], ACT.Silu).then_inc(silu_done[u].sem, 1)
                hid_done[u].wait(act, i, 1)
                act.copy(flat(h_hi[:, u]), hid[:, u, :]).then_inc(h_hi_done[u].sem, 1)
                if more:
                    split_gu(i + 1, u)
                y_ready[u].wait(act, i, 1)
                y_out[u].wait(act, i, 0)
                act.copy(y[:, u, 0, :], ps[:, 6, :]).then_inc(y_act[u].sem, 1)
                if more:
                    split_rest(i + 1, u)

            for u in range(2):
                split_gu(0, u)
                split_rest(0, u)
            pairs(act, body)

        @block.vector
        def _(dve):
            def low(dst, src, hi, sig):
                dve.tensor_tensor(dst, src, hi.bitcast(F32), ALU.subtract).then_inc(sig.sem, 1)

            def split_gu(i, u):
                gu_hi_done[u].wait(dve, i, 1)
                low(flat(gu_lo[:, u]), flat(raw_gu[:, u]), flat(gu_hi[:, u]), gu_lo_done[u])

            def split_x(i, u):
                x_hi_done[u].wait(dve, i, 1)
                low(flat(x_lo[:, u]), flat(ps[:, 0:2, :]), flat(x_hi[:, u]), x_lo_done[u])

            def body(i, u, more):
                silu_done[u].wait(dve, i, 1)
                dve.tensor_tensor(hid[:, u, :], silu[:, u, :], ps[:, 3 + 2 * u, :], ALU.mult).then_inc(hid_done[u].sem, 1)
                h_hi_done[u].wait(dve, i, 1)
                low(flat(h_lo[:, u]), hid[:, u, :], flat(h_hi[:, u]), h_lo_done[u])
                if more:
                    split_gu(i + 1, u)
                y_ready[u].wait(dve, i, 2)
                y_out[u].wait(dve, i, 0)
                dve.tensor_copy(y[:, u, 1, :], ps[:, 7, :]).then_inc(y_dve[u].sem, 1)
                if more:
                    split_x(i + 1, u)

            for u in range(2):
                split_gu(0, u)
                split_x(0, u)
            pairs(dve, body)

        @block.gpsimd
        def _(pool):
            def split_d(i, u):
                d_hi_done[u].wait(pool, i, 1)
                pool.tensor_tensor(flat(d_lo[:, u]), flat(raw_d[:, u]), flat(d_hi[:, u]).bitcast(F32), ALU.subtract
                                   ).then_inc(d_lo_done[u].sem, 1)

            def body(i, u, more):
                if more:
                    split_d(i + 1, u)

            split_d(0, 0)
            split_d(0, 1)
            pairs(pool, body)


def combine(nc, env, tag, x_in, x_out, out_rows, slots, weights):
    with semaphores(nc) as take, ExitStack() as ctx:
        def sb(name, shape, dtype=F32):
            return ctx.enter_context(nc.sbuf_tensor(f"{tag}_{name}", shape, dtype))

        def signals(name, per, start=1):
            return [Signal(nc, take(f"{tag}_{name}{u}"), per, start) for u in range(2)]

        got = sb("got", [P, 2, TOPK, D])
        acc = sb("acc", [P, 2, D])
        slot_now, weight_now = sb("slot_now", [P, 2, TOPK], I32), sb("weight_now", [P, 2, TOPK])
        carrier, pool_carrier = sb("carrier", [P, 1]), sb("pool_carrier", [P, 4])
        x_sem, got_sem, out_sem = signals("x_in", 16), signals("got", 16 * TOPK, start=0), signals("out", 16)
        slot_sem, weight_sem, summed = signals("slot", 1), signals("weight", 1), signals("summed", TOPK)
        HALF = B * NT // 2
        block = ctx.enter_context(nc.Block())
        rows_in = x_in.rearrange("(t p) d -> t p d", p=P)
        rows_out = x_out.rearrange("(t p) d -> t p d", p=P)

        @block.sync
        def _(sp):
            with sp.Fori(0, HALF) as i:
                for u in range(2):
                    out_sem[u].wait(sp, i, 0)
                    sp.dma_start(acc[:, u, :], rows_in[bass.ds(i * 2 + u, 1)].rearrange("t p d -> (t p) d")).then_inc(x_sem[u].sem, 16)
                for u in range(2):
                    summed[u].wait(sp, i, TOPK)
                    sp.dma_start(rows_out[bass.ds(i * 2 + u, 1)].rearrange("t p d -> (t p) d"), acc[:, u, :]).then_inc(out_sem[u].sem, 16)
            for u in range(2):
                out_sem[u].wait(sp, HALF, 0)

        @block.gpsimd
        def _(pool):
            with pool.Fori(0, HALF) as i:
                for u in range(2):
                    at = (i * 2 + u) * TOPK
                    summed[u].wait(pool, i, 0)
                    pool.tensor_tensor(pool_carrier[:, 2 * u + 0:2 * u + 1], env.minus_half[:, 0:1], env.minus_half[:, 0:1], ALU.mult)
                    pool.tensor_copy(slot_now[:, u, :], slots[:, bass.ds(at, TOPK)]).then_inc(slot_sem[u].sem, 1)
                    slot_sem[u].wait(pool, i, 1)
                    pool.tensor_tensor(pool_carrier[:, 2 * u + 1:2 * u + 2], env.minus_half[:, 0:1], env.minus_half[:, 0:1], ALU.mult)
                    for k in range(TOPK):
                        pool.indirect_dma_start(got[:, u, k, :], None, out_rows, bass.IndirectOffsetOnAxis(slot_now[:, u, k:k + 1], 0)
                                                ).then_inc(got_sem[u].sem, 16)

        @block.vector
        def _(dve):
            with dve.Fori(0, HALF) as i:
                for u in range(2):
                    at = (i * 2 + u) * TOPK
                    summed[u].wait(dve, i, 0)
                    dve.memset(carrier[:], 0.0)
                    dve.tensor_copy(weight_now[:, u, :], weights[:, bass.ds(at, TOPK)]).then_inc(weight_sem[u].sem, 1)
                    weight_sem[u].wait(dve, i, 1)
                    x_sem[u].wait(dve, i, 16)
                    got_sem[u].wait(dve, i, 16 * TOPK)
                    for k in range(TOPK):
                        if k:
                            summed[u].wait(dve, i, k)
                        dve.scalar_tensor_tensor(out=acc[:, u, :], in0=got[:, u, k, :], scalar=weight_now[:, u, k:k + 1], in1=acc[:, u, :],
                                                 op0=ALU.mult, op1=ALU.add).then_inc(summed[u].sem, 1)



HID = 2048


def network(nc, env, tag, x_in, x_mid, x_out, w1, w3, w2):
    HC2 = HID // P
    HALF = HC2 // 2
    with ExitStack() as ctx:
        def sb(name, shape, dtype=F32, stack=ctx):
            return stack.enter_context(nc.sbuf_tensor(f"{tag}_{name}", shape, dtype))

        w2m = sb("w2m", [P, NT, HID])
        had = sb("had", [P, P], F32R)
        with semaphores(nc) as take, ExitStack() as prep:
            other = sb("w2n", [P, NT, HID], stack=prep)
            had_raw = sb("had_raw", [P, P], stack=prep)
            w2_in, mixed = (take(f"{tag}_{n}") for n in ("w2_in", "mixed"))
            block = prep.enter_context(nc.Block())

            @block.sync
            def _(sp):
                sp.dma_start(w2m[:], tiles(w2)).then_inc(w2_in, 16)
                sp.dma_start(had_raw[:], env.hadamard).then_inc(w2_in, 16)

            @block.vector
            def _(dve):
                dve.wait_ge(w2_in, 32)
                n = 1
                src, dst = w2m, other
                while n < HC2:
                    a, b, c, d = (m[:].rearrange("p t (g h k) -> p (t g) h k", h=2, k=n * P)[:, :, h, :]
                                  for m in (src, dst) for h in range(2))
                    dve.tensor_tensor(c, a, b, ALU.add).then_inc(mixed, 1)
                    dve.tensor_tensor(d, a, b, ALU.subtract).then_inc(mixed, 1)
                    n, src, dst = 2 * n, dst, src
                    dve.wait_ge(mixed, 2 * (n.bit_length() - 1))
                assert src is w2m
                dve.tensor_copy(had[:], had_raw[:]).then_inc(mixed, 1)
                dve.wait_ge(mixed, 2 * (HC2.bit_length() - 1) + 1)

        def pair(name, shape):
            return sb(f"{name}_hi", shape, F32R), sb(f"{name}_lo", shape, F32R)

        w1T, w3T, w2T = pair("w1", [P, NC, HALF * P]), pair("w3", [P, NC, HALF * P]), pair("w2", [P, HALF, D])
        for half in range(2):
            rows = slice(half * HALF * P, (half + 1) * HALF * P)
            load_weights(nc, env, f"{tag}_w{half}", [(w1[rows, :], *w1T), (w3[rows, :], *w3T)])
            with semaphores(nc) as take, ExitStack() as prep:
                t_hi, t_lo = (prep.enter_context(nc.sbuf_tensor(f"{tag}_{n}{half}", [P, 2, D], F32R)) for n in ("t_hi", "t_lo"))
                scaled = prep.enter_context(nc.sbuf_tensor(f"{tag}_scaled{half}", [P, 2, D], F32))
                ps = prep.enter_context(nc.psum_tensor(f"{tag}_pps{half}", [P, 4, 512], F32))
                turned, t_hi_done, t_lo_done, prod, sc_done, w_hi, w_lo = (
                    take(f"{tag}_{n}{half}") for n in ("turned", "thi", "tlo", "prod", "sc", "whi", "wlo"))
                block = prep.enter_context(nc.Block())

                @block.tensor
                def _(pe):
                    def product(k):
                        pe.wait_ge(t_lo_done, k + 1)
                        if k >= 2:
                            pe.wait_ge(sc_done, k - 1)
                        pe.matmul(ps[:, 2 + k % 2, :], had[:], t_hi[:, k % 2, :], start=True, stop=False)
                        pe.matmul(ps[:, 2 + k % 2, :], had[:], t_lo[:, k % 2, :], start=False, stop=True).then_inc(prod, 1)

                    for k in range(HALF):
                        at = (half * HALF + k) * P
                        if k >= 2:
                            pe.wait_ge(t_lo_done, k - 1)
                        for t in range(NT):
                            mm = pe.transpose(ps[:, k % 2, t * P:(t + 1) * P], w2m[:, t, at:at + P], env.ident[:])
                        mm.then_inc(turned, 1)
                        if k >= 1:
                            product(k - 1)
                    product(HALF - 1)

                @block.scalar
                def _(act):
                    def second(k):
                        act.wait_ge(prod, k + 1)
                        if k >= 2:
                            act.wait_ge(w_lo, k - 1)
                        act.mul(scaled[:, k % 2, :], ps[:, 2 + k % 2, :], HID ** -0.5).then_inc(sc_done, 1)
                        act.wait_ge(sc_done, k + 1)
                        act.copy(w2T[0][:, k, :], scaled[:, k % 2, :]).then_inc(w_hi, 1)

                    for k in range(HALF):
                        act.wait_ge(turned, k + 1)
                        if k >= 2:
                            act.wait_ge(prod, k - 1)
                        act.copy(t_hi[:, k % 2, :], ps[:, k % 2, :]).then_inc(t_hi_done, 1)
                        if k >= 1:
                            second(k - 1)
                    second(HALF - 1)

                @block.vector
                def _(dve):
                    def second(k):
                        dve.wait_ge(w_hi, k + 1)
                        dve.tensor_tensor(w2T[1][:, k, :], scaled[:, k % 2, :], w2T[0][:, k, :].bitcast(F32), ALU.subtract).then_inc(w_lo, 1)

                    for k in range(HALF):
                        dve.wait_ge(t_hi_done, k + 1)
                        dve.tensor_tensor(t_lo[:, k % 2, :], ps[:, k % 2, :], t_hi[:, k % 2, :].bitcast(F32), ALU.subtract).then_inc(t_lo_done, 1)
                        if k >= 1:
                            second(k - 1)
                    second(HALF - 1)
            half_network(nc, env, f"{tag}{half}", x_in, (x_in, x_mid)[half], (x_mid, x_out)[half], w1T, w3T, w2T, HALF)


def half_network(nc, env, tag, x_in, x_res, x_out, w1T, w3T, w2T, chunks):
    with semaphores(nc) as take, ExitStack() as ctx:
        def sb(name, shape, dtype=F32):
            return ctx.enter_context(nc.sbuf_tensor(f"{tag}_{name}", shape, dtype))

        def sem(name):
            return take(f"{tag}_{name}")

        def signal(name, per, start=1):
            return Signal(nc, sem(name), per, start)

        def pair(name, shape):
            return sb(f"{name}_hi", shape, F32R), sb(f"{name}_lo", shape, F32R)

        xs, res = sb("xs", [P, NT, D]), sb("res", [P, NT, D])
        xnT = pair("xnT", [P, NC, S])
        stats, mv, rstd, carrier = sb("stats", [P, NT, 6]), sb("mv", [P, NT, 2]), sb("rstd", [P, NT]), sb("carrier", [P, 1])
        gated, hid = sb("gated", [P, 2, S]), sb("hid", [P, 2, S])
        h_hi, h_lo = sb("h_hi", [P, 2, S], F32R), sb("h_lo", [P, 2, S], F32R)
        ps = ctx.enter_context(nc.psum_tensor(f"{tag}_ps", [P, 8, 512], F32))
        xs_in, res_in, out_sem = signal("xs_in", 16), signal("res_in", 16), signal("out", 16)
        stat, rstd_done, xn_done = signal("stat", 3 * NT), signal("rstd_done", 1), signal("xn_done", NT)
        xT_ready, xT_hi, xT_lo = signal("xT_ready", NC), signal("xT_hi", NC), signal("xT_lo", NC)
        gu_ready, silu_done, hid_done = signal("gu_ready", chunks), signal("silu_done", chunks), signal("hid_done", chunks)
        h_hi_done, h_lo_done, used = signal("h_hi_done", chunks), signal("h_lo_done", chunks), signal("used", chunks)
        y_done = signal("y_done", NT)
        block = ctx.enter_context(nc.Block())

        @block.sync
        def _(sp):
            def batch(x, b):
                return x.rearrange("(b t p) d -> b p t d", p=P, t=NT)[bass.ds(b, 1)].rearrange("b p t d -> (b p) t d")

            def body(b, more):
                out_sem.wait(sp, b, 0)
                sp.dma_start(res[:], batch(x_res, b)).then_inc(res_in.sem, 16)
                if more:
                    xT_ready.wait(sp, b, NC)
                    sp.dma_start(xs[:], batch(x_in, b + 1)).then_inc(xs_in.sem, 16)
                y_done.wait(sp, b, NT)
                sp.dma_start(batch(x_out, b), res[:]).then_inc(out_sem.sem, 16)

            sp.dma_start(xs[:], batch(x_in, 0)).then_inc(xs_in.sem, 16)
            batches(sp, body)
            out_sem.wait(sp, B, 0)

        @block.tensor
        def _(pe):
            def gate_up(b, k):
                if k >= 2:
                    hid_done.wait(pe, b, k - 1)
                for n, w in enumerate((w1T, w3T)):
                    for c in range(NC):
                        mm = split_mm(pe, ps[:, 2 * (k % 2) + n, :], [p[:, c, k * P:(k + 1) * P] for p in w],
                                      [p[:, c, :] for p in xnT], c == 0, c == NC - 1)
                mm.then_inc(gu_ready.sem, 1)

            def down(b, k):
                h_lo_done.wait(pe, b, k + 1)
                if k == 0:
                    y_done.wait(pe, b, 0)
                for t in range(NT):
                    mm = split_mm(pe, ps[:, 4 + t, :], [h[:, k % 2, t * P:(t + 1) * P] for h in (h_hi, h_lo)],
                                  [p[:, k, :] for p in w2T], k == 0, k == chunks - 1)
                mm.then_inc(used.sem, 1)

            def body(b, more):
                hid_done.wait(pe, b, 0)
                for c in range(NC):
                    for t in range(NT):
                        if c == 0:
                            xn_done.wait(pe, b, t + 1)
                        mm = pe.transpose(ps[:, c, t * P:(t + 1) * P], xs[:, t, c * P:(c + 1) * P], env.ident[:])
                    mm.then_inc(xT_ready.sem, 1)
                xT_lo.wait(pe, b, NC)
                gate_up(b, 0)
                for k in range(chunks):
                    if k + 1 < chunks:
                        gate_up(b, k + 1)
                    down(b, k)

            batches(pe, body)

        @block.scalar
        def _(act):
            def body(b, more):
                for c in range(NC):
                    xT_ready.wait(act, b, c + 1)
                    act.copy(xnT[0][:, c, :], ps[:, c, :]).then_inc(xT_hi.sem, 1)
                for k in range(chunks):
                    gu_ready.wait(act, b, k + 1)
                    act.activation(gated[:, k % 2, :], ps[:, 2 * (k % 2), :], ACT.Silu).then_inc(silu_done.sem, 1)
                    hid_done.wait(act, b, k + 1)
                    if k >= 2:
                        used.wait(act, b, k - 1)
                    act.copy(h_hi[:, k % 2, :], hid[:, k % 2, :]).then_inc(h_hi_done.sem, 1)

            batches(act, body)

        @block.vector
        def _(dve):
            def layernorm(b):
                xs_in.wait(dve, b, 16)
                for t in range(NT):
                    dve.bn_stats(stats[:, t, :], xs[:, t, :]).then_inc(stat.sem, 1)
                stat.wait(dve, b, NT)
                dve.memset(carrier[:], 0.0)
                for t in range(NT):
                    dve.bn_aggr(mv[:, t, :], stats[:, t, :]).then_inc(stat.sem, 1)
                stat.wait(dve, b, 2 * NT)
                for t in range(NT):
                    dve.tensor_scalar(mv[:, t, 1:2], mv[:, t, 1:2], EPS, None, ALU.add).then_inc(stat.sem, 1)
                rstd_done.wait(dve, b, 1)
                for t in range(NT):
                    dve.tensor_scalar(xs[:, t, :], xs[:, t, :], mv[:, t, 0:1], rstd[:, t:t + 1],
                                      ALU.subtract, ALU.mult).then_inc(xn_done.sem, 1)

            def body(b, more):
                for c in range(NC):
                    xT_hi.wait(dve, b, c + 1)
                    dve.tensor_tensor(xnT[1][:, c, :], ps[:, c, :], xnT[0][:, c, :].bitcast(F32), ALU.subtract).then_inc(xT_lo.sem, 1)
                for k in range(chunks):
                    silu_done.wait(dve, b, k + 1)
                    dve.tensor_tensor(hid[:, k % 2, :], gated[:, k % 2, :], ps[:, 2 * (k % 2) + 1, :], ALU.mult).then_inc(hid_done.sem, 1)
                    h_hi_done.wait(dve, b, k + 1)
                    dve.tensor_tensor(h_lo[:, k % 2, :], hid[:, k % 2, :], h_hi[:, k % 2, :].bitcast(F32), ALU.subtract).then_inc(h_lo_done.sem, 1)
                    if more and k == chunks // 2:
                        layernorm(b + 1)
                used.wait(dve, b, chunks)
                res_in.wait(dve, b, 16)
                for t in range(NT):
                    dve.tensor_tensor(res[:, t, :], ps[:, 4 + t, :], res[:, t, :], ALU.add).then_inc(y_done.sem, 1)

            layernorm(0)
            batches(dve, body)

        @block.gpsimd
        def _(pool):
            def rstds(b):
                stat.wait(pool, b, 3 * NT)
                pool.tensor_tensor(rstd[:], mv[:, :, 1], env.minus_half[:, 0:NT], ALU.pow).then_inc(rstd_done.sem, 1)

            rstds(0)
            with pool.Fori(0, B - 1) as b:
                rstds(b + 1)



def decoder(nc, arg, out):
    env = Env()
    env.cos, env.sin, env.hadamard = arg["cos"], arg["sin"], arg["hadamard"]
    x = arg["x"].rearrange("b s d -> (b s) d")
    context = arg["ctx_512"].rearrange("b s d -> (b s) d")
    steps = [nc.dram_tensor(f"x_after_{n}", [T, D], F32).ap()
             for n in ("attn0", "graph", "experts", "attn1", "cross", "half")]
    slot_rows = nc.dram_tensor("slot_rows", [SLOTS, D], F32).ap()
    out_rows = nc.dram_tensor("out_rows", [SLOTS + 1, D], F32).ap()
    with ExitStack() as ctx:
        alloc_consts(nc, env, ctx)
        constants(nc, env)
        attention(nc, env, "a0", x, steps[0], arg["L0_attn_Wq"], arg["L0_attn_Wk"], arg["L0_attn_Wv"], arg["L0_attn_Wo"],
                  gate=arg["L0_attn_gate"])
        with ExitStack() as moe:
            slots = moe.enter_context(nc.sbuf_tensor("slots", [P, B * NT * TOPK], I32))
            weights = moe.enter_context(nc.sbuf_tensor("weights", [P, B * NT * TOPK], F32))
            graph_and_router(nc, env, "gr", steps[0], steps[1], context, arg["L0_xattn_Wq"], arg["L0_xattn_Wk"],
                             arg["L0_xattn_gamma_raw"], arg["L0_ffn_w_cls"], arg["L0_ffn_bias"], slot_rows,
                             out_rows[SLOTS:SLOTS + 1, :], slots, weights)
            experts(nc, env, "ex", slot_rows, out_rows[0:SLOTS, :], arg["L0_ffn_w_gate_up"], arg["L0_ffn_w_down"])
            combine(nc, env, "co", steps[1], steps[2], out_rows, slots, weights)
        attention(nc, env, "a1", steps[2], steps[3], arg["L1_attn_w_q"], arg["L1_attn_w_k"], arg["L1_attn_w_v"], arg["L1_attn_w_o"])
        wkv = arg["L1_xattn_Wkv_expand"]
        attention(nc, env, "c1", steps[3], steps[4], arg["L1_xattn_Wq"], wkv[0:D, :], wkv[D:2 * D, :], arg["L1_xattn_Wout"],
                  ctx_in=context, causal=True)
        network(nc, env, "ff", steps[4], steps[5], out.rearrange("b s d -> (b s) d"),
                arg["L1_ffn_W1"], arg["L1_ffn_W3"], arg["L1_ffn_W2"])


_INS = ["x", "ctx_512", "L0_attn_Wq", "L0_attn_Wk", "L0_attn_Wv", "L0_attn_Wo", "L0_attn_gate", "L0_xattn_Wq",
        "L0_xattn_Wk", "L0_xattn_gamma_raw", "L0_ffn_w_cls", "L0_ffn_bias", "L0_ffn_w_gate_up", "L0_ffn_w_down",
        "L1_attn_w_q", "L1_attn_w_k", "L1_attn_w_v", "L1_attn_w_o", "L1_xattn_Wq", "L1_xattn_Wkv_expand",
        "L1_xattn_Wout", "L1_ffn_W1", "L1_ffn_W2", "L1_ffn_W3"]


def _tables(np):
    inv_freq = (np.float32(1) / np.float32(10000) ** (np.arange(0, D, 2, dtype=np.float32) / np.float32(D))).astype(np.float32)
    angle = (np.arange(S, dtype=np.float32)[None, :] * inv_freq[:, None]).astype(np.float32)
    bits = np.array([[bin(i & j).count("1") % 2 for j in range(P)] for i in range(P)])
    return {"cos": np.cos(angle), "sin": np.sin(angle), "hadamard": (1 - 2 * bits).astype(np.float32)}


def kernel(**inputs):
    import numpy as _np
    import concourse.bacc as _bacc
    from concourse import mybir as _mybir
    from concourse.bass_utils import run_bass_kernel_spmd as _run

    nc = _bacc.Bacc("TRN2", target_bir_lowering=False, num_devices=1)
    arrays, arg = {}, {}
    given = {name: _np.ascontiguousarray(inputs[name]) for name in _INS}
    given["L0_xattn_gamma_raw"] = given["L0_xattn_gamma_raw"].reshape(1)
    given.update(_tables(_np))
    for name, a in given.items():
        arrays[f"in_{name}_dram"] = a
        arg[name] = nc.dram_tensor(f"in_{name}_dram", a.shape, _mybir.dt.from_np(a.dtype), kind="ExternalInput").ap()
    out = nc.dram_tensor("out_0_dram", (B, S, D), F32, kind="ExternalOutput").ap()
    decoder(nc, arg, out)
    r = _run(nc, [arrays], core_ids=[0])
    return r.results[0]["out_0_dram"]
```

```python
from contextlib import ExitStack, contextmanager

import concourse.bass as bass
from concourse import mybir

ALU = mybir.AluOpType
ACT = mybir.ActivationFunctionType
AX = mybir.AxisListType
F32 = mybir.dt.float32
F32R = mybir.dt.float32r
BF16 = mybir.dt.bfloat16
I32 = mybir.dt.int32
U32 = mybir.dt.uint32

P = 128
B, S, D = 4, 512, 512
T = B * S
NT = S // P
NC = D // P
H, HD = 16, 32
HID = 2048
HC = P // HD
L = 128
EPS = 1e-5
SCALE = HD ** -0.5
VW = 66
NEG = -1e30


class Env:
    pass


@contextmanager
def semaphores(nc):
    taken = []

    def take(name):
        taken.append(nc.alloc_semaphore(name=name))
        return taken[-1]

    yield take
    nc.clear_and_free_semaphores(taken)
    nc.all_engine_barrier()


def split_mm(pe, out, lhs, rhs, start, stop):
    (lh, ll), (rh, rl) = lhs, rhs
    pe.matmul(out, lh, rh, start=start, stop=False, skip_group_check=True)
    pe.matmul(out, lh, rl, start=False, stop=False, skip_group_check=True)
    return pe.matmul(out, ll, rh, start=False, stop=stop, skip_group_check=True)


def tiles(ap):
    return ap.rearrange("(t p) d -> p t d", p=P)



def constants(nc, env):
    with semaphores(nc) as take, ExitStack() as ctx:
        done = take("const_done")
        copied = take("const_copied")
        scratch = ctx.enter_context(nc.sbuf_tensor("const_scratch", [P, HC * 7 * HD], F32))
        block = ctx.enter_context(nc.Block())
        ident = env.ident
        sel = scratch[:].rearrange("p (j m) -> p j m", j=HC)

        @block.gpsimd
        def _(pool):
            pool.memset(ident[:], 0.0).then_inc(done, 1)
            pool.memset(scratch[:], 0.0).then_inc(done, 1)
            pool.memset(env.minus_half[:], -0.5).then_inc(done, 1)
            pool.memset(env.blockmask[:], 1.0).then_inc(done, 1)
            pool.wait_ge(done, 4)
            mask = env.blockmask[:].rearrange("p (h w) -> p h w", w=HD + 1)
            pool.affine_select(out=mask, in_=mask, compare_op=ALU.is_ge, fill=0.0, base=0,
                               pattern=[[-HD, HC], [0, HD + 1]], channel_multiplier=1).then_inc(done, 1)
            pool.wait_ge(done, 5)
            pool.affine_select(out=mask, in_=mask, compare_op=ALU.is_ge, fill=0.0, base=HD - 1,
                               pattern=[[HD, HC], [0, HD + 1]], channel_multiplier=-1).then_inc(done, 1)
            pool.affine_select(out=ident[:], in_=ident[:], compare_op=ALU.not_equal, fill=1.0, base=0,
                               pattern=[[-1, P]], channel_multiplier=1).then_inc(done, 1)
            for at, n in ((2, 2), (6, 1)):
                part = sel[:, :, at * HD:(at + n) * HD].rearrange("p j (k m) -> p j k m", m=HD)
                pool.affine_select(out=part, in_=part, compare_op=ALU.not_equal, fill=1.0, base=0,
                                   pattern=[[-HD, HC], [0, n], [-1, HD]], channel_multiplier=1).then_inc(done, 1)

        @block.vector
        def _(dve):
            dve.wait_ge(done, 9)
            dve.tensor_copy(env.ident_r[:], ident[:]).then_inc(copied, 1)
            dve.tensor_copy(env.sel[:], sel).then_inc(copied, 1)
            dve.tensor_scalar(env.one_r[:], ident[:, 0:1], 0.0, 1.0, ALU.mult, ALU.add).then_inc(copied, 1)
            dve.wait_ge(copied, 3)


def causal_masks(nc, qk, kq):
    with semaphores(nc) as take, ExitStack() as ctx:
        made, copied = take("causal_made"), take("causal_copied")
        raw = ctx.enter_context(nc.sbuf_tensor("causal_raw", [P, 2, P], F32))
        block = ctx.enter_context(nc.Block())

        @block.gpsimd
        def _(pool):
            pool.memset(raw[:], 0.0).then_inc(made, 1)
            pool.wait_ge(made, 1)
            pool.affine_select(out=raw[:, 0, :], in_=raw[:, 0, :], compare_op=ALU.is_ge, fill=NEG, base=0,
                               pattern=[[-1, P]], channel_multiplier=1).then_inc(made, 1)
            pool.affine_select(out=raw[:, 1, :], in_=raw[:, 1, :], compare_op=ALU.is_ge, fill=NEG, base=0,
                               pattern=[[1, P]], channel_multiplier=-1).then_inc(made, 1)

        @block.vector
        def _(dve):
            dve.wait_ge(made, 3)
            dve.tensor_copy(qk[:], raw[:, 0, :]).then_inc(copied, 1)
            dve.tensor_copy(kq[:], raw[:, 1, :]).then_inc(copied, 1)
            dve.wait_ge(copied, 2)



def load_weights(nc, env, tag, jobs, also=None):
    stages = [(n, r) for n, (w, _, _) in enumerate(jobs) for r in range(w.shape[0] // 512)]
    with semaphores(nc) as take, ExitStack() as ctx:
        sem = lambda n: take(f"{tag}_{n}")
        raw = ctx.enter_context(nc.sbuf_tensor(f"{tag}_raw", [P, 2, NT, 512], F32))
        ps = ctx.enter_context(nc.psum_tensor(f"{tag}_ps", [P, 8, 512], F32))
        loaded = [sem(f"loaded{i}") for i in range(2)]
        turned, high_done, low_done = sem("turned"), sem("high_done"), sem("low_done")
        block = ctx.enter_context(nc.Block())
        banks = []
        for s, (n, _) in enumerate(stages):
            banks += [(s, c) for c in range(jobs[n][0].shape[1] // P)]

        @block.sync
        def _(sp):
            for s, (n, r) in enumerate(stages):
                w = jobs[n][0]
                if s >= 2:
                    sp.wait_ge(turned, sum(1 for q, _ in banks if q <= s - 2))
                sp.dma_start(raw[:, s % 2, :, 0:w.shape[1]],
                             tiles(w[r * 512:(r + 1) * 512, :])).then_inc(loaded[s % 2], 16)
                if also is not None and s == 1:
                    also(sp)

        @block.tensor
        def _(pe):
            for u, (s, c) in enumerate(banks):
                pe.wait_ge(loaded[s % 2], 16 * (s // 2 + 1))
                if u >= 8:
                    pe.wait_ge(low_done, u - 7)
                for t in range(NT):
                    mm = pe.transpose(ps[:, u % 8, t * P:(t + 1) * P],
                                      raw[:, s % 2, t, c * P:(c + 1) * P], env.ident[:])
                mm.then_inc(turned, 1)

        @block.scalar
        def _(act):
            for u, (s, c) in enumerate(banks):
                n, r = stages[s]
                act.wait_ge(turned, u + 1)
                act.copy(jobs[n][1][:, c, r * 512:(r + 1) * 512], ps[:, u % 8, :]).then_inc(high_done, 1)

        @block.vector
        def _(dve):
            for u, (s, c) in enumerate(banks):
                n, r = stages[s]
                cols = slice(r * 512, (r + 1) * 512)
                dve.wait_ge(high_done, u + 1)
                dve.tensor_tensor(jobs[n][2][:, c, cols], ps[:, u % 8, :],
                                  jobs[n][1][:, c, cols].bitcast(F32), ALU.subtract).then_inc(low_done, 1)



class Signal:

    def __init__(self, nc, sem, per, start=None):
        self.sem, self.per, self.start = sem, per, per if start is None else start
        if self.start:
            nc.sync.sem_inc(sem, self.start)

    def wait(self, eng, b, n):
        assert self.start + n > 0
        eng.wait_ge(self.sem, b * self.per + n + self.start)


def batches(eng, body):
    with eng.Fori(0, B - 1) as b:
        body(b, True)
    body(B - 1, False)


def attention(nc, env, tag, x_in, x_out, wq, wk, wv, wo, gate=None, ctx_in=None, causal=False):
    linear = gate is not None
    PH_ACT, PH_DVE = ((0, 1, 2, 3), ()) if linear else ((0, 1), (2, 3))
    KC = NC if ctx_in is None else 1
    with semaphores(nc) as take, ExitStack() as ctx:
        def sb(name, shape, dtype=F32):
            return ctx.enter_context(nc.sbuf_tensor(f"{tag}_{name}", shape, dtype))

        def sem(name):
            return take(f"{tag}_{name}")

        def signal(name, per, start=None):
            return Signal(nc, sem(name), per, start)

        def pair(name, shape):
            return sb(f"{name}_hi", shape, F32R), sb(f"{name}_lo", shape, F32R)

        wqT, wkT, wvT, woT = pair("wq", [P, NC, D]), pair("wk", [P, KC, D]), pair("wv", [P, KC, D]), pair("wo", [P, NC, D])
        xs = sb("xs", [P, NT, D])
        xs_in, ctx_loaded = signal("xs_in", 16), signal("ctx_loaded", 16)
        if ctx_in is not None:
            ctx_sb = sb("ctx_sb", [P, NT, L])

        def load(sp, b):
            sp.dma_start(xs[:], x_in.rearrange("(b t p) d -> b p t d", p=P, t=NT)[bass.ds(b, 1)]
                         .rearrange("b p t d -> (b p) t d")).then_inc(xs_in.sem, 16)
            if ctx_in is not None:
                sp.dma_start(ctx_sb[:], ctx_in.rearrange("(b t p) d -> b p t d", p=P, t=NT)[bass.ds(b, 1)]
                             .rearrange("b p t d -> (b p) t d")).then_inc(ctx_loaded.sem, 16)

        load_weights(nc, env, f"{tag}_w", [(wq, *wqT), (wk, *wkT), (wv, *wvT), (wo, *woT)], also=lambda sp: load(sp, 0))

        if causal:
            causal_qk, causal_kq = sb("causal_qk", [P, P], F32R), sb("causal_kq", [P, P], F32R)
            causal_masks(nc, causal_qk, causal_kq)
        NST = 3
        res = sb("res", [P, 2, D])
        xnT = pair("xnT", [P, NC, S])
        qT, kT = pair("qT", [P, NC, S]), pair("kT", [P, NC, S])
        v_split = sb("v_split", [P, NT, H, VW], F32R)
        qs, ks = sb("qs", [P, NST, S], F32R), sb("ks", [P, NST, S], F32R)
        probs = sb("probs", [P, NT, S])
        probs_hi, probs_lo = sb("probs_hi", [P, NT, S], F32R), sb("probs_lo", [P, NT, S], F32R)
        heads_out = sb("heads_out", [P, NT, D])
        u_sb = sb("u_sb", [P, 2, S])
        stats, mv = sb("stats", [P, NT, 6]), sb("mv", [P, NT, 2])
        rstd = sb("rstd", [P, NT])
        carrier = sb("carrier", [P, 1])
        negmax = sb("negmax", [P, 2, NT])
        dneg = sb("dneg", [P, 2, S], F32R)
        rsum = sb("rsum", [P, NT])
        piece_a, piece_b = sb("piece_a", [P, NT, HD]), sb("piece_b", [P, NT, HD])
        if ctx_in is not None:
            cT = pair("cT", [P, 1, S])
        if linear:
            HW = HC * (HD + 1)
            cosT, sinT = sb("cosT", [P, NC // 2, S]), sb("sinT", [P, NC // 2, S])
            gate_e, g_not, g_sig = sb("gate_e", [P, H]), sb("g_not", [P, H]), sb("g_sig", [P, H])
            spare = xs[:].rearrange("p t d -> p (t d)")
            v_one = spare[:, 0:2 * NT * HW].rearrange("p (u t h w) -> p u t h w", u=2, t=NT, h=HC)
            mem = spare[:, 2 * NT * HW:(2 * NT + 1) * HW].rearrange("p (h w) -> p h w", h=HC)
            den = spare[:, (2 * NT + 1) * HW:(2 * NT + 1) * HW + 2 * HC].rearrange("p (t h) -> p t h", t=2)

        def feature(c, w):
            return u_sb[:, w, :] if c % 2 else probs[:, 2 * w + 1, :]
        ps = ctx.enter_context(nc.psum_tensor(f"{tag}_ps", [P, 8, 512], F32))

        def kf(c):
            return heads_out[:, :, c * P:(c + 1) * P]

        NXT = NC + (ctx_in is not None)
        ONES = 2 if linear else 1
        NS = 6 if linear else 4
        res_in = [signal(f"res_in{i}", 32) for i in range(2)]
        res_out = [signal(f"res_out{i}", 32) for i in range(2)]
        stat, rstd_done, xn_done = signal("stat", 3 * NT), signal("rstd_done", 1), signal("xn_done", NT)
        xT_ready, xT_hi, xT_lo = signal("xT_ready", NXT), signal("xT_hi", NXT), signal("xT_lo", NXT)
        q_ready, q_hi, q_lo = signal("q_ready", 2 * NC), signal("q_hi", 2 * NC), signal("q_lo", 2 * NC)
        rot_mul, rot_done = signal("rot_mul", 4 * NC), signal("rot_done", 2 * NC)
        v_ready, v_hi, v_lo = signal("v_ready", NT), signal("v_hi", NT), signal("v_lo", NT)
        stack_ready, stack_done = signal("stack_ready", 2 * H), signal("stack_done", 2 * H)
        qk_ready, max_done = signal("qk_ready", H * NT), signal("max_done", H * NT)
        dneg_done = signal("dneg_done", H)
        kq_ready, exp_done = signal("kq_ready", H * NT), signal("exp_done", H * NT)
        ph_act, ph_dve = signal("ph_act", H * len(PH_ACT)), signal("ph_dve", H * (NT - len(PH_ACT)))
        pl_dve, pl_pool = signal("pl_dve", H * len(PL_DVE)), signal("pl_pool", H * (NT - len(PL_DVE)))
        pv_step, u_done, uT_ready = signal("pv_step", H * NT), signal("u_done", H), signal("uT_ready", H)
        norm = signal("norm", H * NS)
        oT_ready, oT_hi, oT_lo = signal("oT_ready", NC), signal("oT_hi", NC), signal("oT_lo", NC)
        y_ready, y_done = signal("y_ready", NT), signal("y_done", NT)
        sum_done, clip_done, fexp_done, feat_done = (signal(n, 2 * NC) for n in ("sum_done", "clip_done", "fexp_done", "feat_done"))
        kf_ready, kf_done, v_one_done = signal("kf_ready", NC), signal("kf_done", NC), signal("v_one_done", NC)
        one_col = signal("one_col", 1)
        mem_ready, mem_done = signal("mem_ready", NC), signal("mem_done", NC)
        mo_ready, mo_step = signal("mo_ready", 2 * NC), signal("mo_step", 6 * NC)
        const_in, ones_done, gates = sem("const_in"), sem("ones_done"), sem("gates")

        reader, bank_of, before = {}, {}, {}
        last = [None] * 8

        def plan(key, bank, sig, n):
            reader[key], bank_of[key], before[key] = (sig, n), bank, last[bank]
            last[bank] = key

        pairs = [(w, c) for w in "qk" for c in ((0, 2, 1, 3) if linear else range(NC))]
        stage = [(k, rot_done, n // 2 * 2 + 2) if linear else (k, q_lo, n + 1) for n, k in enumerate(pairs)]
        values = [(("v", t), v_lo, t + 1) for t in range(NT)]
        STACKS_AT, SCORES_AT = (2, 3) if linear else (0, 1)
        stage += values[0:SCORES_AT + 1] + [(("qk", 0, t), max_done, t + 1) for t in range(NT)] + values[SCORES_AT + 1:]
        for c in range(NC + 1 if linear else 0):
            if c < NC:
                stage += [(("kf", c), kf_done, c + 1)]
            if c >= 1:
                stage += [(("mem", c - 1), mem_done, c), (("mo", c - 1, 0), mo_step, 6 * c - 3), (("mo", c - 1, 1), mo_step, 6 * c)]
        RING = 4
        for i in range(H):
            for kind, t in SCORES:
                if kind == "kq":
                    stage.append((("kq", i, t), exp_done, i * NT + t + 1))
                elif i + 1 < H:
                    stage.append((("qk", i + 1, t), max_done, (i + 1) * NT + t + 1))
        stage += [(("xT", c), xT_lo, c + 1) for c in range(NC)]
        stage += [(("cT", 0), xT_lo, NXT)] if ctx_in is not None else []
        for n, (key, sig, k) in enumerate(stage):
            plan(key, n % RING, sig, k)
        for h in range(H):
            plan(("pv", h), 4 + h % 2, u_done, h + 1)
        for i in range(-2, H + 2):
            if i + 2 < H:
                plan(("qs", i + 2), 6, stack_done, 2 * (i + 2) + 1)
                plan(("ks", i + 2), 7, stack_done, 2 * (i + 2) + 2)
            if i >= 2:
                plan(("uT", i - 2), 6 + i % 2, norm, (i - 1) * NS)
        for c in range(NC):
            plan(("oT", c), c, oT_lo, c + 1)
        for t in range(NT):
            plan(("y", t), t, y_done, t + 1)

        def bank(key, lo=0, hi=512, rows=P):
            return ps[0:rows, bank_of[key], lo:hi]

        def low_done(eng, b, h, t):
            sig, ts = (pl_dve, PL_DVE) if t in PL_DVE else (pl_pool, PL_POOL)
            sig.wait(eng, b, h * len(ts) + ts.index(t) + 1)

        def high_done(eng, b, h, t):
            sig, ts = (ph_act, PH_ACT) if t in PH_ACT else (ph_dve, PH_DVE)
            sig.wait(eng, b, h * len(ts) + ts.index(t) + 1)

        def keys_from(t):
            return t * P if causal else 0

        def rotated(n):
            return (probs, heads_out)[n // 2 % 2][:, 2 * (n % 2), :]

        def select(j, kind):
            at = {"q_lo": 0, "k_lo": 1, "q_hi": 2, "k_hi": 3}[kind] * HD
            return env.sel[:, j, at:at + P]

        block = ctx.enter_context(nc.Block())

        @block.sync
        def _(sp):
            if linear:
                sp.dma_start(cosT[:], env.cos.rearrange("(c p) s -> p c s", p=P)).then_inc(const_in, 16)
                sp.dma_start(sinT[:], env.sin.rearrange("(c p) s -> p c s", p=P)).then_inc(const_in, 16)
                sp.dma_start(gate_e[:], gate.rearrange("a h b c -> (a b c h)").partition_broadcast(P)).then_inc(const_in, 16)
            tile_in = x_in.rearrange("(b t p) d -> t b p d", p=P, t=NT)
            tile_out = x_out.rearrange("(b t p) d -> t b p d", p=P, t=NT)

            def store(b, t):
                y_done.wait(sp, b, t + 1)
                sp.dma_start(tile_out[t, bass.ds(b, 1)].rearrange("b p d -> (b p) d"), res[:, t % 2, :]).then_inc(res_out[t % 2].sem, 16)

            def body(b, more):
                if more:
                    xT_ready.wait(sp, b, NXT)
                    if linear:
                        mo_step.wait(sp, b, 6 * NC)
                    load(sp, b + 1)
                for t in range(NT):
                    res_out[t % 2].wait(sp, b, t // 2 * 16)
                    sp.dma_start(res[:, t % 2, :], tile_in[t, bass.ds(b, 1)].rearrange("b p d -> (b p) d")).then_inc(res_in[t % 2].sem, 16)
                    if t >= 1:
                        store(b, t - 1)
                store(b, NT - 1)

            batches(sp, body)
            for i in range(2):
                res_out[i].wait(sp, B, 0)

        @block.tensor
        def _(pe):
            def take(b, key, more=True):
                ahead = lambda k: int(k[0] in ("xT", "cT"))
                prev = before[key]
                while not more and prev is not None and ahead(prev):
                    prev = before[prev]
                apart = -ahead(key)
                if prev is None:
                    prev, apart = last[bank_of[key]], apart - 1
                sig, n = reader[prev]
                sig.wait(pe, b, n + (apart + ahead(prev)) * sig.per)

            def stack(b, h):
                c, j = h // HC, h % HC
                for which, (hi, lo) in (("qs", qT), ("ks", kT)):
                    take(b, (which, h))
                    pe.matmul(bank((which, h)), select(j, which[0] + "_hi"), hi[:, c, :], start=True, stop=False)
                    pe.matmul(bank((which, h)), select(j, which[0] + "_lo"), lo[:, c, :], start=False, stop=True).then_inc(stack_ready.sem, 1)

            def scores_qk(b, h, t):
                if t == 0:
                    stack_done.wait(pe, b, 2 * h + 2)
                take(b, ("qk", h, t))
                n = (t + 1) * P if causal else S
                mm = pe.matmul(bank(("qk", h, t), 0, n), qs[:, h % NST, t * P:(t + 1) * P], ks[:, h % NST, 0:n],
                               start=True, stop=not causal, skip_group_check=True)
                if causal:
                    mm = pe.matmul(bank(("qk", h, t), n - P, n), env.ident_r[:], causal_qk[:],
                                   start=False, stop=True, skip_group_check=True)
                mm.then_inc(qk_ready.sem, 1)

            def scores_kq(b, h, t):
                take(b, ("kq", h, t))
                if t == 0:
                    dneg_done.wait(pe, b, h + 1)
                lo = keys_from(t)
                pe.matmul(bank(("kq", h, t), lo, S), ks[:, h % NST, t * P:(t + 1) * P], qs[:, h % NST, lo:S],
                          start=True, stop=False, skip_group_check=True)
                if causal:
                    pe.matmul(bank(("kq", h, t), lo, lo + P), env.ident_r[:], causal_kq[:],
                              start=False, stop=False, skip_group_check=True)
                mm = pe.matmul(bank(("kq", h, t), lo, S), env.one_r[:].to_broadcast([P, P]), dneg[:, h % 2, lo:S], start=False, stop=True, skip_group_check=True)
                mm.then_inc(kq_ready.sem, 1)

            def weigh(b, h, t):
                if t == 0:
                    take(b, ("pv", h))
                low_done(pe, b, h, t)
                lo = keys_from(t)
                for part in (probs_hi, probs_lo):
                    mm = pe.matmul(bank(("pv", h), lo, S, VW - 1), v_split[:, t, h, 0:VW - 1], part[:, t, lo:S],
                                   start=t == 0 and part is probs_hi, stop=t == NT - 1 and part is probs_lo, skip_group_check=True)
                mm.then_inc(pv_step.sem, 1)

            def turn_sums(b, h):
                u_done.wait(pe, b, h + 1)
                take(b, ("uT", h))
                for t in range(NT):
                    mm = pe.transpose(bank(("uT", h), t * VW, t * VW + VW - 1), u_sb[0:VW - 1, h % 2, t * P:(t + 1) * P],
                                      env.ident[0:VW - 1, 0:VW - 1])
                mm.then_inc(uT_ready.sem, 1)

            def turn_features(b, c):
                feat_done.wait(pe, b, 2 * c + 1)
                take(b, ("kf", c))
                for t in range(NT):
                    mm = pe.transpose(bank(("kf", c), t * P, (t + 1) * P), feature(c, 0)[:, t * P:(t + 1) * P], env.ident[:])
                mm.then_inc(kf_ready.sem, 1)

            def linear_chunk(b, c):
                kf_done.wait(pe, b, c + 1)
                if c == 0:
                    one_col.wait(pe, b, 1)
                v_one_done.wait(pe, b, c + 1)
                take(b, ("mem", c))
                for t in range(NT):
                    mm = pe.matmul(bank(("mem", c), 0, HW), kf(c)[:, t, :], v_one[:, c % 2, t].rearrange("p h w -> p (h w)"),
                                   start=t == 0, stop=t == NT - 1)
                mm.then_inc(mem_ready.sem, 1)
                mem_done.wait(pe, b, c + 1)
                feat_done.wait(pe, b, 2 * c + 2)
                for half in range(2):
                    take(b, ("mo", c, half))
                    for t in range(2):
                        at = (2 * half + t) * P
                        mm = pe.matmul(bank(("mo", c, half), t * HW, (t + 1) * HW), feature(c, 1)[:, at:at + P],
                                       mem.rearrange("p h w -> p (h w)"), start=t == 0, stop=t == 1, skip_group_check=True)
                    mm.then_inc(mo_ready.sem, 1)

            def turn_x(b, c):
                take(b, ("xT", c))
                for t in range(NT):
                    if c == 0:
                        xn_done.wait(pe, b, t + 1)
                    mm = pe.transpose(bank(("xT", c), t * P, (t + 1) * P), xs[:, t, c * P:(c + 1) * P], env.ident[:])
                mm.then_inc(xT_ready.sem, 1)

            def turn_context(b):
                take(b, ("cT", 0))
                ctx_loaded.wait(pe, b, 16)
                for t in range(NT):
                    mm = pe.transpose(bank(("cT", 0), t * P, (t + 1) * P), ctx_sb[:, t, :], env.ident[:])
                mm.then_inc(xT_ready.sem, 1)

            def turn_heads(b, c, more):
                norm.wait(pe, b, HC * (c + 1) * NS)
                take(b, ("oT", c), more)
                for t in range(NT):
                    mm = pe.transpose(bank(("oT", c), t * P, (t + 1) * P), heads_out[:, t, c * P:(c + 1) * P], env.ident[:])
                mm.then_inc(oT_ready.sem, 1)

            def body(b, more):
                xT_lo.wait(pe, b, NC)
                for which, c in pairs:
                    from_ctx = which == "k" and ctx_in is not None
                    if from_ctx:
                        xT_lo.wait(pe, b, NXT)
                    w, src = (wqT if which == "q" else wkT), (cT if from_ctx else xnT)
                    take(b, (which, c))
                    for dc in range(KC if which == "k" else NC):
                        mm = split_mm(pe, bank((which, c)), [p[:, dc, c * P:(c + 1) * P] for p in w], [p[:, dc, :] for p in src],
                                      dc == 0, dc == (KC if which == "k" else NC) - 1)
                    mm.then_inc(q_ready.sem, 1)
                for t in range(NT):
                    take(b, ("v", t))
                    for dc in range(KC):
                        mm = split_mm(pe, bank(("v", t)), [p[:, dc, t * P:(t + 1) * P] for p in (xnT if ctx_in is None else cT)],
                                      [p[:, dc, :] for p in wvT], dc == 0, dc == KC - 1)
                    mm.then_inc(v_ready.sem, 1)
                    if t == STACKS_AT:
                        q_lo.wait(pe, b, 2 * NC)
                        stack(b, 0)
                        stack(b, 1)
                    for q in range(NT if t == SCORES_AT else 0):
                        scores_qk(b, 0, q)
                for c in range(NC + 1 if linear else 0):
                    if c < NC:
                        turn_features(b, c)
                    if c >= 1:
                        linear_chunk(b, c - 1)

                for i in range(H + 2):
                    if i == 1:
                        v_lo.wait(pe, b, NT)
                    for kind, t in SCORES:
                        if kind == "kq" and t >= 1 and 1 <= i <= H:
                            weigh(b, i - 1, t - 1)
                        if kind == "kq" and i < H:
                            scores_kq(b, i, t)
                        if kind == "kq" and i == H and more:
                            turn_x(b + 1, t)
                        if kind == "qk" and i + 1 < H:
                            scores_qk(b, i + 1, t)
                        if (kind, t) == ("kq", 2) and i + 2 < H:
                            stack(b, i + 2)
                    if i == H and more and ctx_in is not None:
                        turn_context(b + 1)
                    if i == H + 1:
                        turn_heads(b, 0, more)
                    if i >= 2:
                        turn_sums(b, i - 2)
                    if 1 <= i <= H:
                        weigh(b, i - 1, NT - 1)
                for c in range(1, NC):
                    turn_heads(b, c, more)

                for t in range(NT):
                    take(b, ("y", t))
                    for dc in range(NC):
                        if t == 0:
                            oT_lo.wait(pe, b, dc + 1)
                        mm = split_mm(pe, bank(("y", t)), [p[:, dc, t * P:(t + 1) * P] for p in (probs_hi, probs_lo)],
                                      [p[:, dc, :] for p in woT], dc == 0, dc == NC - 1)
                    mm.then_inc(y_ready.sem, 1)

            pe.wait_ge(ones_done, ONES)
            for c in range(NC):
                turn_x(0, c)
            if ctx_in is not None:
                turn_context(0)
                xT_lo.wait(pe, 0, NXT)
            batches(pe, body)

        @block.scalar
        def _(act):
            def stack_out(b, h):
                for n, (dst, which) in enumerate(((qs, "qs"), (ks, "ks"))):
                    stack_ready.wait(act, b, 2 * h + n + 1)
                    act.copy(dst[:, h % NST, :], bank((which, h))).then_inc(stack_done.sem, 1)

            def split_turned(b, c):
                xT_ready.wait(act, b, c + 1)
                dst, key = (xnT[0][:, c, :], ("xT", c)) if c < NC else (cT[0][:, 0, :], ("cT", 0))
                act.copy(dst, bank(key)).then_inc(xT_hi.sem, 1)

            def body(b, more):
                for n, (which, c) in enumerate(pairs):
                    dst = (qT if which == "q" else kT)[0][:, c, :]
                    if linear:
                        rot_done.wait(act, b, n + 1)
                        act.copy(dst, rotated(n)).then_inc(q_hi.sem, 1)
                    else:
                        q_ready.wait(act, b, n + 1)
                        act.copy(dst, bank((which, c))).then_inc(q_hi.sem, 1)
                for t in range(NT):
                    v_ready.wait(act, b, t + 1)
                    act.copy(v_split[:, t, :, 0:HD], bank(("v", t)).rearrange("p (h w) -> p h w", w=HD)).then_inc(v_hi.sem, 1)
                    if t == STACKS_AT:
                        stack_out(b, 0)
                        stack_out(b, 1)
                for c in range(NC if linear else 0):
                    for w in range(2):
                        clip_done.wait(act, b, 2 * c + w + 1)
                        act.activation(feature(c, w), feature(c, w), ACT.Exp).then_inc(fexp_done.sem, 1)
                    kf_ready.wait(act, b, c + 1)
                    act.copy(kf(c), bank(("kf", c)).rearrange("p (t d) -> p t d", d=P)).then_inc(kf_done.sem, 1)
                for i in range(H + 2):
                    for t in range(NT):
                        lo = keys_from(t)
                        if i == H and more:
                            split_turned(b + 1, t)
                        if i < H:
                            kq_ready.wait(act, b, i * NT + t + 1)
                            if i >= 1:
                                low_done(act, b, i - 1, t)
                            act.activation(probs[:, t, lo:S], bank(("kq", i, t), lo, S), ACT.Exp, scale=SCALE).then_inc(exp_done.sem, 1)
                        if t == 0 and i >= 2:
                            h = i - 2
                            pv_step.wait(act, b, (h + 1) * NT)
                            if h >= 2:
                                uT_ready.wait(act, b, h - 1)
                            act.copy(u_sb[0:VW - 1, h % 2, :], bank(("pv", h), 0, S, VW - 1)).then_inc(u_done.sem, 1)
                        if t == 2 and i + 2 < H:
                            stack_out(b, i + 2)
                        if t in PH_ACT and i < H:
                            exp_done.wait(act, b, i * NT + t + 1)
                            if i >= 1:
                                pv_step.wait(act, b, (i - 1) * NT + t + 1)
                            act.copy(probs_hi[:, t, lo:S], probs[:, t, lo:S]).then_inc(ph_act.sem, 1)
                    if i == H and more and ctx_in is not None:
                        split_turned(b + 1, NC)
                for c in range(NC):
                    oT_ready.wait(act, b, c + 1)
                    act.copy(probs_hi[:, c, :], bank(("oT", c))).then_inc(oT_hi.sem, 1)

            if linear:
                act.wait_ge(const_in, 48)
                act.activation(gate_e[:], gate_e[:], ACT.Exp, scale=-1.0).then_inc(gates, 1)
            for c in range(NXT):
                split_turned(0, c)
            batches(act, body)

        @block.vector
        def _(dve):
            def statistics(b, t):
                if t == 0:
                    xs_in.wait(dve, b, 16)
                dve.bn_stats(stats[:, t, :], xs[:, t, :]).then_inc(stat.sem, 1)

            def variances(b):
                stat.wait(dve, b, NT)
                dve.memset(carrier[:], 0.0)
                for t in range(NT):
                    dve.bn_aggr(mv[:, t, :], stats[:, t, :]).then_inc(stat.sem, 1)
                stat.wait(dve, b, 2 * NT)
                for t in range(NT):
                    dve.tensor_scalar(mv[:, t, 1:2], mv[:, t, 1:2], EPS, None, ALU.add).then_inc(stat.sem, 1)

            def layernorm(b, t):
                rstd_done.wait(dve, b, 1)
                dve.tensor_scalar(xs[:, t, :], xs[:, t, :], mv[:, t, 0:1], rstd[:, t:t + 1],
                                  ALU.subtract, ALU.mult).then_inc(xn_done.sem, 1)

            def low(dst, hi, src, sig):
                dve.tensor_tensor(dst, src, hi.bitcast(F32), ALU.subtract).then_inc(sig.sem, 1)

            def maxima(b, h, t):
                n = (t + 1) * P if causal else S
                qk_ready.wait(dve, b, h * NT + t + 1)
                dve.reduce_max(negmax[:, h % 2, t:t + 1], bank(("qk", h, t), 0, n), AX.X, negate=True).then_inc(max_done.sem, 1)

            def diagonals(b, h):
                max_done.wait(dve, b, (h + 1) * NT)
                if h >= 2:
                    kq_ready.wait(dve, b, (h - 1) * NT)
                dve.tensor_tensor(dneg[:, h % 2, :].rearrange("p (t k) -> p t k", k=P), env.ident[:].rearrange("p (o k) -> p o k", o=1).to_broadcast([P, NT, P]),
                                  negmax[:, h % 2, :].rearrange("p (t o) -> p t o", o=1).to_broadcast([P, NT, P]), ALU.mult).then_inc(dneg_done.sem, 1)

            def high(b, h, t):
                lo = keys_from(t)
                exp_done.wait(dve, b, h * NT + t + 1)
                if h >= 1:
                    pv_step.wait(dve, b, (h - 1) * NT + t + 1)
                dve.tensor_copy(probs_hi[:, t, lo:S], probs[:, t, lo:S]).then_inc(ph_dve.sem, 1)

            def low_probs(b, h, t):
                lo = keys_from(t)
                high_done(dve, b, h, t)
                low(probs_lo[:, t, lo:S], probs_hi[:, t, lo:S], probs[:, t, lo:S], pl_dve)

            def normalise(b, h):
                uT = bank(("uT", h), 0, NT * VW).rearrange("p (t w) -> p t w", w=VW)
                out = heads_out[:, :, h * HD:(h + 1) * HD]
                n = h * NS

                def step(k, ins):
                    ins.then_inc(norm.sem, 1)
                    norm.wait(dve, b, n + k)

                uT_ready.wait(dve, b, h + 1)
                step(1, dve.reciprocal(rsum[:], uT[:, :, HD]))
                if linear:
                    step(2, dve.tensor_scalar(rsum[:], rsum[:], g_not[:, h:h + 1], None, ALU.mult))
                by = rsum[:].rearrange("p (t o) -> p t o", o=1).to_broadcast([P, NT, HD])
                dve.tensor_tensor(piece_a[:], uT[:, :, 0:HD], by, ALU.mult).then_inc(norm.sem, 1)
                dve.tensor_tensor(piece_b[:], uT[:, :, HD + 1:2 * HD + 1], by, ALU.mult).then_inc(norm.sem, 1)
                if linear:
                    norm.wait(dve, b, n + 4)
                    step(5, dve.tensor_tensor(piece_a[:], piece_a[:], piece_b[:], ALU.add))
                    dve.tensor_tensor(out, out, piece_a[:], ALU.add).then_inc(norm.sem, 1)
                else:
                    norm.wait(dve, b, n + 3)
                    dve.tensor_tensor(out, piece_a[:], piece_b[:], ALU.add).then_inc(norm.sem, 1)

            def rotate(b, pair):
                which, c = pairs[2 * pair]
                tmp = (probs, heads_out)[pair % 2]
                first, second = bank((which, c)), bank((which, c + 2))
                q_ready.wait(dve, b, 2 * pair + 2)
                if pair >= 2:
                    q_lo.wait(dve, b, 2 * pair - 2)
                for k, (src, table) in enumerate(((first, cosT), (second, sinT), (second, cosT), (first, sinT))):
                    dve.tensor_tensor(tmp[:, k, :], src, table[:, c, :], ALU.mult).then_inc(rot_mul.sem, 1)
                rot_mul.wait(dve, b, 4 * pair + 2)
                dve.tensor_tensor(tmp[:, 0, :], tmp[:, 0, :], tmp[:, 1, :], ALU.subtract).then_inc(rot_done.sem, 1)
                rot_mul.wait(dve, b, 4 * pair + 4)
                dve.tensor_tensor(tmp[:, 2, :], tmp[:, 2, :], tmp[:, 3, :], ALU.add).then_inc(rot_done.sem, 1)

            def features(b, c):
                for w in range(2):
                    sum_done.wait(dve, b, 2 * c + w + 1)
                    if c >= 2:
                        (kf_ready.wait(dve, b, c - 1) if w == 0 else mo_ready.wait(dve, b, 2 * c - 2))
                    dve.tensor_scalar(feature(c, w), probs[:, 2 * w, :], 0.0, None, ALU.min).then_inc(clip_done.sem, 1)
                for w in range(2):
                    fexp_done.wait(dve, b, 2 * c + w + 1)
                    dve.scalar_tensor_tensor(out=feature(c, w), in0=probs[:, 2 * w, :], scalar=0.0, in1=feature(c, w),
                                             op0=ALU.max, op1=ALU.add).then_inc(feat_done.sem, 1)

            def linear_out(b, c):
                mem_ready.wait(dve, b, c + 1)
                if c >= 1:
                    mo_ready.wait(dve, b, 2 * c)
                dve.tensor_tensor(mem.rearrange("p h w -> p (h w)"), bank(("mem", c), 0, HW), env.blockmask[:], ALU.mult).then_inc(mem_done.sem, 1)
                for half in range(2):
                    mo = bank(("mo", c, half), 0, 2 * HW).rearrange("p (t h w) -> p t h w", h=HC, w=HD + 1)
                    n = 6 * c + 3 * half
                    mo_ready.wait(dve, b, 2 * c + half + 1)
                    mo_step.wait(dve, b, n)
                    dve.reciprocal(den, mo[:, :, :, HD]).then_inc(mo_step.sem, 1)
                    mo_step.wait(dve, b, n + 1)
                    dve.tensor_tensor(den, den, g_sig[:, HC * c:HC * c + HC].rearrange("p (o h) -> p o h", o=1).to_broadcast([P, 2, HC]),
                                      ALU.mult).then_inc(mo_step.sem, 1)
                    mo_step.wait(dve, b, n + 2)
                    dve.tensor_tensor(heads_out[:, 2 * half:2 * half + 2, c * P:(c + 1) * P].rearrange("p t (h w) -> p t h w", w=HD),
                                      mo[:, :, :, 0:HD], den.rearrange("p t (h o) -> p t h o", o=1).to_broadcast([P, 2, HC, HD]),
                                      ALU.mult).then_inc(mo_step.sem, 1)

            def split_turned(b, c):
                hi, lo = (xnT[0][:, c, :], xnT[1][:, c, :]) if c < NC else (cT[0][:, 0, :], cT[1][:, 0, :])
                xT_hi.wait(dve, b, c + 1)
                low(lo, hi, bank(("xT", c) if c < NC else ("cT", 0)), xT_lo)

            def split_heads(b, c):
                oT_hi.wait(dve, b, c + 1)
                low(probs_lo[:, c, :], probs_hi[:, c, :], bank(("oT", c)), oT_lo)

            def body(b, more):
                if linear:
                    xT_ready.wait(dve, b, NXT)
                    dve.memset(v_one[:, :, :, :, HD:HD + 1], 1.0).then_inc(one_col.sem, 1)
                    for pr in range(NC):
                        rotate(b, pr)
                else:
                    for n, (which, c) in enumerate(pairs):
                        hi, lo = (p[:, c, :] for p in (qT if which == "q" else kT))
                        q_hi.wait(dve, b, n + 1)
                        low(lo, hi, bank((which, c)), q_lo)
                for t in range(NT):
                    v_hi.wait(dve, b, t + 1)
                    low(v_split[:, t, :, HD + 1:2 * HD + 1], v_split[:, t, :, 0:HD],
                        bank(("v", t)).rearrange("p (h w) -> p h w", w=HD), v_lo)
                    if t == SCORES_AT:
                        for q in range(NT):
                            maxima(b, 0, q)
                        diagonals(b, 0)
                for c in range(NC + 1 if linear else 0):
                    if c < NC:
                        features(b, c)
                    if c >= 1:
                        linear_out(b, c - 1)
                for i in range(H + 2):
                    if i + 1 < H:
                        for t in range(NT):
                            maxima(b, i + 1, t)
                        diagonals(b, i + 1)
                    for t in range(NT if i < H else 0):
                        if t in PH_DVE and t < NT - 1:
                            high(b, i, t)
                        if t in PL_DVE and t < NT - 1:
                            low_probs(b, i, t)
                    for c in range(NXT if i == H and more else 0):
                        split_turned(b + 1, c)
                    if i == H + 1:
                        split_heads(b, 0)
                    if i >= 2:
                        normalise(b, i - 2)
                    if i < H and NT - 1 in PH_DVE:
                        high(b, i, NT - 1)
                    if i < H and NT - 1 in PL_DVE:
                        low_probs(b, i, NT - 1)
                    if more and LN_AT <= i < LN_AT + NT:
                        statistics(b + 1, i - LN_AT)
                    if more and i == LN_AT + NT:
                        variances(b + 1)
                    if more and LN_AT + NT < i <= LN_AT + 2 * NT:
                        layernorm(b + 1, i - LN_AT - NT - 1)
                for c in range(1, NC):
                    split_heads(b, c)
                for t in range(NT):
                    y_ready.wait(dve, b, t + 1)
                    res_in[t % 2].wait(dve, b, t // 2 * 16 + 16)
                    dve.tensor_tensor(res[:, t % 2, :], bank(("y", t)), res[:, t % 2, :], ALU.add).then_inc(y_done.sem, 1)

            dve.tensor_scalar(v_split[:, :, :, HD:HD + 1], env.ident[:, 0:NT * H].rearrange("p (t h o) -> p t h o", h=H, o=1), 0.0, 1.0,
                              ALU.mult, ALU.add).then_inc(ones_done, 1)
            if linear:
                dve.wait_ge(gates, 1)
                dve.tensor_scalar(gate_e[:], gate_e[:], 1.0, None, ALU.add).then_inc(gates, 1)
                dve.wait_ge(gates, 2)
                dve.reciprocal(g_sig[:], gate_e[:]).then_inc(gates, 1)
                dve.wait_ge(gates, 3)
                dve.tensor_scalar(g_not[:], g_sig[:], -1.0, 1.0, ALU.mult, ALU.add).then_inc(ones_done, 1)
                dve.wait_ge(ones_done, 2)
            for t in range(NT):
                statistics(0, t)
            variances(0)
            for t in range(NT):
                layernorm(0, t)
            for c in range(NXT):
                split_turned(0, c)
            batches(dve, body)

        @block.gpsimd
        def _(pool):
            def rstds(b):
                stat.wait(pool, b, 3 * NT)
                pool.tensor_tensor(rstd[:], mv[:, :, 1], env.minus_half[:, 0:NT], ALU.pow).then_inc(rstd_done.sem, 1)

            def body(b, more):
                if linear:
                    for n, (which, c) in enumerate(pairs):
                        hi, lo = (p[:, c, :] for p in (qT if which == "q" else kT))
                        q_hi.wait(pool, b, n + 1)
                        pool.tensor_tensor(lo, rotated(n), hi.bitcast(F32), ALU.subtract).then_inc(q_lo.sem, 1)
                    for c in range(NC):
                        for w, (hi, lo) in enumerate((kT, qT)):
                            q_lo.wait(pool, b, 2 * NC)
                            if c >= 1:
                                feat_done.wait(pool, b, 2 * c + w - 1)
                            pool.tensor_tensor(probs[:, 2 * w, :], hi[:, c, :].bitcast(F32), lo[:, c, :].bitcast(F32), ALU.add).then_inc(sum_done.sem, 1)
                        v_lo.wait(pool, b, NT)
                        if c >= 2:
                            mem_ready.wait(pool, b, c - 1)
                        hs = slice(HC * c, HC * c + HC)
                        pool.tensor_tensor(v_one[:, c % 2, :, :, 0:HD], v_split[:, :, hs, 0:HD].bitcast(F32),
                                           v_split[:, :, hs, HD + 1:2 * HD + 1].bitcast(F32), ALU.add).then_inc(v_one_done.sem, 1)
                for i in range(H):
                    for t in PL_POOL:
                        lo = keys_from(t)
                        high_done(pool, b, i, t)
                        if i >= 1:
                            pv_step.wait(pool, b, (i - 1) * NT + t + 1)
                        pool.tensor_tensor(probs_lo[:, t, lo:S], probs[:, t, lo:S], probs_hi[:, t, lo:S].bitcast(F32),
                                           ALU.subtract).then_inc(pl_pool.sem, 1)
                    if more and i == LN_AT + NT:
                        rstds(b + 1)

            rstds(0)
            batches(pool, body)


PL_DVE, PL_POOL = (1,), (0, 2, 3)
LN_AT = 5
SCORES = (("kq", 0), ("qk", 0), ("qk", 1), ("kq", 1), ("qk", 2), ("qk", 3), ("kq", 2), ("kq", 3))


def alloc_consts(nc, env, ctx):
    def sb(name, shape, dtype=F32):
        return ctx.enter_context(nc.sbuf_tensor(name, shape, dtype))

    env.ident, env.ident_r, env.one_r = sb("ident", [P, P]), sb("ident_r", [P, P], F32R), sb("one_r", [P, 1], F32R)
    env.sel = sb("sel", [P, HC, 7 * HD], F32R)
    env.blockmask = sb("blockmask", [P, HC * (HD + 1)])
    env.minus_half = sb("minus_half", [P, NT])



E_ROUTED, E_ALL, TOPK = 32, 64, 8
CAP = 256
SLOTS = E_ROUTED * CAP
W_SCALE, W_EPS = 1.5, 1e-20
GRAPH_HEADS = 4
GRAPH_TOP = max(1, int(S * 0.3))
GRAPH_SCALE = 1.0 / ((L // GRAPH_HEADS) ** 0.5 * GRAPH_HEADS)


def graph_and_router(nc, env, tag, x_in, x_out, ctx_in, wq, wk, gamma, w_cls, bias, slot_rows, none_row, slots, weights):
    with semaphores(nc) as take, ExitStack() as ctx:
        def sb(name, shape, dtype=F32):
            return ctx.enter_context(nc.sbuf_tensor(f"{tag}_{name}", shape, dtype))

        def sem(name):
            return take(f"{tag}_{name}")

        def signal(name, per, start=None):
            return Signal(nc, sem(name), per, start)

        def pair(name, shape):
            return sb(f"{name}_hi", shape, F32R), sb(f"{name}_lo", shape, F32R)

        wqT, wkT, wcT = pair("wq", [P, L]), pair("wk", [P, L]), pair("wc", [P, NC, E_ALL])
        w_raw, wc_raw = sb("w_raw", [P, 2, L]), sb("wc_raw", [E_ALL, D])
        cin = sb("cin", [P, NT, L])
        cT, qT, kT = pair("cT", [P, S]), pair("qT", [P, S]), pair("kT", [P, S])
        sim, work = sb("sim", [P, NT, S]), sb("work", [P, NT, S])
        top = sb("top", [P, NT, 8])
        xs, xo, xn = sb("xs", [P, NT, D]), sb("xo", [P, NT, D]), sb("xn", [P, NT, D])
        stats, mv, rstd = sb("stats", [P, NT, 6]), sb("mv", [P, NT, 2]), sb("rstd", [P, NT])
        carrier = sb("carrier", [P, 1])
        pool_carrier = sb("pool_carrier", [P, 2])
        gam = sb("gam", [P, 4])
        xnT = pair("xnT", [P, NC, S])
        bias_sb = sb("bias", [P, E_ALL])
        iota_i, iota = sb("iota_i", [P, E_ALL], I32), sb("iota", [P, E_ALL])
        before, ones = sb("before", [P, P], BF16), sb("ones", [P, P], BF16)
        tri = sb("tri", [P, P])
        logit, expd, score, biased = (sb(n, [P, NT, E_ALL]) for n in ("logit", "expd", "score", "biased"))
        r4 = sb("r4", [P, 6, NT])
        top_v, top_i = sb("top_v", [P, NT, TOPK]), sb("top_i", [P, NT, TOPK], U32)
        choice = sb("choice", [P, NT * TOPK])
        hot = sb("hot", [P, NT, TOPK, E_ALL])
        prod = sb("prod", [P, NT, TOPK, E_ALL])
        mask = sb("mask", [P, NT, E_ROUTED], BF16)
        place = sb("place", [P, NT, E_ROUTED])
        taken = sb("taken", [P, E_ROUTED])
        k8 = sb("k8", [P, 5, NT * TOPK])
        slot_now = sb("slot_now", [P, NT * TOPK], I32)
        zeros = sb("zeros", [P, 4 * D])
        ZERO_DMAS = SLOTS // P // 4
        zeroed = sem("zeroed")
        ps = ctx.enter_context(nc.psum_tensor(f"{tag}_ps", [P, 8, 512], F32))

        def bcast_last(ap, n, width):
            return ap.rearrange("p (n o) -> p n o", o=1).to_broadcast([P, n, width])

        def bcast_mid(ap, n):
            return ap.rearrange("p (o w) -> p o w", o=1).to_broadcast([P, n, ap.shape[-1]])

        MASK, ROUTE_STEPS = 11, 39
        in_sem, xs_in, ctx_sem, out_sem = sem("in"), signal("xs_in", 16), signal("ctx_in", 16), signal("x_out", 16)
        prep_pe, prep_act, prep_dve, prep_pool = sem("prep_pe"), sem("prep_act"), sem("prep_dve"), sem("prep_pool")
        turn, hi, lo = signal("turn", 3), signal("hi", 3), signal("lo", 3)
        xt, xhi, xlo = signal("xt", NC), signal("xhi", NC), signal("xlo", NC)
        sim_ready, sim_copied = signal("sim_ready", NT), signal("sim_copied", NT)
        ROUNDS = (GRAPH_TOP - 1) // 8
        maxed, struck = signal("maxed", NT * (ROUNDS + 1)), signal("struck", NT * ROUNDS)
        tanh_done, kept, adj = signal("tanh_done", NT), signal("kept", NT), signal("adj", NT)
        adjT, sums = signal("adjT", NT), signal("sums", 3 * NT)
        stat, rstd_done, xn_done = signal("stat", 6 * NT), signal("rstd_done", 2), signal("xn_done", 2 * NT)
        logits_ready, exp_done, route = signal("logits_ready", 1), signal("exp_done", 1), signal("route", ROUTE_STEPS)
        counted, slots_done, scattered = signal("counted", 1), signal("slots_done", 1), signal("scattered", NT * TOPK * 16, start=0)
        stored = signal("stored", 1)

        logits, counts = ps[:, 3, 0:NT * E_ALL], ps[:, 3, NT * E_ALL:NT * E_ALL + (NT + 1) * E_ROUTED]

        block = ctx.enter_context(nc.Block())

        @block.sync
        def _(sp):
            sp.dma_start(w_raw[:, 0, :], wq).then_inc(in_sem, 16)
            sp.dma_start(w_raw[:, 1, :], wk).then_inc(in_sem, 16)
            sp.dma_start(wc_raw[:], w_cls).then_inc(in_sem, 16)
            sp.dma_start(bias_sb[:], bias.partition_broadcast(P)).then_inc(in_sem, 16)
            sp.dma_start(gam[:, 0:1], gamma.partition_broadcast(P)).then_inc(in_sem, 16)

            def load_context(b):
                sp.dma_start(cin[:], ctx_in.rearrange("(b t p) d -> b p t d", p=P, t=NT)[bass.ds(b, 1)]
                             .rearrange("b p t d -> (b p) t d")).then_inc(ctx_sem.sem, 16)

            def load_x(b):
                sp.dma_start(xs[:], x_in.rearrange("(b t p) d -> b p t d", p=P, t=NT)[bass.ds(b, 1)]
                             .rearrange("b p t d -> (b p) t d")).then_inc(xs_in.sem, 16)

            def body(b, more):
                if more:
                    turn.wait(sp, b, 1)
                    load_context(b + 1)
                    sums.wait(sp, b, NT)
                    load_x(b + 1)
                sums.wait(sp, b, 3 * NT)
                sp.dma_start(x_out.rearrange("(b t p) d -> b p t d", p=P, t=NT)[bass.ds(b, 1)]
                             .rearrange("b p t d -> (b p) t d"), xo[:]).then_inc(out_sem.sem, 16)

            load_context(0)
            load_x(0)
            sp.wait_ge(prep_pool, 4)
            many = slot_rows.rearrange("(p q r) d -> q p (r d)", p=P, r=zeros.shape[1] // D)
            for q in range(ZERO_DMAS):
                sp.dma_start(many[q], zeros[:]).then_inc(zeroed, 16)
            sp.dma_start(none_row, zeros[0:1, 0:D]).then_inc(zeroed, 16)
            batches(sp, body)
            out_sem.wait(sp, B, 0)
            sp.wait_ge(zeroed, 16 * (ZERO_DMAS + 1))

        @block.tensor
        def _(pe):
            pe.wait_ge(in_sem, 80)
            for n in range(2):
                pe.transpose(ps[:, n, 0:P], w_raw[:, n, :], env.ident[:]).then_inc(prep_pe, 1)
            for c in range(NC):
                mm = pe.transpose(ps[:, 2, c * E_ALL:(c + 1) * E_ALL], wc_raw[:, c * P:(c + 1) * P], env.ident[0:E_ALL, 0:E_ALL])
            mm.then_inc(prep_pe, 1)
            pe.wait_ge(prep_dve, 4)

            def queries_keys(b):
                ctx_sem.wait(pe, b, 16)
                lo.wait(pe, b, 0)
                for t in range(NT):
                    mm = pe.transpose(ps[:, 0, t * P:(t + 1) * P], cin[:, t, :], env.ident[:])
                mm.then_inc(turn.sem, 1)
                lo.wait(pe, b, 1)
                for n, w in enumerate((wqT, wkT)):
                    split_mm(pe, ps[:, 1 + n, :], [p[:] for p in w], [p[:] for p in cT], True, True).then_inc(turn.sem, 1)

            def similarities(b):
                lo.wait(pe, b, 3)
                xlo.wait(pe, b, 0)
                for t in range(NT):
                    split_mm(pe, ps[:, 4 + t, :], [p[:, t * P:(t + 1) * P] for p in qT], [p[:] for p in kT], True, True
                             ).then_inc(sim_ready.sem, 1)

            def body(b, more):
                adj.wait(pe, b, NT)
                for t in range(NT):
                    for u in range(NT):
                        mm = pe.transpose(ps[:, 4 + t, u * P:(u + 1) * P], work[:, u, t * P:(t + 1) * P], env.ident[:])
                    mm.then_inc(adjT.sem, 1)
                if more:
                    queries_keys(b + 1)
                xn_done.wait(pe, b, 2 * NT)
                for c in range(NC):
                    for t in range(NT):
                        mm = pe.transpose(ps[:, 4 + c, t * P:(t + 1) * P], xn[:, t, c * P:(c + 1) * P], env.ident[:])
                    mm.then_inc(xt.sem, 1)
                xlo.wait(pe, b, NC)
                route.wait(pe, b, 0)
                for t in range(NT):
                    for c in range(NC):
                        mm = split_mm(pe, logits[:, t * E_ALL:(t + 1) * E_ALL], [p[:, c, t * P:(t + 1) * P] for p in xnT],
                                      [p[:, c, :] for p in wcT], t == 0 and c == 0, t == NT - 1 and c == NC - 1)
                mm.then_inc(logits_ready.sem, 1)
                if more:
                    similarities(b + 1)
                route.wait(pe, b, MASK)
                for t in range(NT):
                    pe.matmul(counts[:, t * E_ROUTED:(t + 1) * E_ROUTED], before[:], mask[:, t, :], start=t == 0, stop=False,
                              skip_group_check=True)
                    for u in range(t):
                        pe.matmul(counts[:, t * E_ROUTED:(t + 1) * E_ROUTED], ones[:], mask[:, u, :], start=False, stop=False,
                                  skip_group_check=True)
                for u in range(NT):
                    mm = pe.matmul(counts[:, NT * E_ROUTED:(NT + 1) * E_ROUTED], ones[:], mask[:, u, :], start=False, stop=u == NT - 1,
                                   skip_group_check=True)
                mm.then_inc(counted.sem, 1)

            queries_keys(0)
            similarities(0)
            batches(pe, body)

        @block.scalar
        def _(act):
            for n, w in enumerate((wqT, wkT)):
                act.wait_ge(prep_pe, n + 1)
                act.copy(w[0][:], ps[:, n, 0:P]).then_inc(prep_act, 1)
            act.wait_ge(prep_pe, 3)
            act.copy(wcT[0][:].rearrange("p c e -> p (c e)"), ps[:, 2, 0:NC * E_ALL]).then_inc(prep_act, 1)
            act.activation(gam[:, 1:2], gam[:, 0:1], ACT.Exp, scale=-1.0).then_inc(prep_act, 1)

            def high_parts(b):
                for n, dst in enumerate((cT, qT, kT)):
                    turn.wait(act, b, n + 1)
                    act.copy(dst[0][:], ps[:, n, :]).then_inc(hi.sem, 1)

            def keep_similarities(b):
                for t in range(NT):
                    sim_ready.wait(act, b, t + 1)
                    adj.wait(act, b, 0)
                    act.copy(sim[:, t, :], ps[:, 4 + t, :]).then_inc(sim_copied.sem, 1)

            def body(b, more):
                for t in range(NT):
                    maxed.wait(act, b, NT * (ROUNDS + 1))
                    act.activation(work[:, t, :], sim[:, t, :], ACT.Tanh, scale=0.5 * GRAPH_SCALE).then_inc(tanh_done.sem, 1)
                if more:
                    high_parts(b + 1)
                for c in range(NC):
                    xt.wait(act, b, c + 1)
                    act.copy(xnT[0][:, c, :], ps[:, 4 + c, :]).then_inc(xhi.sem, 1)
                route.wait(act, b, 2)
                act.activation(expd[:], logit[:], ACT.Exp).then_inc(exp_done.sem, 1)
                if more:
                    keep_similarities(b + 1)

            high_parts(0)
            keep_similarities(0)
            batches(act, body)

        @block.vector
        def _(dve):
            for n, w in enumerate((wqT, wkT)):
                dve.wait_ge(prep_act, n + 1)
                dve.tensor_tensor(w[1][:], ps[:, n, 0:P], w[0][:].bitcast(F32), ALU.subtract).then_inc(prep_dve, 1)
            dve.wait_ge(prep_act, 3)
            dve.tensor_tensor(wcT[1][:].rearrange("p c e -> p (c e)"), ps[:, 2, 0:NC * E_ALL],
                              wcT[0][:].rearrange("p c e -> p (c e)").bitcast(F32), ALU.subtract).then_inc(prep_dve, 1)
            dve.wait_ge(prep_pool, 3)
            dve.tensor_copy(before[:], tri[:]).then_inc(prep_dve, 1)
            dve.memset(taken[:], 0.0).then_inc(prep_dve, 1)
            dve.tensor_copy(iota[:], iota_i[:]).then_inc(prep_dve, 1)
            dve.wait_ge(prep_act, 4)
            dve.tensor_scalar(gam[:, 0:1], gam[:, 1:2], 1.0, None, ALU.add).then_inc(prep_dve, 1)
            dve.wait_ge(prep_dve, 7)
            dve.reciprocal(gam[:, 1:2], gam[:, 0:1]).then_inc(prep_dve, 1)
            dve.wait_ge(prep_dve, 8)
            dve.tensor_scalar(gam[:, 2:3], gam[:, 1:2], 0.25, None, ALU.mult).then_inc(prep_dve, 1)
            dve.tensor_scalar(gam[:, 3:4], gam[:, 1:2], -1.0, 1.0, ALU.mult, ALU.add).then_inc(prep_dve, 1)
            dve.wait_ge(prep_dve, 10)

            def layernorm(b, src, k):
                for t in range(NT):
                    dve.bn_stats(stats[:, t, :], src[:, t, :]).then_inc(stat.sem, 1)
                stat.wait(dve, b, 3 * NT * k + NT)
                dve.memset(carrier[:], 0.0)
                for t in range(NT):
                    dve.bn_aggr(mv[:, t, :], stats[:, t, :]).then_inc(stat.sem, 1)
                stat.wait(dve, b, 3 * NT * k + 2 * NT)
                for t in range(NT):
                    dve.tensor_scalar(mv[:, t, 1:2], mv[:, t, 1:2], EPS, None, ALU.add).then_inc(stat.sem, 1)
                rstd_done.wait(dve, b, k + 1)
                for t in range(NT):
                    dve.tensor_scalar(xn[:, t, :], src[:, t, :], mv[:, t, 0:1], rstd[:, t:t + 1],
                                      ALU.subtract, ALU.mult).then_inc(xn_done.sem, 1)

            def low_parts(b):
                for n, dst in enumerate((cT, qT, kT)):
                    hi.wait(dve, b, n + 1)
                    dve.tensor_tensor(dst[1][:], ps[:, n, :], dst[0][:].bitcast(F32), ALU.subtract).then_inc(lo.sem, 1)

            def body(b, more):
                sim_copied.wait(dve, b, NT)
                adjT.wait(dve, b, 0)
                dve.memset(carrier[:], 0.0)
                for r in range(ROUNDS + 1):
                    src = sim if r == 0 else work
                    for t in range(NT):
                        dve.max(top[:, t, :], src[:, t, :]).then_inc(maxed.sem, 1)
                    maxed.wait(dve, b, NT * (r + 1))
                    dve.memset(carrier[:], 0.0)
                    if r < ROUNDS:
                        for t in range(NT):
                            dve.match_replace(work[:, t, :], top[:, t, :], src[:, t, :], 2 * NEG).then_inc(struck.sem, 1)
                        struck.wait(dve, b, NT * (r + 1))
                        dve.memset(carrier[:], 0.0)
                xs_in.wait(dve, b, 16)
                stored.wait(dve, b, 0)
                out_sem.wait(dve, b, 0)
                layernorm(b, xs, 0)
                for t in range(NT):
                    xn_done.wait(dve, b, t + 1)
                    dve.scalar_tensor_tensor(out=xo[:, t, :], in0=xn[:, t, :], scalar=gam[:, 3:4], in1=xs[:, t, :],
                                             op0=ALU.mult, op1=ALU.add).then_inc(sums.sem, 1)
                last = GRAPH_TOP - 1 - 8 * ROUNDS
                for t in range(NT):
                    tanh_done.wait(dve, b, t + 1)
                    dve.tensor_scalar(sim[:, t, :], sim[:, t, :], top[:, t, last:last + 1], gam[:, 2:3],
                                      ALU.is_ge, ALU.mult).then_inc(kept.sem, 1)
                for t in range(NT):
                    kept.wait(dve, b, t + 1)
                    dve.scalar_tensor_tensor(out=work[:, t, :], in0=work[:, t, :], scalar=1.0, in1=sim[:, t, :],
                                             op0=ALU.add, op1=ALU.mult).then_inc(adj.sem, 1)
                for t in range(NT):
                    adj.wait(dve, b, t + 1)
                    sums.wait(dve, b, t + 1)
                    dve.tensor_tensor(xo[:, t, :], xo[:, t, :], work[:, t, :], ALU.add).then_inc(sums.sem, 1)
                for t in range(NT):
                    adjT.wait(dve, b, t + 1)
                    sums.wait(dve, b, NT + t + 1)
                    dve.tensor_tensor(xo[:, t, :], xo[:, t, :], ps[:, 4 + t, :], ALU.add).then_inc(sums.sem, 1)
                if more:
                    low_parts(b + 1)
                sums.wait(dve, b, 3 * NT)
                layernorm(b, xo, 1)
                for c in range(NC):
                    xhi.wait(dve, b, c + 1)
                    dve.tensor_tensor(xnT[1][:, c, :], ps[:, 4 + c, :], xnT[0][:, c, :].bitcast(F32), ALU.subtract).then_inc(xlo.sem, 1)
                router(b)

            def router(b):
                n = [0]

                def step(ins, wait=True):
                    ins.then_inc(route.sem, 1)
                    n[0] += 1
                    if wait:
                        route.wait(dve, b, n[0])

                lg = logits.rearrange("p (t e) -> p t e", e=E_ALL)
                logits_ready.wait(dve, b, 1)
                step(dve.reduce_max(r4[:, 0, :], lg, AX.X))
                step(dve.tensor_tensor(logit[:], lg, bcast_last(r4[:, 0, :], NT, E_ALL), ALU.subtract))
                exp_done.wait(dve, b, 1)
                step(dve.reduce_sum(r4[:, 1, :], expd[:], AX.X))
                step(dve.reciprocal(r4[:, 2, :], r4[:, 1, :]))
                step(dve.tensor_tensor(score[:], expd[:], bcast_last(r4[:, 2, :], NT, E_ALL), ALU.mult))
                step(dve.tensor_tensor(biased[:], score[:], bcast_mid(bias_sb[:], NT), ALU.add))
                dve.memset(carrier[:], 0.0)
                for t in range(NT):
                    mx = dve.max(top_v[:, t, :], biased[:, t, :])
                step(mx)
                dve.memset(carrier[:], 0.0)
                for t in range(NT):
                    mx = dve.max_index(top_i[:, t, :], top_v[:, t, :], biased[:, t, :])
                step(mx)
                step(dve.tensor_copy(choice[:], top_i[:].rearrange("p t k -> p (t k)")))
                step(dve.tensor_tensor(hot[:].rearrange("p t k e -> p (t k) e"), bcast_mid(iota[:], NT * TOPK),
                                       bcast_last(choice[:], NT * TOPK, E_ALL), ALU.is_equal))
                with nc.allow_low_precision(reason="zeros and ones"):
                    step(dve.tensor_reduce(mask[:], hot[:, :, :, 0:E_ROUTED].rearrange("p t k e -> p t e k"), AX.X, ALU.add), wait=False)
                assert n[0] == MASK
                for t in range(NT):
                    step(dve.tensor_tensor(prod[:, t], hot[:, t], bcast_mid(score[:, t, :], TOPK), ALU.mult), wait=t == NT - 1)
                step(dve.reduce_sum(k8[:, 0, :], prod[:].rearrange("p t k e -> p (t k) e"), AX.X))
                step(dve.reduce_sum(r4[:, 3, :], k8[:, 0, :].rearrange("p (t k) -> p t k", k=TOPK), AX.X))
                step(dve.tensor_scalar(r4[:, 3, :], r4[:, 3, :], W_EPS, None, ALU.add))
                step(dve.reciprocal(r4[:, 4, :], r4[:, 3, :]))
                step(dve.tensor_scalar(r4[:, 4, :], r4[:, 4, :], W_SCALE, None, ALU.mult))
                step(dve.tensor_tensor(k8[:, 0, :].rearrange("p (t k) -> p t k", k=TOPK), k8[:, 0, :].rearrange("p (t k) -> p t k", k=TOPK),
                                       bcast_last(r4[:, 4, :], NT, TOPK), ALU.mult))
                step(dve.tensor_scalar(k8[:, 1, :], choice[:], float(E_ROUTED), None, ALU.is_lt))
                step(dve.tensor_tensor(k8[:, 2, :], k8[:, 0, :], k8[:, 1, :], ALU.mult))
                step(dve.tensor_tensor(k8[:, 0, :], k8[:, 0, :], k8[:, 2, :], ALU.subtract))
                step(dve.reduce_sum(r4[:, 5, :], k8[:, 0, :].rearrange("p (t k) -> p t k", k=TOPK), AX.X))
                step(dve.tensor_scalar(r4[:, 5, :], r4[:, 5, :], 1.0, None, ALU.add))
                step(dve.tensor_tensor(k8[:, 2, :].rearrange("p (t k) -> p t k", k=TOPK), k8[:, 2, :].rearrange("p (t k) -> p t k", k=TOPK),
                                       bcast_last(r4[:, 5, :], NT, TOPK), ALU.mult))
                counted.wait(dve, b, 1)
                step(dve.tensor_tensor(place[:], counts[:, 0:NT * E_ROUTED].rearrange("p (t e) -> p t e", e=E_ROUTED),
                                       bcast_mid(taken[:], NT), ALU.add))
                step(dve.tensor_tensor(taken[:], taken[:], counts[:, NT * E_ROUTED:(NT + 1) * E_ROUTED], ALU.add))
                for t in range(NT):
                    step(dve.tensor_tensor(prod[:, t, :, 0:E_ROUTED], hot[:, t, :, 0:E_ROUTED], bcast_mid(place[:, t, :], TOPK), ALU.mult),
                         wait=t == NT - 1)
                step(dve.reduce_sum(k8[:, 3, :], prod[:, :, :, 0:E_ROUTED].rearrange("p t k e -> p (t k) e"), AX.X))
                step(dve.tensor_scalar(k8[:, 0, :], k8[:, 3, :], float(CAP), None, ALU.is_lt))
                step(dve.tensor_tensor(k8[:, 1, :], k8[:, 1, :], k8[:, 0, :], ALU.mult))
                step(dve.scalar_tensor_tensor(out=k8[:, 4, :], in0=choice[:], scalar=float(CAP), in1=k8[:, 3, :], op0=ALU.mult, op1=ALU.add))
                step(dve.scalar_tensor_tensor(out=k8[:, 4, :], in0=k8[:, 4, :], scalar=-float(SLOTS), in1=k8[:, 1, :], op0=ALU.add, op1=ALU.mult))
                step(dve.tensor_scalar(k8[:, 4, :], k8[:, 4, :], float(SLOTS), None, ALU.add))
                at = b * (NT * TOPK)
                stored.wait(dve, b, 0)
                dve.tensor_tensor(weights[:, bass.ds(at, NT * TOPK)], k8[:, 2, :], k8[:, 1, :], ALU.mult)
                dve.tensor_copy(slots[:, bass.ds(at, NT * TOPK)], k8[:, 4, :])
                dve.tensor_copy(slot_now[:], k8[:, 4, :]).then_inc(slots_done.sem, 1)
                assert n[0] == ROUTE_STEPS, n[0]

            low_parts(0)
            batches(dve, body)

        @block.gpsimd
        def _(pool):
            pool.memset(tri[:], 1.0).then_inc(prep_pool, 1)
            pool.memset(ones[:], 1.0)
            pool.wait_ge(prep_pool, 1)
            pool.affine_select(out=tri[:], in_=tri[:], compare_op=ALU.is_gt, fill=0.0, base=0,
                               pattern=[[1, P]], channel_multiplier=-1).then_inc(prep_pool, 1)
            pool.iota(iota_i[:], pattern=[[1, E_ALL]], base=0, channel_multiplier=0).then_inc(prep_pool, 1)
            pool.memset(zeros[:], 0.0).then_inc(prep_pool, 1)

            def body(b, more):
                for k in range(2):
                    stat.wait(pool, b, 3 * NT * (k + 1))
                    pool.tensor_tensor(rstd[:], mv[:, :, 1], env.minus_half[:, 0:NT], ALU.pow).then_inc(rstd_done.sem, 1)
                slots_done.wait(pool, b, 1)
                pool.tensor_tensor(pool_carrier[:, 0:1], env.minus_half[:, 0:1], env.minus_half[:, 0:1], ALU.mult)
                for t in range(NT):
                    for k in range(TOPK):
                        n = t * TOPK + k
                        pool.indirect_dma_start(slot_rows, bass.IndirectOffsetOnAxis(slot_now[:, n:n + 1], 0), xn[:, t, :], None,
                                                bounds_check=SLOTS - 1, oob_is_err=False).then_inc(scattered.sem, 16)
                scattered.wait(pool, b, NT * TOPK * 16)
                pool.tensor_tensor(pool_carrier[:, 1:2], env.minus_half[:, 0:1], env.minus_half[:, 0:1], ALU.mult).then_inc(stored.sem, 1)

            pool.wait_ge(zeroed, 16 * (ZERO_DMAS + 1))
            batches(pool, body)
            stored.wait(pool, B, 0)



I_DIM = 256


def experts(nc, env, tag, slot_rows, out_rows, w_gate_up, w_down):
    F = 2 * I_DIM // P
    G = I_DIM // P
    CT = CAP // P
    PAIRS = E_ROUTED // 2
    with semaphores(nc) as take, ExitStack() as ctx:
        def sb(name, shape, dtype=F32):
            return ctx.enter_context(nc.sbuf_tensor(f"{tag}_{name}", shape, dtype))

        def signals(name, per):
            return [Signal(nc, take(f"{tag}_{name}{u}"), per) for u in range(2)]

        raw_gu, raw_d = sb("raw_gu", [P, 2, NC, 2 * I_DIM]), sb("raw_d", [P, 2, G, D])
        gu_hi, gu_lo = sb("gu_hi", [P, 2, NC, 2 * I_DIM], F32R), sb("gu_lo", [P, 2, NC, 2 * I_DIM], F32R)
        d_hi, d_lo = sb("d_hi", [P, 2, G, D], F32R), sb("d_lo", [P, 2, G, D], F32R)
        rows = sb("rows", [P, 2, CT, D])
        x_hi, x_lo = sb("x_hi", [P, 2, NC, CAP], F32R), sb("x_lo", [P, 2, NC, CAP], F32R)
        silu, hid = sb("silu", [P, 2, G * CAP]), sb("hid", [P, 2, G * CAP])
        h_hi, h_lo = sb("h_hi", [P, 2, G, CAP], F32R), sb("h_lo", [P, 2, G, CAP], F32R)
        y = sb("y", [P, 2, CT, D])
        ps = ctx.enter_context(nc.psum_tensor(f"{tag}_ps", [P, 8, 512], F32))

        w_in, rows_in, y_out = signals("w_in", 32), signals("rows_in", 16), signals("y_out", 16)
        gu_hi_done, gu_lo_done = signals("gu_hi_done", 1), signals("gu_lo_done", 1)
        d_hi_done, d_lo_done = signals("d_hi_done", 1), signals("d_lo_done", 1)
        turned, x_hi_done, x_lo_done = signals("turned", 1), signals("x_hi_done", 1), signals("x_lo_done", 1)
        gu_ready, silu_done, hid_done = signals("gu_ready", 1), signals("silu_done", 1), signals("hid_done", 1)
        h_hi_done, h_lo_done = signals("h_hi_done", 1), signals("h_lo_done", 1)
        y_ready, y_act, y_dve = signals("y_ready", CT), signals("y_act", 1), signals("y_dve", 1)

        def pairs(eng, body):
            with eng.Fori(0, PAIRS - 1) as i:
                body(i, 0, True)
                body(i, 1, True)
            body(PAIRS - 1, 0, False)
            body(PAIRS - 1, 1, False)

        gu_dram = w_gate_up.rearrange("e (c p) f -> e p c f", p=P)
        d_dram = w_down.rearrange("e (c p) f -> e p c f", p=P)
        rows_dram = slot_rows.rearrange("(e t p) d -> e p t d", p=P, t=CT)
        y_dram = out_rows.rearrange("(e t p) d -> e p t d", p=P, t=CT)
        block = ctx.enter_context(nc.Block())

        @block.sync
        def _(sp):
            def load(i, u):
                e = i * 2 + u
                turned[u].wait(sp, i, 0)
                sp.dma_start(rows[:, u], rows_dram[bass.ds(e, 1)].rearrange("e p t d -> (e p) t d")).then_inc(rows_in[u].sem, 16)
                gu_lo_done[u].wait(sp, i, 0)
                d_lo_done[u].wait(sp, i, 0)
                sp.dma_start(raw_gu[:, u], gu_dram[bass.ds(e, 1)].rearrange("e p c f -> (e p) c f")).then_inc(w_in[u].sem, 16)
                sp.dma_start(raw_d[:, u], d_dram[bass.ds(e, 1)].rearrange("e p c f -> (e p) c f")).then_inc(w_in[u].sem, 16)

            def store(i, u):
                y_act[u].wait(sp, i, 1)
                y_dve[u].wait(sp, i, 1)
                sp.dma_start(y_dram[bass.ds(i * 2 + u, 1)].rearrange("e p t d -> (e p) t d"), y[:, u]).then_inc(y_out[u].sem, 16)

            load(0, 0)
            load(0, 1)
            load(1, 0)
            with sp.Fori(0, PAIRS - 2) as i:
                load(i + 1, 1)
                store(i, 0)
                load(i + 2, 0)
                store(i, 1)
            load(PAIRS - 1, 1)
            for i in (PAIRS - 2, PAIRS - 1):
                store(i, 0)
                store(i, 1)
            for u in range(2):
                y_out[u].wait(sp, PAIRS, 0)

        @block.tensor
        def _(pe):
            def turn(i, u, after):
                rows_in[u].wait(pe, i, 16)
                if after is not None:
                    x_lo_done[after[1]].wait(pe, after[0], 1)
                for c in range(NC):
                    for t in range(CT):
                        at = c * CAP + t * P
                        mm = pe.transpose(ps[:, at // 512, at % 512:at % 512 + P], rows[:, u, t, c * P:(c + 1) * P], env.ident[:])
                mm.then_inc(turned[u].sem, 1)

            def gate_up(i, u):
                gu_hi_done[u].wait(pe, i, 1)
                gu_lo_done[u].wait(pe, i, 1)
                x_lo_done[u].wait(pe, i, 1)
                hid_done[u].wait(pe, i, 0)
                for f in range(F):
                    at = f * CAP
                    for c in range(NC):
                        mm = split_mm(pe, ps[:, 2 + 2 * u + at // 512, at % 512:at % 512 + CAP],
                                      [w[:, u, c, f * P:(f + 1) * P] for w in (gu_hi, gu_lo)], [x[:, u, c, :] for x in (x_hi, x_lo)],
                                      c == 0, c == NC - 1)
                mm.then_inc(gu_ready[u].sem, 1)

            def down(i, u, after):
                h_lo_done[u].wait(pe, i, 1)
                d_hi_done[u].wait(pe, i, 1)
                d_lo_done[u].wait(pe, i, 1)
                if after is not None:
                    y_act[after[1]].wait(pe, *after[0])
                    y_dve[after[1]].wait(pe, *after[0])
                for t in range(CT):
                    for g in range(G):
                        mm = split_mm(pe, ps[:, 6 + t, :], [h[:, u, g, t * P:(t + 1) * P] for h in (h_hi, h_lo)],
                                      [w[:, u, g, :] for w in (d_hi, d_lo)], g == 0, g == G - 1)
                    mm.then_inc(y_ready[u].sem, 1)

            turn(0, 0, None)
            turn(0, 1, (0, 0))
            gate_up(0, 0)
            with pe.Fori(0, PAIRS - 1) as i:
                turn(i + 1, 0, (i, 1))
                gate_up(i, 1)
                down(i, 0, ((i, 0), 1))
                turn(i + 1, 1, (i + 1, 0))
                gate_up(i + 1, 0)
                down(i, 1, ((i, 1), 0))
            gate_up(PAIRS - 1, 1)
            down(PAIRS - 1, 0, ((PAIRS - 1, 0), 1))
            down(PAIRS - 1, 1, ((PAIRS - 1, 1), 0))

        def flat(ap):
            return ap.rearrange("p a b -> p (a b)")

        @block.scalar
        def _(act):
            def split_gu(i, u):
                w_in[u].wait(act, i, 32)
                gu_ready[u].wait(act, i, 0)
                act.copy(flat(gu_hi[:, u]), flat(raw_gu[:, u])).then_inc(gu_hi_done[u].sem, 1)

            def split_down(i, u):
                y_ready[u].wait(act, i, 0)
                act.copy(flat(d_hi[:, u]), flat(raw_d[:, u])).then_inc(d_hi_done[u].sem, 1)

            def split_x(i, u):
                turned[u].wait(act, i, 1)
                act.copy(flat(x_hi[:, u]), flat(ps[:, 0:2, :])).then_inc(x_hi_done[u].sem, 1)

            def body(i, u, more):
                gu_ready[u].wait(act, i, 1)
                act.activation(silu[:, u, :], ps[:, 2 + 2 * u, :], ACT.Silu).then_inc(silu_done[u].sem, 1)
                hid_done[u].wait(act, i, 1)
                act.copy(flat(h_hi[:, u]), hid[:, u, :]).then_inc(h_hi_done[u].sem, 1)
                if more:
                    split_x(i + 1, u)
                    split_gu(i + 1, u)
                y_ready[u].wait(act, i, 1)
                y_out[u].wait(act, i, 0)
                act.copy(y[:, u, 0, :], ps[:, 6, :]).then_inc(y_act[u].sem, 1)
                if more:
                    split_down(i + 1, u)

            for u in range(2):
                split_gu(0, u)
                split_down(0, u)
                split_x(0, u)
            pairs(act, body)

        @block.vector
        def _(dve):
            def low(dst, src, hi, sig):
                dve.tensor_tensor(dst, src, hi.bitcast(F32), ALU.subtract).then_inc(sig.sem, 1)

            def split_gu(i, u):
                gu_hi_done[u].wait(dve, i, 1)
                low(flat(gu_lo[:, u]), flat(raw_gu[:, u]), flat(gu_hi[:, u]), gu_lo_done[u])

            def split_x(i, u):
                x_hi_done[u].wait(dve, i, 1)
                low(flat(x_lo[:, u]), flat(ps[:, 0:2, :]), flat(x_hi[:, u]), x_lo_done[u])

            def body(i, u, more):
                silu_done[u].wait(dve, i, 1)
                dve.tensor_tensor(hid[:, u, :], silu[:, u, :], ps[:, 3 + 2 * u, :], ALU.mult).then_inc(hid_done[u].sem, 1)
                h_hi_done[u].wait(dve, i, 1)
                low(flat(h_lo[:, u]), hid[:, u, :], flat(h_hi[:, u]), h_lo_done[u])
                if more:
                    split_x(i + 1, u)
                    split_gu(i + 1, u)
                y_ready[u].wait(dve, i, 2)
                y_out[u].wait(dve, i, 0)
                dve.tensor_copy(y[:, u, 1, :], ps[:, 7, :]).then_inc(y_dve[u].sem, 1)

            for u in range(2):
                split_gu(0, u)
                split_x(0, u)
            pairs(dve, body)

        @block.gpsimd
        def _(pool):
            def split_d(i, u):
                d_hi_done[u].wait(pool, i, 1)
                pool.tensor_tensor(flat(d_lo[:, u]), flat(raw_d[:, u]), flat(d_hi[:, u]).bitcast(F32), ALU.subtract
                                   ).then_inc(d_lo_done[u].sem, 1)

            def body(i, u, more):
                if more:
                    split_d(i + 1, u)

            split_d(0, 0)
            split_d(0, 1)
            pairs(pool, body)


def combine(nc, env, tag, x_in, x_out, out_rows, slots, weights, w2, w2_mixed):
    with semaphores(nc) as take, ExitStack() as ctx:
        def sb(name, shape, dtype=F32):
            return ctx.enter_context(nc.sbuf_tensor(f"{tag}_{name}", shape, dtype))

        def signals(name, per, start=None):
            return [Signal(nc, take(f"{tag}_{name}{u}"), per, start) for u in range(2)]

        ROUND = B * NT // NT
        EACH = ROUND // 2
        STAGES = (HID // P).bit_length() - 1
        assert STAGES == ROUND
        got = sb("got", [P, 2, TOPK, D])
        acc = sb("acc", [P, 2, D])
        slot_now, weight_now = sb("slot_now", [P, 2, TOPK], I32), sb("weight_now", [P, 2, TOPK])
        mix, w2_raw = sb("mix", [P, 2, HID]), sb("w2_raw", [P, HID])
        carrier, pool_carrier = sb("carrier", [P, 1]), sb("pool_carrier", [P, 4])
        x_sem, got_sem, out_sem = signals("x_in", 16 * EACH), signals("got", 16 * TOPK * EACH, start=0), signals("out", 16 * EACH)
        slot_sem, weight_sem, summed = signals("slot", EACH), signals("weight", EACH), signals("summed", TOPK * EACH)
        w2_in, w2_out = (Signal(nc, take(f"{tag}_{n}"), 16) for n in ("w2_in", "w2_out"))
        mixed = Signal(nc, take(f"{tag}_mixed"), 2 * STAGES)
        block = ctx.enter_context(nc.Block())
        rows_in = x_in.rearrange("(t p) d -> t p d", p=P)
        rows_out = x_out.rearrange("(t p) d -> t p d", p=P)

        @block.sync
        def _(sp):
            def load_w2(i):
                sp.dma_start(w2_raw[:], w2.rearrange("(t p) h -> t p h", p=P)[bass.ds(i, 1)].rearrange("t p h -> (t p) h")
                             ).then_inc(w2_in.sem, 16)

            def body(i, more):
                for v in range(0, ROUND, 2):
                    for u in range(2):
                        out_sem[u].wait(sp, i, 16 * (v // 2))
                        sp.dma_start(acc[:, u, :], rows_in[bass.ds(i * ROUND + v + u, 1)].rearrange("t p d -> (t p) d")
                                     ).then_inc(x_sem[u].sem, 16)
                    if more and v == 0:
                        mixed.wait(sp, i, 2)
                        load_w2(i + 1)
                    for u in range(2):
                        if v + u == ROUND - 1:
                            mixed.wait(sp, i, 2 * STAGES)
                            sp.dma_start(w2_mixed.rearrange("(t p) h -> t p h", p=P)[bass.ds(i, 1)].rearrange("t p h -> (t p) h"),
                                         mix[:, (STAGES - 1) % 2, :]).then_inc(w2_out.sem, 16)
                        summed[u].wait(sp, i, TOPK * (v // 2 + 1))
                        sp.dma_start(rows_out[bass.ds(i * ROUND + v + u, 1)].rearrange("t p d -> (t p) d"), acc[:, u, :]
                                     ).then_inc(out_sem[u].sem, 16)

            load_w2(0)
            batches(sp, body)
            for u in range(2):
                out_sem[u].wait(sp, NT, 0)
            w2_out.wait(sp, NT, 0)

        @block.gpsimd
        def _(pool):
            with pool.Fori(0, NT) as i:
                for v in range(ROUND):
                    u, n = v % 2, v // 2
                    at = (i * ROUND + v) * TOPK
                    summed[u].wait(pool, i, TOPK * n)
                    pool.tensor_tensor(pool_carrier[:, 2 * u:2 * u + 1], env.minus_half[:, 0:1], env.minus_half[:, 0:1], ALU.mult)
                    pool.tensor_copy(slot_now[:, u, :], slots[:, bass.ds(at, TOPK)]).then_inc(slot_sem[u].sem, 1)
                    slot_sem[u].wait(pool, i, n + 1)
                    pool.tensor_tensor(pool_carrier[:, 2 * u + 1:2 * u + 2], env.minus_half[:, 0:1], env.minus_half[:, 0:1], ALU.mult)
                    for k in range(TOPK):
                        pool.indirect_dma_start(got[:, u, k, :], None, out_rows, bass.IndirectOffsetOnAxis(slot_now[:, u, k:k + 1], 0)
                                                ).then_inc(got_sem[u].sem, 16)

        @block.vector
        def _(dve):
            def butterfly(i, stage):
                n = 1 << stage
                src, dst = mix[:, (stage - 1) % 2, :] if stage else w2_raw[:], mix[:, stage % 2, :]
                a, b, c, d = (m.rearrange("p (g h k) -> p g h k", h=2, k=n * P)[:, :, h, :] for m in (src, dst) for h in range(2))
                if stage == 0:
                    w2_in.wait(dve, i, 16)
                if stage == 1:
                    w2_out.wait(dve, i, 0)
                mixed.wait(dve, i, 2 * stage)
                dve.tensor_tensor(c, a, b, ALU.add).then_inc(mixed.sem, 1)
                dve.tensor_tensor(d, a, b, ALU.subtract).then_inc(mixed.sem, 1)

            with dve.Fori(0, NT) as i:
                for v in range(ROUND):
                    u, n = v % 2, v // 2
                    butterfly(i, v)
                    at = (i * ROUND + v) * TOPK
                    summed[u].wait(dve, i, TOPK * n)
                    dve.memset(carrier[:], 0.0)
                    dve.tensor_copy(weight_now[:, u, :], weights[:, bass.ds(at, TOPK)]).then_inc(weight_sem[u].sem, 1)
                    weight_sem[u].wait(dve, i, n + 1)
                    x_sem[u].wait(dve, i, 16 * (n + 1))
                    got_sem[u].wait(dve, i, 16 * TOPK * (n + 1))
                    for k in range(TOPK):
                        if k:
                            summed[u].wait(dve, i, TOPK * n + k)
                        dve.scalar_tensor_tensor(out=acc[:, u, :], in0=got[:, u, k, :], scalar=weight_now[:, u, k:k + 1], in1=acc[:, u, :],
                                                 op0=ALU.mult, op1=ALU.add).then_inc(summed[u].sem, 1)



def network(nc, env, tag, x_in, x_mid, x_out, w1, w3, w2_mixed):
    HC2 = HID // P
    HALF = HC2 // 2
    with semaphores(nc) as take_outer, ExitStack() as ctx:
        def sb(name, shape, dtype=F32):
            return ctx.enter_context(nc.sbuf_tensor(f"{tag}_{name}", shape, dtype))

        w2_in = take_outer(f"{tag}_w2_in")
        xs = sb("xs", [P, NT, D])

        w2m = sb("w2m", [P, NT, HID])
        had = sb("had", [P, P], F32R)
        had_raw = sb("had_raw", [P, P])

        xs_in = [Signal(nc, take_outer(f"{tag}_xs_in{half}"), 16) for half in range(2)]

        def load_ahead(sp, half):
            if half == 0:
                sp.dma_start(w2m[:], tiles(w2_mixed)).then_inc(w2_in, 16)
                sp.dma_start(had_raw[:], env.hadamard).then_inc(w2_in, 16)
            sp.dma_start(xs[:], tiles(x_in[0:S, :])).then_inc(xs_in[half].sem, 16)

        def pair(name, shape):
            return sb(f"{name}_hi", shape, F32R), sb(f"{name}_lo", shape, F32R)

        w1T, w3T, w2T = pair("w1", [P, NC, HALF * P]), pair("w3", [P, NC, HALF * P]), pair("w2", [P, HALF, D])
        for half in range(2):
            rows = slice(half * HALF * P, (half + 1) * HALF * P)
            load_weights(nc, env, f"{tag}_w{half}", [(w1[rows, :], *w1T), (w3[rows, :], *w3T)],
                         also=lambda sp: load_ahead(sp, half))
            with semaphores(nc) as take, ExitStack() as prep:
                t_hi, t_lo = (prep.enter_context(nc.sbuf_tensor(f"{tag}_{n}{half}", [P, 2, D], F32R)) for n in ("t_hi", "t_lo"))
                scaled = prep.enter_context(nc.sbuf_tensor(f"{tag}_scaled{half}", [P, 2, D], F32))
                ps = prep.enter_context(nc.psum_tensor(f"{tag}_pps{half}", [P, 4, 512], F32))
                turned, t_hi_done, t_lo_done, prod, sc_done, w_hi, w_lo = (
                    take(f"{tag}_{n}{half}") for n in ("turned", "thi", "tlo", "prod", "sc", "whi", "wlo"))
                had_done = take(f"{tag}_had_done{half}")
                block = prep.enter_context(nc.Block())

                @block.tensor
                def _(pe):
                    def product(k):
                        pe.wait_ge(t_lo_done, k + 1)
                        if k >= 2:
                            pe.wait_ge(sc_done, k - 1)
                        pe.matmul(ps[:, 2 + k % 2, :], had[:], t_hi[:, k % 2, :], start=True, stop=False)
                        pe.matmul(ps[:, 2 + k % 2, :], had[:], t_lo[:, k % 2, :], start=False, stop=True).then_inc(prod, 1)

                    if half == 0:
                        pe.wait_ge(had_done, 1)
                    for k in range(HALF):
                        at = (half * HALF + k) * P
                        if k >= 2:
                            pe.wait_ge(t_lo_done, k - 1)
                        for t in range(NT):
                            mm = pe.transpose(ps[:, k % 2, t * P:(t + 1) * P], w2m[:, t, at:at + P], env.ident[:])
                        mm.then_inc(turned, 1)
                        if k >= 1:
                            product(k - 1)
                    product(HALF - 1)

                @block.scalar
                def _(act):
                    def second(k):
                        act.wait_ge(prod, k + 1)
                        if k >= 2:
                            act.wait_ge(w_lo, k - 1)
                        act.mul(scaled[:, k % 2, :], ps[:, 2 + k % 2, :], HID ** -0.5).then_inc(sc_done, 1)
                        act.wait_ge(sc_done, k + 1)
                        act.copy(w2T[0][:, k, :], scaled[:, k % 2, :]).then_inc(w_hi, 1)

                    for k in range(HALF):
                        act.wait_ge(turned, k + 1)
                        if k >= 2:
                            act.wait_ge(prod, k - 1)
                        act.copy(t_hi[:, k % 2, :], ps[:, k % 2, :]).then_inc(t_hi_done, 1)
                        if k >= 1:
                            second(k - 1)
                    second(HALF - 1)

                @block.vector
                def _(dve):
                    def second(k):
                        dve.wait_ge(w_hi, k + 1)
                        dve.tensor_tensor(w2T[1][:, k, :], scaled[:, k % 2, :], w2T[0][:, k, :].bitcast(F32), ALU.subtract).then_inc(w_lo, 1)

                    if half == 0:
                        dve.wait_ge(w2_in, 32)
                        dve.tensor_copy(had[:], had_raw[:]).then_inc(had_done, 1)
                    for k in range(HALF):
                        dve.wait_ge(t_hi_done, k + 1)
                        dve.tensor_tensor(t_lo[:, k % 2, :], ps[:, k % 2, :], t_hi[:, k % 2, :].bitcast(F32), ALU.subtract).then_inc(t_lo_done, 1)
                        if k >= 1:
                            second(k - 1)
                    second(HALF - 1)
            half_network(nc, env, f"{tag}{half}", x_in, (x_in, x_mid)[half], (x_mid, x_out)[half], w1T, w3T, w2T, HALF,
                         xs, xs_in[half])


def half_network(nc, env, tag, x_in, x_res, x_out, w1T, w3T, w2T, chunks, xs, xs_in):
    with semaphores(nc) as take, ExitStack() as ctx:
        def sb(name, shape, dtype=F32):
            return ctx.enter_context(nc.sbuf_tensor(f"{tag}_{name}", shape, dtype))

        def sem(name):
            return take(f"{tag}_{name}")

        def signal(name, per, start=None):
            return Signal(nc, sem(name), per, start)

        def pair(name, shape):
            return sb(f"{name}_hi", shape, F32R), sb(f"{name}_lo", shape, F32R)

        res = sb("res", [P, NT, D])
        xnT = pair("xnT", [P, NC, S])
        stats, mv, rstd, carrier = sb("stats", [P, NT, 6]), sb("mv", [P, NT, 2]), sb("rstd", [P, NT]), sb("carrier", [P, 1])
        gated, hid = sb("gated", [P, 2, S]), sb("hid", [P, 2, S])
        h_hi, h_lo = sb("h_hi", [P, 2, S], F32R), sb("h_lo", [P, 2, S], F32R)
        ps = ctx.enter_context(nc.psum_tensor(f"{tag}_ps", [P, 8, 512], F32))
        res_in, out_sem = signal("res_in", 16), signal("out", 16)
        stat, rstd_done, xn_done = signal("stat", 3 * NT), signal("rstd_done", 1), signal("xn_done", NT)
        xT_ready, xT_hi, xT_lo = signal("xT_ready", NC), signal("xT_hi", NC), signal("xT_lo", NC)
        gu_ready, silu_done, hid_done = signal("gu_ready", chunks), signal("silu_done", chunks), signal("hid_done", chunks)
        h_hi_done, h_lo_done, used = signal("h_hi_done", chunks), signal("h_lo_done", chunks), signal("used", chunks)
        y_done = signal("y_done", NT)
        block = ctx.enter_context(nc.Block())

        @block.sync
        def _(sp):
            def batch(x, b):
                return x.rearrange("(b t p) d -> b p t d", p=P, t=NT)[bass.ds(b, 1)].rearrange("b p t d -> (b p) t d")

            def body(b, more):
                out_sem.wait(sp, b, 0)
                sp.dma_start(res[:], batch(x_res, b)).then_inc(res_in.sem, 16)
                if more:
                    xT_ready.wait(sp, b, NC)
                    sp.dma_start(xs[:], batch(x_in, b + 1)).then_inc(xs_in.sem, 16)
                y_done.wait(sp, b, NT)
                sp.dma_start(batch(x_out, b), res[:]).then_inc(out_sem.sem, 16)

            batches(sp, body)
            out_sem.wait(sp, B, 0)

        @block.tensor
        def _(pe):
            def gate_up(b, k):
                if k >= 2:
                    hid_done.wait(pe, b, k - 1)
                for n, w in enumerate((w1T, w3T)):
                    for c in range(NC):
                        mm = split_mm(pe, ps[:, 2 * (k % 2) + n, :], [p[:, c, k * P:(k + 1) * P] for p in w],
                                      [p[:, c, :] for p in xnT], c == 0, c == NC - 1)
                mm.then_inc(gu_ready.sem, 1)

            def down(b, k):
                h_lo_done.wait(pe, b, k + 1)
                if k == 0:
                    y_done.wait(pe, b, 0)
                for t in range(NT):
                    mm = split_mm(pe, ps[:, 4 + t, :], [h[:, k % 2, t * P:(t + 1) * P] for h in (h_hi, h_lo)],
                                  [p[:, k, :] for p in w2T], k == 0, k == chunks - 1)
                mm.then_inc(used.sem, 1)

            def body(b, more):
                hid_done.wait(pe, b, 0)
                for c in range(NC):
                    for t in range(NT):
                        if c == 0:
                            xn_done.wait(pe, b, t + 1)
                        mm = pe.transpose(ps[:, c, t * P:(t + 1) * P], xs[:, t, c * P:(c + 1) * P], env.ident[:])
                    mm.then_inc(xT_ready.sem, 1)
                xT_lo.wait(pe, b, NC)
                gate_up(b, 0)
                for k in range(chunks):
                    if k + 1 < chunks:
                        gate_up(b, k + 1)
                    down(b, k)

            batches(pe, body)

        @block.scalar
        def _(act):
            def body(b, more):
                for c in range(NC):
                    xT_ready.wait(act, b, c + 1)
                    act.copy(xnT[0][:, c, :], ps[:, c, :]).then_inc(xT_hi.sem, 1)
                for k in range(chunks):
                    gu_ready.wait(act, b, k + 1)
                    act.activation(gated[:, k % 2, :], ps[:, 2 * (k % 2), :], ACT.Silu).then_inc(silu_done.sem, 1)
                    hid_done.wait(act, b, k + 1)
                    if k >= 2:
                        used.wait(act, b, k - 1)
                    act.copy(h_hi[:, k % 2, :], hid[:, k % 2, :]).then_inc(h_hi_done.sem, 1)

            batches(act, body)

        @block.vector
        def _(dve):
            def layernorm(b):
                xs_in.wait(dve, b, 16)
                for t in range(NT):
                    dve.bn_stats(stats[:, t, :], xs[:, t, :]).then_inc(stat.sem, 1)
                stat.wait(dve, b, NT)
                dve.memset(carrier[:], 0.0)
                for t in range(NT):
                    dve.bn_aggr(mv[:, t, :], stats[:, t, :]).then_inc(stat.sem, 1)
                stat.wait(dve, b, 2 * NT)
                for t in range(NT):
                    dve.tensor_scalar(mv[:, t, 1:2], mv[:, t, 1:2], EPS, None, ALU.add).then_inc(stat.sem, 1)
                rstd_done.wait(dve, b, 1)
                for t in range(NT):
                    dve.tensor_scalar(xs[:, t, :], xs[:, t, :], mv[:, t, 0:1], rstd[:, t:t + 1],
                                      ALU.subtract, ALU.mult).then_inc(xn_done.sem, 1)

            def body(b, more):
                for c in range(NC):
                    xT_hi.wait(dve, b, c + 1)
                    dve.tensor_tensor(xnT[1][:, c, :], ps[:, c, :], xnT[0][:, c, :].bitcast(F32), ALU.subtract).then_inc(xT_lo.sem, 1)
                for k in range(chunks):
                    silu_done.wait(dve, b, k + 1)
                    dve.tensor_tensor(hid[:, k % 2, :], gated[:, k % 2, :], ps[:, 2 * (k % 2) + 1, :], ALU.mult).then_inc(hid_done.sem, 1)
                    h_hi_done.wait(dve, b, k + 1)
                    dve.tensor_tensor(h_lo[:, k % 2, :], hid[:, k % 2, :], h_hi[:, k % 2, :].bitcast(F32), ALU.subtract).then_inc(h_lo_done.sem, 1)
                    if more and k == chunks // 2:
                        layernorm(b + 1)
                used.wait(dve, b, chunks)
                res_in.wait(dve, b, 16)
                for t in range(NT):
                    dve.tensor_tensor(res[:, t, :], ps[:, 4 + t, :], res[:, t, :], ALU.add).then_inc(y_done.sem, 1)

            layernorm(0)
            batches(dve, body)

        @block.gpsimd
        def _(pool):
            def rstds(b):
                stat.wait(pool, b, 3 * NT)
                pool.tensor_tensor(rstd[:], mv[:, :, 1], env.minus_half[:, 0:NT], ALU.pow).then_inc(rstd_done.sem, 1)

            rstds(0)
            with pool.Fori(0, B - 1) as b:
                rstds(b + 1)



def decoder(nc, arg, out):
    env = Env()
    env.cos, env.sin, env.hadamard = arg["cos"], arg["sin"], arg["hadamard"]
    x = arg["x"].rearrange("b s d -> (b s) d")
    context = arg["ctx_512"].rearrange("b s d -> (b s) d")
    steps = [nc.dram_tensor(f"x_after_{n}", [T, D], F32).ap()
             for n in ("attn0", "graph", "experts", "attn1", "cross", "half")]
    w2_mixed = nc.dram_tensor("w2_mixed", [D, HID], F32).ap()
    slot_rows = nc.dram_tensor("slot_rows", [SLOTS, D], F32).ap()
    out_rows = nc.dram_tensor("out_rows", [SLOTS + 1, D], F32).ap()
    with ExitStack() as ctx:
        alloc_consts(nc, env, ctx)
        constants(nc, env)
        attention(nc, env, "a0", x, steps[0], arg["L0_attn_Wq"], arg["L0_attn_Wk"], arg["L0_attn_Wv"], arg["L0_attn_Wo"],
                  gate=arg["L0_attn_gate"])
        with ExitStack() as moe:
            slots = moe.enter_context(nc.sbuf_tensor("slots", [P, B * NT * TOPK], I32))
            weights = moe.enter_context(nc.sbuf_tensor("weights", [P, B * NT * TOPK], F32))
            graph_and_router(nc, env, "gr", steps[0], steps[1], context, arg["L0_xattn_Wq"], arg["L0_xattn_Wk"],
                             arg["L0_xattn_gamma_raw"], arg["L0_ffn_w_cls"], arg["L0_ffn_bias"], slot_rows,
                             out_rows[SLOTS:SLOTS + 1, :], slots, weights)
            experts(nc, env, "ex", slot_rows, out_rows[0:SLOTS, :], arg["L0_ffn_w_gate_up"], arg["L0_ffn_w_down"])
            combine(nc, env, "co", steps[1], steps[2], out_rows, slots, weights, arg["L1_ffn_W2"], w2_mixed)
        attention(nc, env, "a1", steps[2], steps[3], arg["L1_attn_w_q"], arg["L1_attn_w_k"], arg["L1_attn_w_v"], arg["L1_attn_w_o"])
        wkv = arg["L1_xattn_Wkv_expand"]
        attention(nc, env, "c1", steps[3], steps[4], arg["L1_xattn_Wq"], wkv[0:D, :], wkv[D:2 * D, :], arg["L1_xattn_Wout"],
                  ctx_in=context, causal=True)
        network(nc, env, "ff", steps[4], steps[5], out.rearrange("b s d -> (b s) d"),
                arg["L1_ffn_W1"], arg["L1_ffn_W3"], w2_mixed)


_INS = ["x", "ctx_512", "L0_attn_Wq", "L0_attn_Wk", "L0_attn_Wv", "L0_attn_Wo", "L0_attn_gate", "L0_xattn_Wq",
        "L0_xattn_Wk", "L0_xattn_gamma_raw", "L0_ffn_w_cls", "L0_ffn_bias", "L0_ffn_w_gate_up", "L0_ffn_w_down",
        "L1_attn_w_q", "L1_attn_w_k", "L1_attn_w_v", "L1_attn_w_o", "L1_xattn_Wq", "L1_xattn_Wkv_expand",
        "L1_xattn_Wout", "L1_ffn_W1", "L1_ffn_W2", "L1_ffn_W3"]


def _tables(np):
    inv_freq = (np.float32(1) / np.float32(10000) ** (np.arange(0, D, 2, dtype=np.float32) / np.float32(D))).astype(np.float32)
    angle = (np.arange(S, dtype=np.float32)[None, :] * inv_freq[:, None]).astype(np.float32)
    bits = np.array([[bin(i & j).count("1") % 2 for j in range(P)] for i in range(P)])
    return {"cos": np.cos(angle), "sin": np.sin(angle), "hadamard": (1 - 2 * bits).astype(np.float32)}


def kernel(**inputs):
    import numpy as _np
    import concourse.bacc as _bacc
    from concourse import mybir as _mybir
    from concourse.bass_utils import run_bass_kernel_spmd as _run

    nc = _bacc.Bacc("TRN2", target_bir_lowering=False, num_devices=1)
    arrays, arg = {}, {}
    given = {name: _np.ascontiguousarray(inputs[name]) for name in _INS}
    given["L0_xattn_gamma_raw"] = given["L0_xattn_gamma_raw"].reshape(1)
    given.update(_tables(_np))
    for name, a in given.items():
        arrays[f"in_{name}_dram"] = a
        arg[name] = nc.dram_tensor(f"in_{name}_dram", a.shape, _mybir.dt.from_np(a.dtype), kind="ExternalInput").ap()
    out = nc.dram_tensor("out_0_dram", (B, S, D), F32, kind="ExternalOutput").ap()
    decoder(nc, arg, out)
    r = _run(nc, [arrays], core_ids=[0])
    return r.results[0]["out_0_dram"]
```
